# Optimizing a Trainium2 kernel written in Bass

```python
import numpy as np
import jax
import jax.numpy as jnp

def _softmax(x, axis=-1):
    return jax.nn.softmax(x, axis=axis)

def _gelu(x):
    return jax.nn.gelu(x, approximate=True)

def _silu(x):
    return jax.nn.silu(x)

def _sigmoid(x):
    return jax.nn.sigmoid(x)

def _layernorm(x, axis=-1, eps=1e-05):
    m = jnp.mean(x, axis=axis, keepdims=True)
    v = jnp.var(x, axis=axis, keepdims=True)
    return (x - m) / jnp.sqrt(v + eps)

def _scatter_add(tgt, idx, src, axis=0):
    return tgt.at[idx].add(src)

def _segment_sum(src, seg, n):
    return jax.ops.segment_sum(src, seg, n)
kernel_name = 'mk_adaln_d1_jaxref_r4_b88a9c'

def setup_inputs(seed: int=0):
    np.random.seed(seed)
    _w = jnp.asarray

    def _L0_attn_setup():
        import jax, jax.numpy as jnp
        import numpy as np
        B, L, DM = (4, 128, 256)
        DS, DC, EXP = (16, 4, 2)
        DI = EXP * DM
        DTR = (DM + 15) // 16
        EPS = 1e-12
        SLOPE = 0.01

        def _ln(x, w, b):
            m = x.mean(-1, keepdims=True)
            v = ((x - m) ** 2).mean(-1, keepdims=True)
            return (x - m) * jax.lax.rsqrt(v + EPS) * w + b

        def _mamba(x, in_proj_w, conv_w, conv_b, x_proj_w, dt_proj_w, dt_proj_b, A_log, D, out_proj_w):
            xz = jnp.einsum('bld,ed->ble', x, in_proj_w)
            xs, z = jnp.split(xz, 2, axis=-1)
            kern = conv_w.T[:, None, :]
            xs = jax.lax.conv_general_dilated(xs, kern, window_strides=(1,), padding=[(DC - 1, 0)], dimension_numbers=('NWC', 'WIO', 'NWC'), feature_group_count=DI)
            xs = jax.nn.silu(xs + conv_b)
            x_dbl = jnp.einsum('bld,ed->ble', xs, x_proj_w)
            dt_r = x_dbl[..., :DTR]
            Bm = x_dbl[..., DTR:DTR + DS]
            Cm = x_dbl[..., DTR + DS:]
            dt = jax.nn.softplus(jnp.einsum('blr,dr->bld', dt_r, dt_proj_w) + dt_proj_b)
            A = -jnp.exp(A_log)
            dA = jnp.exp(dt[..., None] * A)
            dBx = dt[..., None] * Bm[:, :, None, :] * xs[..., None]

            def step(h, inp):
                dA_t, dBx_t, C_t = inp
                h = dA_t * h + dBx_t
                y = jnp.einsum('bdn,bn->bd', h, C_t)
                return (h, y)
            h0 = jnp.zeros((x.shape[0], DI, DS), dtype=x.dtype)
            _, ys = jax.lax.scan(step, h0, (dA.transpose(1, 0, 2, 3), dBx.transpose(1, 0, 2, 3), Cm.transpose(1, 0, 2)))
            y = ys.transpose(1, 0, 2) + D * xs
            y = y * jax.nn.silu(z)
            return jnp.einsum('bld,ed->ble', y, out_proj_w)
        key = jax.random.key(seed)
        ks = jax.random.split(key, 16)
        s = 0.02
        inp = {'x': jax.random.normal(ks[0], (B, L, DM), dtype=jnp.float32), 'in_proj_w': jax.random.normal(ks[1], (2 * DI, DM), dtype=jnp.float32) * s, 'conv_w': jax.random.normal(ks[2], (DI, DC), dtype=jnp.float32) * s, 'conv_b': jnp.zeros((DI,), dtype=jnp.float32), 'x_proj_w': jax.random.normal(ks[3], (DTR + 2 * DS, DI), dtype=jnp.float32) * s, 'dt_proj_w': jax.random.normal(ks[4], (DI, DTR), dtype=jnp.float32) * s, 'dt_proj_b': jax.random.normal(ks[5], (DI,), dtype=jnp.float32) * s, 'A_log': jnp.log(jnp.tile(jnp.arange(1, DS + 1, dtype=jnp.float32), (DI, 1))), 'D': jnp.ones((DI,), dtype=jnp.float32), 'out_proj_w': jax.random.normal(ks[6], (DM, DI), dtype=jnp.float32) * s, 'ln1_w': jnp.ones((DM,), dtype=jnp.float32), 'ln1_b': jnp.zeros((DM,), dtype=jnp.float32), 'ffn_w1': jax.random.normal(ks[7], (2 * DM, DM), dtype=jnp.float32) * s, 'ffn_b1': jnp.zeros((2 * DM,), dtype=jnp.float32), 'ffn_w2': jax.random.normal(ks[8], (DM, 2 * DM), dtype=jnp.float32) * s, 'ffn_b2': jnp.zeros((DM,), dtype=jnp.float32), 'ln2_w': jnp.ones((DM,), dtype=jnp.float32), 'ln2_b': jnp.zeros((DM,), dtype=jnp.float32)}
        return inp
    _L0_attn_in = _L0_attn_setup()

    def _L0_ffn_setup():
        import jax, jax.numpy as jnp
        import numpy as np
        HIDDEN = 256
        FFN = 4 * HIDDEN
        NUM_EXPERTS = 8
        TOP_K = 2
        B, S = (4, 512)
        key = jax.random.key(seed)
        ks = jax.random.split(key, 7)
        scale = 0.02
        return {'x': jax.random.normal(ks[0], (B, S, HIDDEN), dtype=jnp.float32), 'gate_w': jax.random.normal(ks[1], (HIDDEN, NUM_EXPERTS), dtype=jnp.float32) * scale, 'gate_b': jnp.zeros((NUM_EXPERTS,), dtype=jnp.float32), 'w1': jax.random.normal(ks[2], (NUM_EXPERTS, HIDDEN, FFN), dtype=jnp.float32) * scale, 'b1': jnp.zeros((NUM_EXPERTS, FFN), dtype=jnp.float32), 'w2': jax.random.normal(ks[3], (NUM_EXPERTS, FFN, HIDDEN), dtype=jnp.float32) * scale, 'b2': jnp.zeros((NUM_EXPERTS, HIDDEN), dtype=jnp.float32)}
    _L0_ffn_in = _L0_ffn_setup()
    _L0_c = _w((lambda *s: np.random.randn(*s).astype(np.float32) * 0.05)(8, 256))
    _L0_wmod = _w((lambda *s: np.random.randn(*s).astype(np.float32) * 0.05)(256, 6 * 256) * 256 ** (-0.5))
    _d = {'L0_attn_x': _L0_attn_in['x'], 'L0_attn_in_proj_w': _L0_attn_in['in_proj_w'], 'L0_attn_conv_w': _L0_attn_in['conv_w'], 'L0_attn_conv_b': _L0_attn_in['conv_b'], 'L0_attn_x_proj_w': _L0_attn_in['x_proj_w'], 'L0_attn_dt_proj_w': _L0_attn_in['dt_proj_w'], 'L0_attn_dt_proj_b': _L0_attn_in['dt_proj_b'], 'L0_attn_A_log': _L0_attn_in['A_log'], 'L0_attn_D': _L0_attn_in['D'], 'L0_attn_out_proj_w': _L0_attn_in['out_proj_w'], 'L0_attn_ln1_w': _L0_attn_in['ln1_w'], 'L0_attn_ln1_b': _L0_attn_in['ln1_b'], 'L0_attn_ffn_w1': _L0_attn_in['ffn_w1'], 'L0_attn_ffn_b1': _L0_attn_in['ffn_b1'], 'L0_attn_ffn_w2': _L0_attn_in['ffn_w2'], 'L0_attn_ffn_b2': _L0_attn_in['ffn_b2'], 'L0_attn_ln2_w': _L0_attn_in['ln2_w'], 'L0_attn_ln2_b': _L0_attn_in['ln2_b'], 'L0_ffn_gate_w': _L0_ffn_in['gate_w'], 'L0_ffn_gate_b': _L0_ffn_in['gate_b'], 'L0_ffn_w1': _L0_ffn_in['w1'], 'L0_ffn_b1': _L0_ffn_in['b1'], 'L0_ffn_w2': _L0_ffn_in['w2'], 'L0_ffn_b2': _L0_ffn_in['b2'], 'L0_c': _L0_c, 'L0_wmod': _L0_wmod}
    _x0 = _d['L0_attn_x']
    _d['L0_attn_x'] = jax.random.normal(jax.random.fold_in(jax.random.key(seed), 1), (8, 512, 256), dtype=_x0.dtype)
    del _x0
    return _d

def reference(L0_attn_x, L0_attn_in_proj_w, L0_attn_conv_w, L0_attn_conv_b, L0_attn_x_proj_w, L0_attn_dt_proj_w, L0_attn_dt_proj_b, L0_attn_A_log, L0_attn_D, L0_attn_out_proj_w, L0_attn_ln1_w, L0_attn_ln1_b, L0_attn_ffn_w1, L0_attn_ffn_b1, L0_attn_ffn_w2, L0_attn_ffn_b2, L0_attn_ln2_w, L0_attn_ln2_b, L0_ffn_gate_w, L0_ffn_gate_b, L0_ffn_w1, L0_ffn_b1, L0_ffn_w2, L0_ffn_b2, L0_c, L0_wmod):

    def _L0_attn_ref(x, in_proj_w, conv_w, conv_b, x_proj_w, dt_proj_w, dt_proj_b, A_log, D, out_proj_w, ln1_w, ln1_b, ffn_w1, ffn_b1, ffn_w2, ffn_b2, ln2_w, ln2_b):
        import jax, jax.numpy as jnp
        import numpy as np
        B, L, DM = (4, 128, 256)
        DS, DC, EXP = (16, 4, 2)
        DI = EXP * DM
        DTR = (DM + 15) // 16
        EPS = 1e-12
        SLOPE = 0.01

        def _ln(x, w, b):
            m = x.mean(-1, keepdims=True)
            v = ((x - m) ** 2).mean(-1, keepdims=True)
            return (x - m) * jax.lax.rsqrt(v + EPS) * w + b

        def _mamba(x, in_proj_w, conv_w, conv_b, x_proj_w, dt_proj_w, dt_proj_b, A_log, D, out_proj_w):
            xz = jnp.einsum('bld,ed->ble', x, in_proj_w)
            xs, z = jnp.split(xz, 2, axis=-1)
            kern = conv_w.T[:, None, :]
            xs = jax.lax.conv_general_dilated(xs, kern, window_strides=(1,), padding=[(DC - 1, 0)], dimension_numbers=('NWC', 'WIO', 'NWC'), feature_group_count=DI)
            xs = jax.nn.silu(xs + conv_b)
            x_dbl = jnp.einsum('bld,ed->ble', xs, x_proj_w)
            dt_r = x_dbl[..., :DTR]
            Bm = x_dbl[..., DTR:DTR + DS]
            Cm = x_dbl[..., DTR + DS:]
            dt = jax.nn.softplus(jnp.einsum('blr,dr->bld', dt_r, dt_proj_w) + dt_proj_b)
            A = -jnp.exp(A_log)
            dA = jnp.exp(dt[..., None] * A)
            dBx = dt[..., None] * Bm[:, :, None, :] * xs[..., None]

            def step(h, inp):
                dA_t, dBx_t, C_t = inp
                h = dA_t * h + dBx_t
                y = jnp.einsum('bdn,bn->bd', h, C_t)
                return (h, y)
            h0 = jnp.zeros((x.shape[0], DI, DS), dtype=x.dtype)
            _, ys = jax.lax.scan(step, h0, (dA.transpose(1, 0, 2, 3), dBx.transpose(1, 0, 2, 3), Cm.transpose(1, 0, 2)))
            y = ys.transpose(1, 0, 2) + D * xs
            y = y * jax.nn.silu(z)
            return jnp.einsum('bld,ed->ble', y, out_proj_w)
        h = _mamba(x, in_proj_w, conv_w, conv_b, x_proj_w, dt_proj_w, dt_proj_b, A_log, D, out_proj_w)
        h = _ln(h + x, ln1_w, ln1_b)
        f = jnp.einsum('bld,ed->ble', h, ffn_w1) + ffn_b1
        f = jnp.where(f >= 0, f, SLOPE * f)
        f = jnp.einsum('ble,de->bld', f, ffn_w2) + ffn_b2
        return _ln(f + h, ln2_w, ln2_b)

    def _L0_ffn_ref(x, gate_w, gate_b, w1, b1, w2, b2):
        import jax, jax.numpy as jnp
        import numpy as np
        HIDDEN = 256
        FFN = 4 * HIDDEN
        NUM_EXPERTS = 8
        TOP_K = 2
        B, S = (4, 512)
        b, s, h = x.shape
        xt = x.reshape(b * s, h)
        probs = jax.nn.softmax(xt @ gate_w + gate_b, axis=-1)
        _, idx = jax.lax.top_k(probs, TOP_K)
        one_hot = jax.nn.one_hot(idx, NUM_EXPERTS, dtype=xt.dtype)
        mask = (one_hot.sum(axis=1) > 0).astype(xt.dtype)
        h1 = jax.nn.relu(jnp.einsum('th,ehf->etf', xt, w1) + b1[:, None, :])
        out_e = jnp.einsum('etf,efh->eth', h1, w2) + b2[:, None, :]
        out = jnp.einsum('eth,te->th', out_e, mask)
        return out.reshape(b, s, h)
    x = L0_attn_x
    mod = (_silu(L0_c) @ L0_wmod).reshape(L0_c.shape[0], 6, 1, -1)
    sa, ca, ga, sb, cb, gb = (mod[:, 0], mod[:, 1], mod[:, 2], mod[:, 3], mod[:, 4], mod[:, 5])
    ga = (2 * (ga >= 0) - 1) * jnp.maximum(jnp.abs(ga), 0.25)
    gb = (2 * (gb >= 0) - 1) * jnp.maximum(jnp.abs(gb), 0.25)
    h = _layernorm(x, axis=-1) * (1 + ca) + sa
    x = x + ga * _L0_attn_ref(h, L0_attn_in_proj_w, L0_attn_conv_w, L0_attn_conv_b, L0_attn_x_proj_w, L0_attn_dt_proj_w, L0_attn_dt_proj_b, L0_attn_A_log, L0_attn_D, L0_attn_out_proj_w, L0_attn_ln1_w, L0_attn_ln1_b, L0_attn_ffn_w1, L0_attn_ffn_b1, L0_attn_ffn_w2, L0_attn_ffn_b2, L0_attn_ln2_w, L0_attn_ln2_b)
    h = _layernorm(x, axis=-1) * (1 + cb) + sb
    x = x + gb * _L0_ffn_ref(h, L0_ffn_gate_w, L0_ffn_gate_b, L0_ffn_w1, L0_ffn_b1, L0_ffn_w2, L0_ffn_b2)
    return x

_drawn_inputs = setup_inputs


def setup_inputs(seed=0):
    import zlib

    import numpy as np

    out = dict(_drawn_inputs(seed))
    spreads = {'L0_attn_conv_b': (0.0, 0.8),
     'L0_attn_D': (1.0, 0.6),
     'L0_attn_ln1_w': (1.0, 0.2),
     'L0_attn_ln1_b': (0.0, 0.329),
     'L0_attn_ffn_b1': (0.0, 0.8),
     'L0_attn_ffn_b2': (0.0, 0.274),
     'L0_attn_ln2_w': (1.0, 0.2),
     'L0_attn_ln2_b': (0.0, 0.297),
     'L0_ffn_gate_b': (0.0, 0.1),
     'L0_ffn_b1': (0.0, 0.516),
     'L0_ffn_b2': (0.0, 0.1)}
    factors = {'L0_attn_in_proj_w': 8.0,
     'L0_attn_conv_w': 8.0,
     'L0_attn_x_proj_w': 8.0,
     'L0_attn_dt_proj_w': 8.0,
     'L0_attn_dt_proj_b': 24.167,
     'L0_attn_A_log': 8.0,
     'L0_attn_out_proj_w': 8.0}
    for name, (base, spread) in spreads.items():
        noise = np.random.default_rng([zlib.crc32(name.encode()), seed]).standard_normal(out[name].shape)
        drawn = base * np.exp(spread * noise) if base else spread * noise
        out[name] = jnp.asarray(drawn.astype(out[name].dtype))
    for name, factor in factors.items():
        out[name] = (out[name] * factor).astype(out[name].dtype)
    return out
```

```python
import concourse.bass as bass
from concourse import mybir
from contextlib import ExitStack

B, L, DM = 8, 512, 256
DI, DS, DC, DTR = 512, 16, 4, 16
NE, FF = 8, 1024
P = 128
TT = L // P
FT = DM // P
JT = DI // P
UNITS = JT * DS
SLOT = 2
NSLOT = UNITS // SLOT
PAIRS = UNITS // 2
NBX = 3
NHC = 4
NSS = 3
ROWS = 256
CAP = B * L + ROWS
NTILE = 2 * B * L // ROWS + NE
IDLE_ROW = NE * CAP
DUMP = B * L
RW = DM + 1
LN_EPS_OUT, LN_EPS_IN = 1e-5, 1e-12
SLOPE = 0.01

F32 = mybir.dt.float32
U32 = mybir.dt.uint32
I32 = mybir.dt.int32
ALU = mybir.AluOpType
ACT = mybir.ActivationFunctionType
AX = mybir.AxisListType


def wait(engine, sem, value):
    if isinstance(value, int) and value <= 0:
        return
    engine.wait_ge(sem, value)


def wait_apart(engine, sem, value, long_done):
    if not isinstance(value, int):
        value = engine.to_reg(value)
    engine.wait_ge(long_done, 1)
    wait(engine, sem, value)


class Ordered:

    def __init__(self, engine, sem, n):
        self.engine, self.sem, self.n, self.at = engine, sem, n, 0

    def done(self, ins):
        self.at += 1
        ins.then_inc(self.sem, 1)

    def settle(self, seq):
        wait(self.engine, self.sem, seq * self.n + self.at)

    def settle_apart(self, seq, long_done):
        wait_apart(self.engine, self.sem, seq * self.n + self.at, long_done)

    def finish(self):
        assert self.at == self.n, (self.at, self.n)
        self.at = 0


def scan_program(nc, t, d, keep):
    ident, ones, e_iota8, e_base, count = (keep[k] for k in ("ident", "ones", "e_iota8", "e_base", "count"))
    ctx = ExitStack()
    with ctx:
        def sb(name, shape, dt=F32):
            return ctx.enter_context(nc.sbuf_tensor(name, shape, dt))

        def sem(name):
            return ctx.enter_context(nc.semaphore(name))

        w_in = sb("w_in", [P, FT, 2 * DI])
        w_x = sb("w_x", [P, JT, DTR + 2 * DS])
        w_dt = sb("w_dt", [DTR, DI])
        w_out = sb("w_out", [P, JT, DM])
        w_f1 = sb("w_f1", [P, FT, 2 * DM])
        w_f2 = sb("w_f2", [P, JT, DM])
        w_gate = sb("w_gate", [P, FT, NE])
        conv_w = sb("conv_w", [P, JT, DC])
        conv_b = sb("conv_b", [P, JT])
        dt_b = sb("dt_b", [P, JT])
        d_skip = sb("d_skip", [P, JT])
        f1_b = sb("f1_b", [P, JT])
        ln1_w = sb("ln1_w", [P, FT])
        ln1_b = sb("ln1_b", [P, FT])
        a_neg = sb("a_neg", [P, JT, DS])
        f2_b = sb("f2_b", [1, DM])
        gate_b = sb("gate_b", [1, NE])
        before = sb("before", [P, P])
        zero_bias = sb("zero_bias", [P, 1])
        token_no = sb("token_no", [P, TT])
        mod_col = sb("mod_col", [P, 4, B])
        mod_now = sb("mod_now", [P, 4])
        xrow = sb("xrow", [P, TT, DM])
        h_t = sb("h_t", [P, FT, L])
        h_res = sb("h_res", [P, FT, L])
        xs = sb("xs", [P, 2, JT, L])
        zs = sb("zs", [P, JT, L])
        x_dbl = sb("x_dbl", [DTR + 2 * DS, L])
        soft = sb("soft", [P, L])
        relu_dt = sb("relu_dt", [P, L])
        dt = sb("dt", [P, JT, L])
        u = sb("u", [P, JT, L])
        b_bc = sb("b_bc", [P, DS, L])
        c_bc = sb("c_bc", [P, DS, L])
        bx = sb("bx", [P, NBX, 2, L])
        hc = sb("hc", [P, NHC, L])
        yg = sb("yg", [P, JT, L])
        norm = sb("norm", [P, TT, DM])
        h2_t = sb("h2_t", [P, FT, L])
        f1 = sb("f1", [P, JT, L])
        mod_row = sb("mod_row", [P, 4, DM])
        x1 = sb("x1", [P, TT, DM])
        h3 = sb("h3", [P, TT, RW])
        stats = sb("stats", [P, TT, 6])
        mv = sb("mv", [P, TT, 2])
        lnv = sb("lnv", [P, TT])
        rstd = sb("rstd", [P, TT])
        tmp = sb("tmp", [P, TT])
        stats0 = sb("stats0", [P, TT, 6])
        mv0 = sb("mv0", [P, TT, 2])
        lnv0 = sb("lnv0", [P, TT])
        rstd0 = sb("rstd0", [P, TT])
        tmp0 = sb("tmp0", [P, TT])
        logits = sb("logits", [P, TT, NE])
        top_v = sb("top_v", [P, TT, 8])
        top_i = sb("top_i", [P, TT, 8], U32)
        top_f = sb("top_f", [P, TT, 8])
        pick1 = sb("pick1", [P, TT, NE])
        pick2 = sb("pick2", [P, TT, NE])
        picks = sb("picks", [P, TT, NE])
        slot_f = sb("slot_f", [P, TT, NE])
        prod = sb("prod", [P, TT, NE])
        slot_s = sb("slot_s", [P, 2, TT])
        slot_i = sb("slot_i", [P, 2, TT], U32)
        flat_b = b_bc[:, :, :].rearrange("p n l -> p (n l)")
        w_mod = flat_b[:, 0:FT * 6 * DM].rearrange("p (k n) -> p k n", k=FT)
        cond_t = flat_b[:, 3072:3072 + FT * B].rearrange("p (k b) -> p k b", k=FT)
        mod8 = flat_b[0:B, 3328:3328 + 6 * DM].rearrange("p (k n) -> p k n", k=6)
        row8 = flat_b[0:B, 4864:4864 + 5 * DM].rearrange("p (k n) -> p k n", k=5)
        ln2w8 = flat_b[0:B, 6144:6144 + DM]
        ln2b8 = flat_b[0:B, 6400:6400 + DM]
        mag8 = flat_b[0:B, 6656:6656 + 2 * DM].rearrange("p (k n) -> p k n", k=2)
        sgn8 = flat_b[0:B, 7168:7168 + 2 * DM].rearrange("p (k n) -> p k n", k=2)
        flat_c = c_bc[:, :, :].rearrange("p n l -> p (n l)")
        pad_rows = flat_c[:, 0:2 * RW].rearrange("p (k n) -> p k n", k=2)
        pad_no = flat_c[:, 1024:1025]
        zeros = flat_c[:, 2048:2048 + DM]

        ss = [ctx.enter_context(nc.psum_tensor(f"ss{i}", [P, L], F32)) for i in range(NSS)]
        ysum = ctx.enter_context(nc.psum_tensor("ysum", [P, L], F32))
        fp = [ctx.enter_context(nc.psum_tensor(f"fp{i}", [P, L], F32)) for i in range(2)]
        bp = [ctx.enter_context(nc.psum_tensor(f"bp{i}", [P, L], F32)) for i in range(2)]

        loaded = sem("loaded")
        rows_stored = sem("rows_stored")
        inits_stored = sem("inits_stored")
        x_loaded = sem("x_loaded")
        res_loaded = sem("res_loaded")
        bc_stored = sem("bc_stored")
        bc_loaded = [sem(f"bc_loaded{g}") for g in range(4)]
        x1_stored = sem("x1_stored")
        scattered = sem("scattered")
        consts_set = sem("consts_set")
        pool_set = sem("pool_set")
        cond_silu = sem("cond_silu")
        mod_full = sem("mod_full")
        mod_copied = sem("mod_copied")
        a_ready = sem("a_ready")
        rows_ready = sem("rows_ready")
        ln0_var = sem("ln0_var")
        ln0_log = sem("ln0_log")
        x_normed = sem("x_normed")
        xt_full = sem("xt_full")
        h_ready = sem("h_ready")
        xin_full = sem("xin_full")
        tap_last = sem("tap_last")
        conv_done = sem("conv_done")
        xs_ready = sem("xs_ready")
        zin_full = sem("zin_full")
        z_copied = sem("z_copied")
        z_ready = sem("z_ready")
        xproj_full = sem("xproj_full")
        xdbl_ready = sem("xdbl_ready")
        dt_full = sem("dt_full")
        abs_taken = sem("abs_taken")
        log_ready = sem("log_ready")
        relu_ready = sem("relu_ready")
        dt_ready = sem("dt_ready")
        u_ready = sem("u_ready")
        exp_done = sem("exp_done")
        bx_ready = sem("bx_ready")
        scan_done = sem("scan_done")
        hc_ready = sem("hc_ready")
        y_summed = sem("y_summed")
        y_read = sem("y_read")
        y_gated = sem("y_gated")
        out_full = sem("out_full")
        res_copied = sem("res_copied")
        ln_var = sem("ln_var")
        ln_log = sem("ln_log")
        n1_ready = sem("n1_ready")
        n1t_full = sem("n1t_full")
        h2_ready = sem("h2_ready")
        f1_full = sem("f1_full")
        f1_copied = sem("f1_copied")
        f1_ready = sem("f1_ready")
        f2_full = sem("f2_full")
        n2_ready = sem("n2_ready")
        x1_ready = sem("x1_ready")
        n3_ready = sem("n3_ready")
        h3_ready = sem("h3_ready")
        h3t_full = sem("h3t_full")
        h3t_ready = sem("h3t_ready")
        logits_full = sem("logits_full")
        picks_ready = sem("picks_ready")
        rank_full = sem("rank_full")
        slots_ready = sem("slots_ready")
        v_own = sem("v_own")
        vf_own = sem("vf_own")
        p_own = sem("p_own")
        a_own = sem("a_own")
        v0_own = sem("v0_own")
        pp_own = sem("pp_own")
        tap_own = sem("tap_own")

        NW = 26

        block = ctx.enter_context(nc.Block())

        def program(engine, prelude, front, gates, back, scan, last_front=None):
            def slots(f, g, k, s):
                for n in range(NSLOT):
                    if s is not None:
                        scan(s, n)
                    for table, seq in ((gates, g), (back, k), (front, f)):
                        if seq is not None:
                            for step in table.get(n, ()):
                                step(seq)
            prelude()
            slots(0, None, None, None)
            slots(1, 0, None, 0)
            slots(2, 1, 0, 1)
            with engine.Fori(0, B - 3) as i:
                slots(i + 3, i + 2, i + 1, i + 2)
            slots(None, B - 1, B - 2, B - 1)
            slots(None, None, B - 1, None)

        @block.sync
        def _(sp):
            def prelude():
                for dst, src in (
                    (w_mod, t["wmod"].rearrange("(k p) n -> p k n", p=P)),
                    (cond_t, t["cond_t"].rearrange("(k p) b -> p k b", p=P)),
                    (w_in[:, :, :], t["in_proj_t"].rearrange("(k p) n -> p k n", p=P)),
                    (conv_w[:, :, :], t["conv_w"].rearrange("(j p) k -> p j k", p=P)),
                    (conv_b[:, :], t["conv_b"]),
                    (w_x[:, :, :], t["x_proj_t"].rearrange("(k p) n -> p k n", p=P)),
                    (w_dt[:, :], t["dt_proj_t"]),
                    (dt_b[:, :], t["dt_b"]),
                    (a_neg[:, :, :], t["A_log"].rearrange("(j p) n -> p j n", p=P)),
                    (d_skip[:, :], t["D"]),
                    (w_out[:, :, :], t["out_proj_t"].rearrange("(k p) n -> p k n", p=P)),
                    (w_f1[:, :, :], t["ffn_w1_t"].rearrange("(k p) n -> p k n", p=P)),
                    (w_f2[:, :, :], t["ffn_w2_t"].rearrange("(k p) n -> p k n", p=P)),
                    (w_gate[:, :, :], t["gate_w"].rearrange("(k p) n -> p k n", p=P)),
                    (f1_b[:, :], t["ffn_b1"]),
                    (ln1_w[:, :], t["ln1_w"]),
                    (ln1_b[:, :], t["ln1_b"]),
                    (f2_b[:, :], t["ffn_b2"]),
                    (gate_b[:, :], t["gate_b"]),
                    (ln2w8, t["ln2_w"].to_broadcast([B, DM])),
                    (ln2b8, t["ln2_b"].to_broadcast([B, DM])),
                    (ident[:, :], t["ident"]),
                    (before[:, :], t["before"]),
                    (e_base[:, :], t["e_base"].to_broadcast([P, NE])),
                    (e_iota8[:, :], t["e_iota"].to_broadcast([P, NE])),
                    (token_no[:, :], t["token_no"]),
                ):
                    sp.dma_start(dst, src).then_inc(loaded, 16)
                sp.wait_ge(rows_ready, 1)
                sp.dma_start(d["mod_rows"], row8).then_inc(rows_stored, 16)
                sp.wait_ge(rows_stored, 16)
                sp.wait_ge(pool_set, 1)
                zsrc = zeros.unsqueeze(1).to_broadcast([P, (DUMP + P) // P, DM])
                sp.dma_start(d["acc"].rearrange("(k p) n -> p k n", p=P), zsrc).then_inc(inits_stored, 16)
                sp.dma_start(d["region"][IDLE_ROW:IDLE_ROW + ROWS, :].rearrange("(k p) n -> p k n", p=P),
                             pad_rows).then_inc(inits_stored, 16)
                sp.dma_start(d["pads"], pad_rows).then_inc(inits_stored, 16)
                sp.wait_ge(inits_stored, 48)

            def load_x(s):
                wait(sp, x_normed, s)
                sp.dma_start(xrow[:, :, :], t["x"][s, :, :].rearrange("(k p) n -> p k n", p=P)).then_inc(x_loaded, 16)

            def store_bc(s):
                sp.wait_ge(xdbl_ready, s + 1)
                sp.dma_start(d["bc"], x_dbl[DTR:DTR + 2 * DS, :]).then_inc(bc_stored, 16)
                sp.wait_ge(bc_stored, 16 * (s + 1))

            def load_bc(g):
                def step(s):
                    wait(sp, hc_ready, s * UNITS - (UNITS - (JT - 1) * DS - 4 * (g + 1)))
                    n = slice(4 * g, 4 * g + 4)
                    for dst, at in ((b_bc, 0), (c_bc, DS)):
                        src = d["bc"][at + 4 * g:at + 4 * g + 4, :].unsqueeze(0).to_broadcast([P, 4, L])
                        sp.dma_start(dst[:, n, :], src).then_inc(bc_loaded[g], 16)
                return step

            def load_res(s):
                wait(sp, x1_stored, 16 * s)
                wait(sp, n3_ready, s)
                wait(sp, h3_ready, s)
                sp.dma_start(x1[:, :, :], t["x"][s, :, :].rearrange("(k p) n -> p k n", p=P)).then_inc(res_loaded, 16)
                sp.dma_start(mod_row[:, :, :],
                             d["mod_rows"][bass.ds(s, 1), 0:4, :].to_broadcast([P, 4, DM])).then_inc(res_loaded, 16)

            def store_x1(s):
                sp.wait_ge(x1_ready, s + 1)
                sp.dma_start(d["x1"][s, :, :].rearrange("(k p) n -> p k n", p=P), x1[:, :, :]).then_inc(x1_stored, 16)

            program(sp, prelude,
                    front={0: [load_x], 24: [store_bc], 26: [load_bc(0)], 27: [load_bc(1)],
                           29: [load_bc(2)], 31: [load_bc(3)]},
                    gates={}, back={2: [load_res], 20: [store_x1]}, scan=lambda s, n: None)
            sp.wait_ge(x1_stored, 16 * B)

        @block.gpsimd
        def _(pool):
            own = Ordered(pool, p_own, 3)

            def prelude():
                nc.gpsimd.memset(flat_c[:, 0:4096], 0.0).then_inc(pp_own, 1)
                pool.wait_ge(pp_own, 1)
                nc.gpsimd.iota(pad_no.bitcast(U32), [[0, 1]], base=DUMP, channel_multiplier=1).then_inc(pp_own, 1)
                pool.wait_ge(pp_own, 2)
                for k in range(2):
                    last = nc.gpsimd.tensor_copy(pad_rows[:, k, DM:RW].bitcast(U32), pad_no.bitcast(U32))
                last.then_inc(pool_set, 1)

            def softplus(j):
                def step(s):
                    par = s % 2
                    pool.wait_ge(log_ready, s * JT + j + 1)
                    pool.wait_ge(relu_ready, s * JT + j + 1)
                    wait(pool, exp_done, (s - 1) * UNITS + (j + 1) * DS)
                    nc.gpsimd.tensor_tensor(dt[:, j, :], relu_dt[:, :], soft[:, :], ALU.add).then_inc(dt_ready, 1)
                    pool.wait_ge(dt_ready, s * JT + j + 1)
                    nc.gpsimd.tensor_tensor(u[:, j, :], dt[:, j, :], xs[:, par, j, :], ALU.mult).then_inc(u_ready, 1)
                return step

            def copy_res(s):
                wait(pool, out_full, s)
                wait_apart(pool, h_ready, FT * (s + 1), pool_set)
                nc.gpsimd.tensor_copy(h_res[:, :, :], h_t[:, :, :]).then_inc(res_copied, 1)

            def gate_y(j):
                def step(s):
                    pool.wait_ge(y_read, JT * s + j + 1)
                    pool.wait_ge(z_ready, s + 1)
                    nc.gpsimd.tensor_tensor(yg[:, j, :], yg[:, j, :], zs[:, j, :], ALU.mult).then_inc(y_gated, 1)
                return step

            def row(k):
                return mod_row[:, k, :].unsqueeze(1).to_broadcast([P, TT, DM])

            def residual(s):
                pool.wait_ge(n2_ready, s + 1)
                pool.wait_ge(res_loaded, 32 * (s + 1))
                own.done(nc.gpsimd.tensor_tensor(norm[:, :, :], norm[:, :, :], row(0), ALU.mult))
                own.settle(s)
                own.done(nc.gpsimd.tensor_tensor(norm[:, :, :], norm[:, :, :], row(1), ALU.add))
                own.settle(s)
                nc.gpsimd.tensor_tensor(x1[:, :, :], norm[:, :, :], x1[:, :, :], ALU.add).then_inc(x1_ready, 1)

            def modulate(s):
                pool.wait_ge(n3_ready, s + 1)
                own.done(nc.gpsimd.tensor_tensor(norm[:, :, :], norm[:, :, :], row(2), ALU.mult))
                own.settle(s)
                wait(pool, scattered, 16 * 2 * TT * s)
                nc.gpsimd.tensor_tensor(h3[:, :, 0:DM], norm[:, :, :], row(3), ALU.add).then_inc(h3_ready, 1)
                own.finish()

            def scatter(s):
                wait_apart(pool, slots_ready, s + 1, pool_set)
                for k in range(2):
                    for q in range(TT):
                        nc.gpsimd.indirect_dma_start(
                            d["region"], bass.IndirectOffsetOnAxis(slot_i[:, k, q:q + 1], 0), h3[:, q, :], None,
                        ).then_inc(scattered, 16)

            def products(s, n):
                q, j, st = n, n * SLOT // DS, n * SLOT % DS
                if q % (DS // 2) == 0:
                    pool.wait_ge(u_ready, JT * s + j + 1)
                if j == 0 and st % 4 == 0:
                    pool.wait_ge(bc_loaded[st // 4], 32 * (s + 1))
                back_to = {0: -2, 1: 0, 2: -4}.get(q, 2 * q - 4)
                wait(pool, scan_done, UNITS * s + back_to)
                nc.gpsimd.tensor_tensor(bx[:, q % NBX, :, :], u[:, j, :].unsqueeze(1).to_broadcast([P, 2, L]),
                                        b_bc[:, st:st + 2, :], ALU.mult).then_inc(bx_ready, 1)

            program(pool, prelude,
                    front={26: [softplus(0)]},
                    gates={2: [softplus(1)], 4: [softplus(2)], 6: [softplus(3)], 8: [copy_res],
                           21: [gate_y(0)], 22: [gate_y(1)], 26: [gate_y(2)]},
                    back={1: [gate_y(3)], 19: [residual], 24: [modulate], 31: [scatter]},
                    scan=products)
            pool.wait_ge(scattered, 16 * 2 * TT * B)

        @block.scalar
        def _(act):
            def prelude():
                act.wait_ge(loaded, 16 * NW)
                act.wait_ge(consts_set, 1)
                nc.scalar.activation(cond_t, cond_t, ACT.Silu).then_inc(cond_silu, 1)
                nc.scalar.preload_act_table_set("natural_log_exp_and_others")
                nc.scalar.activation(a_neg[:, :, :], a_neg[:, :, :], ACT.Exp).then_inc(a_ready, 1)
                act.wait_ge(a_ready, 1)
                nc.scalar.activation(a_neg[:, :, :], a_neg[:, :, :], ACT.Identity, scale=-1.0,
                                     bias=zero_bias[:, 0:1]).then_inc(a_ready, 1)
                act.wait_ge(a_ready, 2)

            def guess(sem_in, n_in, k_in, sem_out, lnv_, rstd_):
                def step(s):
                    act.wait_ge(sem_in, n_in * s + k_in)
                    nc.scalar.activation(rstd_, lnv_, ACT.Ln, bias=zero_bias[:, 0:1]).then_inc(sem_out, 1)
                    act.wait_ge(sem_out, 2 * (n_in * s + k_in) - 1)
                    nc.scalar.activation(rstd_, rstd_, ACT.Exp, scale=-0.5, bias=zero_bias[:, 0:1]).then_inc(sem_out, 1)
                return step

            def hidden(s):
                act.wait_ge(xt_full, s + 1)
                wait(act, res_copied, s)
                wait(act, zin_full, JT * s)
                act.wait_ge(mod_copied, 2 + s + 1)
                for f in range(FT):
                    nc.scalar.activation(h_t[:, f, :], fp[f][:, :], ACT.Identity, scale=mod_now[:, 2 + f:3 + f],
                                         bias=mod_now[:, f:f + 1]).then_inc(h_ready, 1)

            def tap(j):
                def step(s):
                    if j == 0:
                        wait(act, u_ready, JT * (s - 1))
                        wait(act, y_read, JT * (s - 1))
                    wait_apart(act, xin_full, JT * s + j + 1, consts_set)
                    nc.scalar.activation(xs[:, s % 2, j, :], fp[j % 2][:, :], ACT.Identity,
                                         scale=conv_w[:, j, DC - 1:DC], bias=conv_b[:, j:j + 1]).then_inc(tap_last, 1)
                return step

            def silu_x(s):
                wait_apart(act, conv_done, JT * (s + 1), consts_set)
                nc.scalar.activation(xs[:, s % 2, :, :], xs[:, s % 2, :, :], ACT.Silu).then_inc(xs_ready, 1)
                nc.scalar.preload_act_table_set("natural_log_exp_and_others")

            def silu_z(s):
                act.wait_ge(z_copied, JT * (s + 1))
                nc.scalar.activation(zs[:, :, :], zs[:, :, :], ACT.Silu).then_inc(z_ready, 1)
                if isinstance(s, int) and s == B - 1:
                    nc.scalar.preload_act_table_set("natural_log_exp_and_others")

            def copy_z(j):
                def step(s):
                    act.wait_ge(zin_full, JT * s + j + 1)
                    if j == 0:
                        wait(act, y_gated, JT * s)
                    nc.scalar.activation(zs[:, j, :], fp[(1, 1, 1, 0)[j]][:, :], ACT.Identity,
                                         bias=zero_bias[:, 0:1]).then_inc(z_copied, 1)
                return step

            def copy_xdbl(s):
                act.wait_ge(xproj_full, s + 1)
                wait(act, bc_stored, 16 * s)
                wait(act, dt_full, JT * s)
                nc.scalar.activation(x_dbl[:, :], fp[0][0:DTR + 2 * DS, :], ACT.Identity,
                                     bias=zero_bias[0:DTR + 2 * DS, 0:1]).then_inc(xdbl_ready, 1)

            def softlog(j):
                def step(s):
                    act.wait_ge(dt_full, JT * s + j + 1)
                    wait(act, dt_ready, JT * s + j)
                    nc.scalar.activation(soft[:, :], fp[(1, 0, 0, 0)[j]][:, :], ACT.Abs,
                                         bias=dt_b[:, j:j + 1]).then_inc(abs_taken, 1)
                    act.wait_ge(abs_taken, JT * s + j + 1)
                    nc.scalar.activation(soft[:, :], soft[:, :], ACT.Exp, scale=-1.0,
                                         bias=zero_bias[:, 0:1]).then_inc(a_own, 1)
                    act.wait_ge(a_own, JT * s + j + 1)
                    nc.scalar.activation(soft[:, :], soft[:, :], ACT.Ln, bias=ones[:, 0:1]).then_inc(log_ready, 1)
                return step

            def hidden2(s):
                act.wait_ge(n1t_full, s + 1)
                wait(act, logits_full, s)
                for f in range(FT):
                    nc.scalar.activation(h2_t[:, f, :], bp[f][:, :], ACT.Identity, scale=ln1_w[:, f:f + 1],
                                         bias=ln1_b[:, f:f + 1]).then_inc(h2_ready, 1)

            def copy_f1(j):
                def step(s):
                    act.wait_ge(f1_full, JT * s + j + 1)
                    if j == 0:
                        wait(act, f2_full, s)
                    nc.scalar.activation(f1[:, j, :], bp[j % 2][:, :], ACT.Identity,
                                         bias=f1_b[:, j:j + 1]).then_inc(f1_copied, 1)
                return step

            def copy_h3(s):
                act.wait_ge(h3t_full, s + 1)
                for f in range(FT):
                    nc.scalar.activation(h2_t[:, f, :], bp[f][:, :], ACT.Identity,
                                         bias=zero_bias[:, 0:1]).then_inc(h3t_ready, 1)

            def decay(s, n):
                for k in range(n * SLOT, (n + 1) * SLOT):
                    j, st = divmod(k, DS)
                    if st == 0:
                        act.wait_ge(dt_ready, JT * s + j + 1)
                    before_it = {0: 0, 1: -2, 2: -1}.get(k, k - 2)
                    wait(act, hc_ready, UNITS * s + before_it)
                    nc.scalar.activation(ss[k % NSS][:, :], dt[:, j, :], ACT.Exp, scale=a_neg[:, j, st:st + 1],
                                         bias=zero_bias[:, 0:1]).then_inc(exp_done, 1)

            program(act, prelude,
                    front={8: [guess(ln0_var, 1, 1, ln0_log, lnv0[:, :], rstd0[:, :])],
                           12: [hidden], 14: [tap(0)], 15: [tap(1)], 17: [tap(2)], 18: [tap(3)],
                           20: [silu_x], 23: [copy_xdbl], 25: [softlog(0)]},
                    gates={1: [softlog(1)], 2: [copy_z(0)], 3: [softlog(2)], 4: [copy_z(1)],
                           5: [softlog(3)], 6: [copy_z(2)], 7: [copy_z(3)], 20: [silu_z]},
                    back={6: [guess(ln_var, 3, 1, ln_log, lnv[:, :], rstd[:, :])], 9: [hidden2],
                          11: [copy_f1(0), copy_f1(1)], 12: [copy_f1(2)], 13: [copy_f1(3)],
                          18: [guess(ln_var, 3, 2, ln_log, lnv[:, :], rstd[:, :])],
                          22: [guess(ln_var, 3, 3, ln_log, lnv[:, :], rstd[:, :])], 26: [copy_h3]},
                    scan=decay)

        @block.tensor
        def _(pe):
            def prelude():
                pe.wait_ge(loaded, 16 * NW)
                pe.wait_ge(cond_silu, 1)
                pe.wait_ge(consts_set, 1)
                for k in range(3):
                    for f in range(FT):
                        last = nc.tensor.matmul(ss[k][0:B, :], cond_t[:, f, :], w_mod[:, f, k * L:(k + 1) * L],
                                                start=(f == 0), stop=(f == FT - 1))
                last.then_inc(mod_full, 1)
                for c in range(4):
                    for f in range(FT):
                        last = nc.tensor.matmul(ysum[:, c * B:(c + 1) * B], w_mod[:, f, c * P:(c + 1) * P],
                                                cond_t[:, f, :], start=(f == 0), stop=(f == FT - 1))
                last.then_inc(mod_full, 1)

            def transposes(src, dst, width=None):
                for f in range(FT):
                    for q in range(TT):
                        last = nc.tensor.transpose(dst[f][:, q * P:(q + 1) * P], src[:, q, f * P:(f + 1) * P],
                                                   ident[:, :])
                return last

            def turn_x(s):
                pe.wait_ge(x_normed, s + 1)
                wait(pe, z_copied, JT * s)
                transposes(xrow, fp).then_inc(xt_full, 1)

            def in_proj(dst, col):
                for f in range(FT):
                    last = nc.tensor.matmul(dst, w_in[:, f, col:col + P], h_t[:, f, :],
                                            start=(f == 0), stop=(f == FT - 1))
                return last

            def x_in(j):
                def step(s):
                    pe.wait_ge(h_ready, FT * (s + 1))
                    if j >= 2:
                        pe.wait_ge(conv_done, JT * s + j - 1)
                    in_proj(fp[j % 2][:, :], j * P).then_inc(xin_full, 1)
                return step

            def z_in(j):
                def step(s):
                    if j == 0:
                        pe.wait_ge(relu_ready, JT * s + 1)
                    elif j == 3:
                        pe.wait_ge(relu_ready, JT * s + JT)
                    else:
                        pe.wait_ge(z_copied, JT * s + j)
                    in_proj(fp[(1, 1, 1, 0)[j]][:, :], DI + j * P).then_inc(zin_full, 1)
                return step

            def x_proj(s):
                pe.wait_ge(xs_ready, s + 1)
                for j in range(JT):
                    last = nc.tensor.matmul(fp[0][0:DTR + 2 * DS, :], w_x[:, j, :], xs[:, s % 2, j, :],
                                            start=(j == 0), stop=(j == JT - 1))
                last.then_inc(xproj_full, 1)

            def dt_proj(j):
                def step(s):
                    pe.wait_ge(xdbl_ready, s + 1)
                    if j >= 2:
                        pe.wait_ge(relu_ready, JT * s + j)
                    nc.tensor.matmul(fp[(1, 0, 0, 0)[j]][:, :], w_dt[:, j * P:(j + 1) * P], x_dbl[0:DTR, :],
                                     start=True, stop=True).then_inc(dt_full, 1)
                return step

            def out_proj(s):
                pe.wait_ge(y_gated, JT * (s + 1))
                pe.wait_ge(res_copied, s + 1)
                wait(pe, slots_ready, s)
                for q in range(TT):
                    o = bp[q // 2][:, (q % 2) * DM:(q % 2 + 1) * DM]
                    for j in range(JT):
                        nc.tensor.matmul(o, yg[:, j, q * P:(q + 1) * P], w_out[:, j, :], start=(j == 0), stop=False)
                    for f in range(FT):
                        last = nc.tensor.matmul(o[:, f * P:(f + 1) * P], h_res[:, f, q * P:(q + 1) * P], ident[:, :],
                                                start=False, stop=(f == FT - 1))
                last.then_inc(out_full, 1)

            def turn_n1(s):
                pe.wait_ge(n1_ready, s + 1)
                transposes(norm, bp).then_inc(n1t_full, 1)

            def ffn1(j):
                def step(s):
                    pe.wait_ge(h2_ready, FT * (s + 1))
                    if j >= 2:
                        pe.wait_ge(f1_copied, JT * s + j - 1)
                    for f in range(FT):
                        last = nc.tensor.matmul(bp[j % 2][:, :], w_f1[:, f, j * P:(j + 1) * P], h2_t[:, f, :],
                                                start=(f == 0), stop=(f == FT - 1))
                    last.then_inc(f1_full, 1)
                return step

            def ffn2(s):
                pe.wait_ge(f1_ready, s + 1)
                for q in range(TT):
                    o = bp[q // 2][:, (q % 2) * DM:(q % 2 + 1) * DM]
                    nc.tensor.matmul(o, ones[0:1, :], f2_b[0:1, :], start=True, stop=False)
                    for j in range(JT):
                        nc.tensor.matmul(o, f1[:, j, q * P:(q + 1) * P], w_f2[:, j, :], start=False, stop=False)
                    for f in range(FT):
                        last = nc.tensor.matmul(o[:, f * P:(f + 1) * P], h2_t[:, f, q * P:(q + 1) * P], ident[:, :],
                                                start=False, stop=(f == FT - 1))
                last.then_inc(f2_full, 1)

            def turn_h3(s):
                pe.wait_ge(h3_ready, s + 1)
                transposes(h3, bp).then_inc(h3t_full, 1)

            def gate(s):
                pe.wait_ge(h3t_ready, FT * (s + 1))
                for q in range(TT):
                    o = bp[0][:, q * NE:(q + 1) * NE]
                    nc.tensor.matmul(o, ones[0:1, :], gate_b[0:1, :], start=True, stop=False)
                    for f in range(FT):
                        last = nc.tensor.matmul(o, h2_t[:, f, q * P:(q + 1) * P], w_gate[:, f, :],
                                                start=False, stop=(f == FT - 1))
                last.then_inc(logits_full, 1)

            def rank(s):
                pe.wait_ge(picks_ready, s + 1)
                m = picks[:, :, :].rearrange("p q e -> p (q e)")
                nc.tensor.matmul(bp[1][:, 0:TT * NE], before[:, :], m, start=True, stop=True)
                nc.tensor.matmul(bp[1][:, TT * NE:2 * TT * NE], ones[:, :], m, start=True, stop=True).then_inc(rank_full, 1)

            def state_sum(s, n):
                for k in range(n * SLOT, (n + 1) * SLOT):
                    j, st = divmod(k, DS)
                    if st == 0:
                        wait(pe, y_read, JT * s + j)
                    pe.wait_ge(hc_ready, UNITS * s + k + 1)
                    nc.tensor.matmul(ysum[:, :], ident[:, :], hc[:, k % NHC, :], start=(st == 0),
                                     stop=(st == DS - 1)).then_inc(y_summed, 1)

            def prelude_all():
                prelude()
                pe.wait_ge(mod_copied, 2)

            program(pe, prelude_all,
                    front={11: [turn_x], 13: [x_in(0)], 14: [x_in(1)], 16: [x_in(2)], 17: [x_in(3)],
                           22: [x_proj], 24: [dt_proj(0)]},
                    gates={0: [dt_proj(1)], 1: [z_in(0)], 2: [dt_proj(2)], 3: [z_in(1)], 4: [dt_proj(3)],
                           5: [z_in(2)], 6: [z_in(3)]},
                    back={3: [out_proj], 8: [turn_n1], 10: [ffn1(0), ffn1(1)], 11: [ffn1(2)], 12: [ffn1(3)],
                          15: [ffn2], 25: [turn_h3], 27: [gate], 29: [rank]},
                    scan=state_sum)

        @block.vector
        def _(dve):
            LN = 6
            own = Ordered(dve, v_own, 3 * LN + 6 + 6 + TT)
            own_front = Ordered(dve, vf_own, LN)
            pre = [0]

            def link(ins):
                pre[0] += 1
                ins.then_inc(v0_own, 1)
                dve.wait_ge(v0_own, pre[0])

            def prelude():
                nc.vector.memset(ones[:, :], 1.0)
                nc.vector.memset(zero_bias[:, :], 0.0)
                nc.vector.memset(count[:, :], 0.0).then_inc(consts_set, 1)
                dve.wait_ge(loaded, 16 * NW)
                dve.wait_ge(mod_full, 2)
                for k in range(3):
                    link(nc.vector.tensor_copy(mod8[:, 2 * k:2 * k + 2, :].rearrange("p k n -> p (k n)"), ss[k][0:B, :]))
                nc.vector.tensor_copy(mod_col[:, 0:2, :].rearrange("p k b -> p (k b)"),
                                      ysum[:, 0:2 * B]).then_inc(mod_copied, 1)
                nc.vector.tensor_scalar(mod_col[:, 2:4, :].rearrange("p k b -> p (k b)"), ysum[:, 2 * B:4 * B],
                                        1.0, None, ALU.add).then_inc(mod_copied, 1)
                dve.wait_ge(mod_copied, 2)
                for k, part in enumerate((2, 5)):
                    g = mod8[:, part, :]
                    link(nc.vector.scalar_tensor_tensor(mag8[:, k, :], g, -1.0, g, ALU.mult, ALU.max))
                    link(nc.vector.tensor_scalar(mag8[:, k, :], mag8[:, k, :], 0.25, None, ALU.max))
                    link(nc.vector.tensor_scalar(sgn8[:, k, :], g, 0.0, 2.0, ALU.is_ge, ALU.mult))
                    link(nc.vector.scalar_tensor_tensor(mag8[:, k, :], sgn8[:, k, :], -1.0, mag8[:, k, :],
                                                        ALU.add, ALU.mult))
                link(nc.vector.tensor_tensor(row8[:, 0, :], mag8[:, 0, :], ln2w8, ALU.mult))
                link(nc.vector.tensor_tensor(row8[:, 1, :], mag8[:, 0, :], ln2b8, ALU.mult))
                link(nc.vector.tensor_scalar(row8[:, 2, :], mod8[:, 4, :], 1.0, None, ALU.add))
                link(nc.vector.tensor_copy(row8[:, 3, :], mod8[:, 3, :]))
                nc.vector.tensor_copy(row8[:, 4, :], mag8[:, 1, :]).then_inc(rows_ready, 1)

            def row_stats(s, o, src, eps, var_sem, bufs):
                st_, mv_, lnv_ = bufs[:3]
                for q in range(TT):
                    last = nc.vector.bn_stats(st_[:, q, :], src(q))
                o.done(last)
                o.settle_apart(s, consts_set)
                for q in range(TT):
                    last = nc.vector.bn_aggr(mv_[:, q, :], st_[:, q, :])
                o.done(last)
                o.settle(s)
                nc.vector.tensor_scalar(lnv_[:, :], mv_[:, :, 1], eps, None, ALU.add).then_inc(var_sem, 1)

            def row_norm(s, o, src, dst, log_sem, log_at, ready, bufs):
                _, mv_, lnv_, rstd_, tmp_ = bufs
                dve.wait_ge(log_sem, log_at)
                o.done(nc.vector.tensor_tensor(tmp_[:, :], rstd_[:, :], rstd_[:, :], ALU.mult))
                o.settle(s)
                o.done(nc.vector.tensor_tensor(tmp_[:, :], tmp_[:, :], lnv_[:, :], ALU.mult))
                o.settle(s)
                o.done(nc.vector.tensor_scalar(tmp_[:, :], tmp_[:, :], -0.5, 1.5, ALU.mult, ALU.add))
                o.settle(s)
                o.done(nc.vector.tensor_tensor(rstd_[:, :], rstd_[:, :], tmp_[:, :], ALU.mult))
                o.settle(s)
                for q in range(TT):
                    last = nc.vector.tensor_scalar(dst(q), src(q), mv_[:, q, 0:1], rstd_[:, q:q + 1],
                                                   ALU.subtract, ALU.mult)
                last.then_inc(ready, 1)

            back_bufs = (stats, mv, lnv, rstd, tmp)
            front_bufs = (stats0, mv0, lnv0, rstd0, tmp0)

            def stats_x(s):
                dve.wait_ge(x_loaded, 16 * (s + 1))
                row_stats(s, own_front, lambda q: xrow[:, q, :], LN_EPS_OUT, ln0_var, front_bufs)

            def norm_x(s):
                row_norm(s, own_front, lambda q: xrow[:, q, :], lambda q: xrow[:, q, :],
                         ln0_log, 2 * (s + 1), x_normed, front_bufs)
                wait(dve, h_ready, FT * s)
                nc.vector.tensor_copy(mod_now[:, :], mod_col[:, :, s]).then_inc(mod_copied, 1)
                own_front.finish()

            def conv(j):
                def step(s):
                    dve.wait_ge(tap_last, JT * s + j + 1)
                    for k in range(1, DC):
                        dst = xs[:, s % 2, j, k:L]
                        ins = nc.vector.scalar_tensor_tensor(dst, fp[j % 2][:, 0:L - k], conv_w[:, j, DC - 1 - k:DC - k],
                                                             dst, ALU.mult, ALU.add)
                        if k < DC - 1:
                            ins.then_inc(tap_own, 1)
                            dve.wait_ge(tap_own, (JT * s + j) * (DC - 2) + k)
                        else:
                            ins.then_inc(conv_done, 1)
                return step

            def relu(j):
                def step(s):
                    dve.wait_ge(abs_taken, JT * s + j + 1)
                    wait(dve, dt_ready, JT * s + j)
                    nc.vector.tensor_scalar(relu_dt[:, :], fp[(1, 0, 0, 0)[j]][:, :], dt_b[:, j:j + 1], 0.0,
                                            ALU.add, ALU.max).then_inc(relu_ready, 1)
                return step

            def read_y(j):
                def step(s):
                    dve.wait_ge(y_summed, UNITS * s + (j + 1) * DS)
                    if j == 0:
                        wait(dve, out_full, s)
                    nc.vector.scalar_tensor_tensor(yg[:, j, :], xs[:, s % 2, j, :], d_skip[:, j:j + 1], ysum[:, :],
                                                   ALU.mult, ALU.add).then_inc(y_read, 1)
                return step

            def half(q):
                return bp[q // 2][:, (q % 2) * DM:(q % 2 + 1) * DM]

            def stats1(s):
                dve.wait_ge(out_full, s + 1)
                row_stats(s, own, half, LN_EPS_IN, ln_var, back_bufs)

            def norm1(s):
                wait(dve, h3_ready, s)
                row_norm(s, own, half, lambda q: norm[:, q, :], ln_log, 6 * s + 2, n1_ready, back_bufs)

            def leaky(s):
                dve.wait_ge(f1_copied, JT * (s + 1))
                nc.vector.scalar_tensor_tensor(f1[:, :, :], f1[:, :, :], SLOPE, f1[:, :, :],
                                               ALU.mult, ALU.max).then_inc(f1_ready, 1)

            def stats2(s):
                dve.wait_ge(f2_full, s + 1)
                row_stats(s, own, half, LN_EPS_IN, ln_var, back_bufs)

            def norm2(s):
                row_norm(s, own, half, lambda q: norm[:, q, :], ln_log, 6 * s + 4, n2_ready, back_bufs)

            def stats3(s):
                dve.wait_ge(x1_ready, s + 1)
                row_stats(s, own, lambda q: x1[:, q, :], LN_EPS_OUT, ln_var, back_bufs)

            def norm3(s):
                row_norm(s, own, lambda q: x1[:, q, :], lambda q: norm[:, q, :], ln_log, 6 * s + 6, n3_ready,
                         back_bufs)

            def top2(s):
                dve.wait_ge(logits_full, s + 1)
                own.done(nc.vector.tensor_copy(logits[:, :, :].rearrange("p q e -> p (q e)"), bp[0][:, 0:TT * NE]))
                own.settle_apart(s, consts_set)
                for q in range(TT):
                    last = nc.vector.max(top_v[:, q, :], logits[:, q, :])
                own.done(last)
                own.settle_apart(s, consts_set)
                for q in range(TT):
                    last = nc.vector.max_index(top_i[:, q, :], top_v[:, q, :], logits[:, q, :])
                own.done(last)
                own.settle(s)
                own.done(nc.vector.tensor_copy(top_f[:, :, :], top_i[:, :, :]))
                own.settle(s)
                for k, pick in enumerate((pick1, pick2)):
                    own.done(nc.vector.tensor_tensor(pick[:, :, :], e_iota8[:, :].unsqueeze(1).to_broadcast([P, TT, NE]),
                                                     top_f[:, :, k:k + 1].to_broadcast([P, TT, NE]), ALU.is_equal))
                own.settle(s)
                nc.vector.tensor_tensor(picks[:, :, :], pick1[:, :, :], pick2[:, :, :], ALU.add).then_inc(picks_ready, 1)

            def slots(s):
                dve.wait_ge(rank_full, s + 1)
                wait(dve, scattered, 16 * 2 * TT * s)
                in_tile = bp[1][:, 0:TT * NE].rearrange("p (q e) -> p q e", q=TT)
                of_tile = bp[1][:, TT * NE:2 * TT * NE].rearrange("p (q e) -> p q e", q=TT)
                own.done(nc.vector.tensor_tensor(slot_f[:, :, :], in_tile,
                                                 e_base[:, :].unsqueeze(1).to_broadcast([P, TT, NE]), ALU.add))
                own.settle(s)
                for q in range(TT):
                    nc.vector.tensor_tensor(slot_f[:, q, :], slot_f[:, q, :], count[:, :], ALU.add)
                    own.done(nc.vector.tensor_tensor(count[:, :], count[:, :], of_tile[:, q, :], ALU.add))
                    own.settle(s)
                for k, pick in enumerate((pick1, pick2)):
                    own.done(nc.vector.tensor_tensor(prod[:, :, :], slot_f[:, :, :], pick[:, :, :], ALU.mult))
                    own.settle(s)
                    own.done(nc.vector.tensor_reduce(slot_s[:, k, :], prod[:, :, :], AX.X, ALU.add))
                    own.settle(s)
                nc.vector.tensor_copy(h3[:, :, DM].bitcast(U32), token_no[:, :])
                own.done(nc.vector.tensor_copy(slot_i[:, :, :], slot_s[:, :, :]))
                own.settle(s)
                nc.vector.tensor_scalar(token_no[:, :], token_no[:, :], float(L), None, ALU.add).then_inc(slots_ready, 1)
                own.finish()

            def recur(k, s):
                dve.wait_ge(exp_done, UNITS * s + k + 1)
                if k % 2 == 0:
                    dve.wait_ge(bx_ready, PAIRS * s + k // 2 + 1)
                bank = ss[k % NSS][:, :]
                nc.vector.tensor_tensor_scan(bank, bank, bx[:, (k // 2) % NBX, k % 2, :], 0.0,
                                             ALU.mult, ALU.add).then_inc(scan_done, 1)

            def times_c(k, s):
                dve.wait_ge(scan_done, UNITS * s + k + 1)
                if k < DS and k % 4 == 0:
                    dve.wait_ge(bc_loaded[k // 4], 32 * (s + 1))
                wait(dve, y_summed, UNITS * s + k + 1 - NHC)
                nc.vector.tensor_tensor(hc[:, k % NHC, :], ss[k % NSS][:, :], c_bc[:, k % DS, :],
                                        ALU.mult).then_inc(hc_ready, 1)

            def scans(s, n):
                if n == 0:
                    recur(0, s)
                for k in range(n * SLOT, (n + 1) * SLOT):
                    if k + 1 < UNITS:
                        recur(k + 1, s)
                    times_c(k, s)

            program(dve, prelude,
                    front={6: [stats_x], 9: [norm_x], 15: [conv(0)], 16: [conv(1)], 18: [conv(2)], 19: [conv(3)], 25: [relu(0)]},
                    gates={1: [relu(1)], 3: [relu(2)], 5: [relu(3)], 8: [read_y(0)], 16: [read_y(1)], 24: [read_y(2)]},
                    back={0: [read_y(3)], 4: [stats1], 7: [norm1], 14: [leaky], 16: [stats2], 18: [norm2],
                          21: [stats3], 23: [norm3], 28: [top2], 30: [slots]},
                    scan=scans)


def expert_program(nc, t, d, out, keep):
    ident, e_iota8, e_base, count = (keep[k] for k in ("ident", "e_iota8", "e_base", "count"))
    RB = ROWS // P
    MT = FF // P
    STEPS = B * L // ROWS
    ctx = ExitStack()
    with ctx:
        def sb(name, shape, dt=F32):
            return ctx.enter_context(nc.sbuf_tensor(name, shape, dt))

        def ps(name):
            return ctx.enter_context(nc.psum_tensor(name, [P, 512], F32))

        def sem(name):
            return ctx.enter_context(nc.semaphore(name))

        steps = sb("steps", [1, STEPS])
        tile_no = sb("tile_no", [1, NTILE])
        more = sb("more", [1, NE, STEPS])
        tiles = sb("tiles", [1, NE])
        t_end = sb("t_end", [1, NE])
        t_start = sb("t_start", [1, NE])
        one8 = sb("one8", [1, NE])
        origin = sb("origin", [1, NE])
        owned = sb("owned", [1, NTILE, NE])
        under = sb("under", [1, NTILE, NE])
        row_f = sb("row_f", [1, 3, NTILE])
        tab_f = sb("tab_f", [1, 2 * NTILE + NE])
        tab = sb("tab", [1, 2 * NTILE + NE], I32)
        pads = sb("pads", [P, RB, RW])
        rows = [sb(f"rows{i}", [P, RB, RW]) for i in range(2)]
        w1 = [sb(f"w1_{i}", [P, FT, FF]) for i in range(2)]
        w2 = [sb(f"w2_{i}", [P, MT, DM]) for i in range(2)]
        b1 = [sb(f"b1_{i}", [P, MT]) for i in range(2)]
        b2 = [sb(f"b2_{i}", [P, DM]) for i in range(2)]
        rows_t = [sb(f"rows_t{i}", [P, FT, ROWS]) for i in range(2)]
        hidden = [sb(f"hidden{i}", [P, MT, ROWS]) for i in range(2)]
        result = [sb(f"result{i}", [P, RB, DM]) for i in range(2)]
        acc = [sb(f"acc{i}", [P, TT, DM]) for i in range(2)]
        x1 = [sb(f"x1_{i}", [P, TT, DM]) for i in range(2)]
        gb = [sb(f"gb{i}", [P, DM]) for i in range(2)]
        up = [ps(f"up{i}") for i in range(4)]
        turn = [ps(f"turn{i}") for i in range(2)]
        down = [ps(f"down{i}") for i in range(2)]

        consts_in = sem("consts_in")
        tab_own = sem("tab_own")
        tab_ready = sem("tab_ready")
        padded = sem("padded")
        rows_in = [sem(f"rows_in{i}") for i in range(2)]
        w1_in = [sem(f"w1_in{i}") for i in range(2)]
        w2_in = [sem(f"w2_in{i}") for i in range(2)]
        turned = sem("turned")
        rows_t_ready = sem("rows_t_ready")
        up_full = sem("up_full")
        hidden_ready = sem("hidden_ready")
        down_full = sem("down_full")
        result_ready = sem("result_ready")
        added = sem("added")
        final_in = [sem(f"final_in{i}") for i in range(2)]
        scaled = sem("scaled")
        final_ready = sem("final_ready")
        out_stored = [sem(f"out_stored{i}") for i in range(2)]

        block = ctx.enter_context(nc.Block())

        @block.sync
        def _(sp):
            sp.dma_start(steps[:, :], t["steps"]).then_inc(consts_in, 16)
            sp.dma_start(tile_no[:, :], t["tile_no"]).then_inc(consts_in, 16)
            sp.dma_start(pads[:, :, :], d["pads"]).then_inc(consts_in, 16)
            sp.wait_ge(consts_in, 48)
            sp.wait_ge(tab_ready, 1)
            for e in range(NE):
                end = sp.value_load(tab[0:1, 2 * NTILE + e:2 * NTILE + e + 1], min_val=0, max_val=NE * CAP - ROWS)
                sp.dma_start(d["region"][bass.ds(end, ROWS), :].rearrange("(k p) n -> p k n", p=P),
                             pads[:, :, :]).then_inc(padded, 16)
            sp.wait_ge(padded, 16 * NE)

            def load_tile(j, par, i):
                row = sp.value_load(tab[0:1, bass.ds(j, 1)], min_val=0, max_val=IDLE_ROW)
                e = sp.value_load(tab[0:1, bass.ds(j + NTILE, 1)], min_val=0, max_val=NE - 1)
                wait(sp, added, 32 * (j - 1))
                sp.dma_start(rows[par][:, :, :],
                             d["region"][bass.ds(row, ROWS), :].rearrange("(k p) n -> p k n", p=P)).then_inc(rows_in[par], 16)
                sp.dma_start(w1[par][:, :, :],
                             t["w1"][e, :, :].rearrange("(k p) n -> p k n", p=P)).then_inc(w1_in[par], 16)
                sp.dma_start(b1[par][:, :], t["b1"][e, :, :]).then_inc(w1_in[par], 16)
                sp.dma_start(w2[par][:, :, :],
                             t["w2"][e, :, :].rearrange("(k p) n -> p k n", p=P)).then_inc(w2_in[par], 16)
                sp.dma_start(b2[par][:, :], t["b2"][bass.ds(e, 1), :].to_broadcast([P, DM])).then_inc(w2_in[par], 16)

            load_tile(0, 0, 0)
            load_tile(1, 1, 0)
            with sp.Fori(0, NTILE // 2 - 1) as i:
                load_tile(2 * i + 2, 0, i + 1)
                load_tile(2 * i + 3, 1, i + 1)
            sp.wait_ge(added, 32 * NTILE)

            def load_final(s, par):
                wait(sp, out_stored[par], 16 * (s // 2))
                sp.dma_start(acc[par][:, :, :],
                             d["acc3"][s, :, :].rearrange("(k p) n -> p k n", p=P)).then_inc(final_in[par], 16)
                sp.dma_start(x1[par][:, :, :],
                             d["x1"][s, :, :].rearrange("(k p) n -> p k n", p=P)).then_inc(final_in[par], 16)
                sp.dma_start(gb[par][:, :],
                             d["mod_rows"][s, 4:5, :].to_broadcast([P, DM])).then_inc(final_in[par], 16)

            for s in range(B):
                load_final(s, s % 2)
                if s:
                    sp.wait_ge(final_ready, s)
                    sp.dma_start(out[s - 1, :, :].rearrange("(k p) n -> p k n", p=P),
                                 acc[(s - 1) % 2][:, :, :]).then_inc(out_stored[(s - 1) % 2], 16)
            sp.wait_ge(final_ready, B)
            sp.dma_start(out[B - 1, :, :].rearrange("(k p) n -> p k n", p=P),
                         acc[(B - 1) % 2][:, :, :]).then_inc(out_stored[(B - 1) % 2], 16)
            for par in range(2):
                sp.wait_ge(out_stored[par], 16 * (B // 2))

        @block.gpsimd
        def _(pool):
            def add_rows(j, par):
                pool.wait_ge(result_ready, j + 1)
                for k in range(RB):
                    wait_apart(pool, added, RB * 16 * j + 16 * k, tab_ready)
                    nc.gpsimd.indirect_dma_start(
                        d["acc"], bass.IndirectOffsetOnAxis(rows[par][:, k, DM:RW].bitcast(U32), 0),
                        result[par][:, k, :], None, compute_op=ALU.add).then_inc(added, 16)

            add_rows(0, 0)
            add_rows(1, 1)
            with pool.Fori(0, NTILE // 2 - 1) as i:
                add_rows(2 * i + 2, 0)
                add_rows(2 * i + 3, 1)
            pool.wait_ge(added, 32 * NTILE)

        @block.scalar
        def _(act):
            def relu(j, par, i):
                act.wait_ge(w1_in[par], 32 * (i + 1))
                if not isinstance(j, int):
                    act.wait_ge(down_full, j - 1)
                for c in range(4):
                    act.wait_ge(up_full, 4 * j + c + 1)
                    for m in (2 * c, 2 * c + 1):
                        last = nc.scalar.activation(hidden[par][:, m, :], up[c][:, (m % 2) * ROWS:(m % 2 + 1) * ROWS],
                                                    ACT.Relu, bias=b1[par][:, m:m + 1])
                    last.then_inc(hidden_ready, 1)

            relu(0, 0, 0)
            relu(1, 1, 0)
            with act.Fori(0, NTILE // 2 - 1) as i:
                relu(2 * i + 2, 0, i + 1)
                relu(2 * i + 3, 1, i + 1)

        @block.tensor
        def _(pe):
            def turn_rows(j, par, i):
                pe.wait_ge(rows_in[par], 16 * (i + 1))
                wait(pe, rows_t_ready, j - 1)
                for f in range(FT):
                    for k in range(RB):
                        last = nc.tensor.transpose(turn[par][:, f * ROWS + k * P:f * ROWS + (k + 1) * P],
                                                   rows[par][:, k, f * P:(f + 1) * P], ident[:, :])
                last.then_inc(turned, 1)

            def up_product(j, par, i):
                pe.wait_ge(rows_t_ready, j + 1)
                pe.wait_ge(w1_in[par], 32 * (i + 1))
                for c in range(4):
                    wait(pe, hidden_ready, 4 * j - 4 + c + 1)
                    for m in (2 * c, 2 * c + 1):
                        for f in range(FT):
                            last = nc.tensor.matmul(up[c][:, (m % 2) * ROWS:(m % 2 + 1) * ROWS],
                                                    w1[par][:, f, m * P:(m + 1) * P], rows_t[par][:, f, :],
                                                    start=(f == 0), stop=(f == FT - 1))
                    last.then_inc(up_full, 1)

            def down_product(j, par, i):
                pe.wait_ge(w2_in[par], 32 * (i + 1))
                pe.wait_ge(hidden_ready, 4 * (j + 1))
                wait(pe, result_ready, j - 1)
                for k in range(RB):
                    for m in range(MT):
                        last = nc.tensor.matmul(down[par][:, k * DM:(k + 1) * DM], hidden[par][:, m, k * P:(k + 1) * P],
                                                w2[par][:, m, :], start=(m == 0), stop=(m == MT - 1))
                last.then_inc(down_full, 1)

            def pair(i, more_tiles):
                up_product(2 * i, 0, i)
                turn_rows(2 * i + 1, 1, i)
                down_product(2 * i, 0, i)
                up_product(2 * i + 1, 1, i)
                if more_tiles:
                    turn_rows(2 * i + 2, 0, i + 1)
                down_product(2 * i + 1, 1, i)

            turn_rows(0, 0, 0)
            pair(0, True)
            with pe.Fori(0, NTILE // 2 - 2) as i:
                pair(i + 1, True)
            pair(NTILE // 2 - 1, False)

        @block.vector
        def _(dve):
            n = [0]

            def link(ins):
                n[0] += 1
                ins.then_inc(tab_own, 1)
                dve.wait_ge(tab_own, n[0])

            dve.wait_ge(consts_in, 48)
            nc.vector.memset(one8[:, :], 1.0)
            link(nc.vector.tensor_tensor(more[:, :, :], count[0:1, :].unsqueeze(2).to_broadcast([1, NE, STEPS]),
                                         steps[:, :].unsqueeze(1).to_broadcast([1, NE, STEPS]), ALU.is_gt))
            link(nc.vector.tensor_reduce(tiles[:, :], more[:, :, :], AX.X, ALU.add))
            link(nc.vector.tensor_tensor_scan(t_end[:, :], one8[:, :], tiles[:, :], 0.0, ALU.mult, ALU.add))
            link(nc.vector.tensor_tensor(t_start[:, :], t_end[:, :], tiles[:, :], ALU.subtract))
            link(nc.vector.scalar_tensor_tensor(origin[:, :], t_start[:, :], -float(ROWS), e_base[0:1, :],
                                                ALU.mult, ALU.add))
            tile_b = tile_no[:, :].unsqueeze(2).to_broadcast([1, NTILE, NE])

            def per_tile(x):
                return x.unsqueeze(1).to_broadcast([1, NTILE, NE])

            link(nc.vector.tensor_tensor(owned[:, :, :], tile_b, per_tile(t_start[:, :]), ALU.is_ge))
            link(nc.vector.tensor_tensor(under[:, :, :], tile_b, per_tile(t_end[:, :]), ALU.is_lt))
            link(nc.vector.tensor_tensor(owned[:, :, :], owned[:, :, :], under[:, :, :], ALU.mult))
            link(nc.vector.tensor_reduce(row_f[:, 0, :], owned[:, :, :], AX.X, ALU.add))
            link(nc.vector.tensor_tensor(under[:, :, :], owned[:, :, :], per_tile(origin[:, :]), ALU.mult))
            link(nc.vector.tensor_reduce(row_f[:, 1, :], under[:, :, :], AX.X, ALU.add))
            link(nc.vector.tensor_tensor(under[:, :, :], owned[:, :, :], per_tile(e_iota8[0:1, :]), ALU.mult))
            link(nc.vector.tensor_reduce(tab_f[:, NTILE:2 * NTILE], under[:, :, :], AX.X, ALU.add))
            link(nc.vector.tensor_scalar(row_f[:, 2, :], tile_no[:, :], float(ROWS), -float(IDLE_ROW),
                                         ALU.mult, ALU.add))
            link(nc.vector.tensor_tensor(row_f[:, 2, :], row_f[:, 2, :], row_f[:, 0, :], ALU.mult))
            link(nc.vector.scalar_tensor_tensor(tab_f[:, 0:NTILE], row_f[:, 2, :], float(IDLE_ROW), row_f[:, 1, :],
                                                ALU.add, ALU.add))
            link(nc.vector.tensor_tensor(tab_f[:, 2 * NTILE:], e_base[0:1, :], count[0:1, :], ALU.add))
            nc.vector.tensor_copy(tab[:, :], tab_f[:, :]).then_inc(tab_ready, 1)

            def copy_rows(j, par):
                dve.wait_ge(turned, j + 1)
                wait(dve, up_full, 4 * (j - 1))
                nc.vector.tensor_copy(rows_t[par][:, :, :].rearrange("p f n -> p (f n)"),
                                      turn[par][:, :]).then_inc(rows_t_ready, 1)

            def bias_rows(j, par, i):
                dve.wait_ge(w2_in[par], 32 * (i + 1))
                dve.wait_ge(down_full, j + 1)
                wait(dve, added, 32 * (j - 1))
                nc.vector.tensor_tensor(result[par][:, :, :], down[par][:, :].rearrange("p (k n) -> p k n", k=RB),
                                        b2[par][:, :].unsqueeze(1).to_broadcast([P, RB, DM]),
                                        ALU.add).then_inc(result_ready, 1)

            def pair(i, more_tiles):
                copy_rows(2 * i + 1, 1)
                bias_rows(2 * i, 0, i)
                if more_tiles:
                    copy_rows(2 * i + 2, 0)
                bias_rows(2 * i + 1, 1, i)

            copy_rows(0, 0)
            pair(0, True)
            with dve.Fori(0, NTILE // 2 - 2) as i:
                pair(i + 1, True)
            pair(NTILE // 2 - 1, False)

            for s in range(B):
                par = s % 2
                dve.wait_ge(final_in[par], 48 * (s // 2 + 1))
                nc.vector.tensor_tensor(acc[par][:, :, :], acc[par][:, :, :],
                                        gb[par][:, :].unsqueeze(1).to_broadcast([P, TT, DM]), ALU.mult).then_inc(scaled, 1)
                dve.wait_ge(scaled, s + 1)
                nc.vector.tensor_tensor(acc[par][:, :, :], acc[par][:, :, :], x1[par][:, :, :],
                                        ALU.add).then_inc(final_ready, 1)


def build(nc, t, out):
    d = {
        "mod_rows": nc.dram_tensor("mod_rows", (B, 5, DM), F32).ap(),
        "bc": nc.dram_tensor("bc", (2 * DS, L), F32).ap(),
        "x1": nc.dram_tensor("x1_rows", (B, L, DM), F32).ap(),
        "region": nc.dram_tensor("region", (IDLE_ROW + ROWS, RW), F32).ap(),
        "pads": nc.dram_tensor("pad_tile", (P, 2, RW), F32).ap(),
        "acc": nc.dram_tensor("expert_sum", (DUMP + P, DM), F32).ap(),
    }
    d["acc3"] = d["acc"][0:B * L, :].rearrange("(s l) n -> s l n", s=B)
    with ExitStack() as ctx:
        keep = {name: ctx.enter_context(nc.sbuf_tensor(name, [P, n], F32)) for name, n in
                (("ident", P), ("ones", P), ("e_iota8", NE), ("e_base", NE), ("count", NE))}
        scan_program(nc, t, d, keep)
        expert_program(nc, t, d, out, keep)


def kernel(**inputs):
    import numpy as np
    import concourse.bacc as bacc
    from concourse.bass_utils import run_bass_kernel_spmd

    a = {k: np.asarray(v) for k, v in inputs.items()}
    m = {k[len("L0_attn_"):]: v for k, v in a.items() if k.startswith("L0_attn_")}
    f = {k[len("L0_ffn_"):]: v for k, v in a.items() if k.startswith("L0_ffn_")}
    q = np.arange(P)
    arrays = {
        "x": m["x"], "cond_t": a["L0_c"].T, "wmod": a["L0_wmod"],
        "in_proj_t": m["in_proj_w"].T, "conv_w": m["conv_w"], "conv_b": m["conv_b"].reshape(JT, P).T,
        "x_proj_t": m["x_proj_w"].T, "dt_proj_t": m["dt_proj_w"].T, "dt_b": m["dt_proj_b"].reshape(JT, P).T,
        "A_log": m["A_log"], "D": m["D"].reshape(JT, P).T, "out_proj_t": m["out_proj_w"].T,
        "ln1_w": m["ln1_w"].reshape(FT, P).T, "ln1_b": m["ln1_b"].reshape(FT, P).T,
        "ffn_w1_t": m["ffn_w1"].T, "ffn_b1": m["ffn_b1"].reshape(JT, P).T, "ffn_w2_t": m["ffn_w2"].T,
        "ffn_b2": m["ffn_b2"].reshape(1, DM), "ln2_w": m["ln2_w"].reshape(1, DM), "ln2_b": m["ln2_b"].reshape(1, DM),
        "gate_w": f["gate_w"], "gate_b": f["gate_b"].reshape(1, NE), "w1": f["w1"],
        "b1": f["b1"].reshape(NE, FF // P, P).transpose(0, 2, 1), "w2": f["w2"], "b2": f["b2"],
        "ident": np.eye(P, dtype=np.float32), "before": (q[:, None] < q[None, :]).astype(np.float32),
        "e_iota": np.arange(NE, dtype=np.float32).reshape(1, NE),
        "e_base": (np.arange(NE) * CAP).astype(np.float32).reshape(1, NE),
        "token_no": np.arange(L, dtype=np.float32).reshape(TT, P).T,
        "steps": (np.arange(B * L // ROWS) * ROWS).astype(np.float32).reshape(1, -1),
        "tile_no": np.arange(NTILE, dtype=np.float32).reshape(1, NTILE),
    }
    arrays = {k: np.ascontiguousarray(v) for k, v in arrays.items()}
    nc = bacc.Bacc("TRN2", target_bir_lowering=False, num_devices=1)
    t = {k: nc.dram_tensor(f"in_{k}", v.shape, mybir.dt.from_np(v.dtype), kind="ExternalInput").ap()
         for k, v in arrays.items()}
    out = nc.dram_tensor("out", (B, L, DM), F32, kind="ExternalOutput").ap()
    build(nc, t, out)
    r = run_bass_kernel_spmd(nc, [{f"in_{k}": v for k, v in arrays.items()}], core_ids=[0])
    return r.results[0]["out"]
```

```python
import concourse.bass as bass
from concourse import mybir
from contextlib import ExitStack

B, L, DM = 8, 512, 256
DI, DS, DC, DTR = 512, 16, 4, 16
NE, FF = 8, 1024
P = 128
TT = L // P
FT = DM // P
JT = DI // P
UNITS = JT * DS
SLOT = 2
NSLOT = UNITS // SLOT
PAIRS = UNITS // 2
NBX = 3
NHC = 4
NSS = 3
ROWS = 256
CAP = B * L + ROWS
NTILE = (2 * B * L + NE * (ROWS - 1)) // ROWS
IDLE_ROW = NE * CAP
RW = DM + 2
LN_EPS_OUT, LN_EPS_IN = 1e-5, 1e-12
SLOPE = 0.01
ROOT_GUESS = 0x5F3759DF
NEWTON = 3

F32 = mybir.dt.float32
U32 = mybir.dt.uint32
I32 = mybir.dt.int32
ALU = mybir.AluOpType
ACT = mybir.ActivationFunctionType
AX = mybir.AxisListType


def wait(engine, sem, value):
    if isinstance(value, int) and value <= 0:
        return
    engine.wait_ge(sem, value)


def wait_apart(engine, sem, value, long_done):
    if not isinstance(value, int):
        value = engine.to_reg(value)
    engine.wait_ge(long_done, 1)
    wait(engine, sem, value)


class Ordered:

    def __init__(self, engine, sem, n):
        self.engine, self.sem, self.n, self.at = engine, sem, n, 0

    def done(self, ins):
        self.at += 1
        ins.then_inc(self.sem, 1)

    def settle(self, seq):
        wait(self.engine, self.sem, seq * self.n + self.at)

    def settle_apart(self, seq, long_done):
        wait_apart(self.engine, self.sem, seq * self.n + self.at, long_done)

    def finish(self):
        assert self.at == self.n, (self.at, self.n)
        self.at = 0


def scan_program(nc, t, d, out, keep):
    ident, ones, zero_bias, e_iota8, e_base, count = (
        keep[k] for k in ("ident", "ones", "zero_bias", "e_iota8", "e_base", "count"))
    ctx = ExitStack()
    with ctx:
        def sb(name, shape, dt=F32):
            return ctx.enter_context(nc.sbuf_tensor(name, shape, dt))

        def sem(name):
            return ctx.enter_context(nc.semaphore(name))

        w_in = sb("w_in", [P, FT, 2 * DI])
        w_x = sb("w_x", [P, JT, DTR + 2 * DS])
        w_dt = sb("w_dt", [DTR, DI])
        w_out = sb("w_out", [P, JT, DM])
        w_f1 = sb("w_f1", [P, FT, 2 * DM])
        w_f2 = sb("w_f2", [P, JT, DM])
        w_gate = sb("w_gate", [P, FT, NE])
        conv_w = sb("conv_w", [P, JT, DC])
        conv_b = sb("conv_b", [P, JT])
        dt_b = sb("dt_b", [P, JT])
        d_skip = sb("d_skip", [P, JT])
        f1_b = sb("f1_b", [P, JT])
        ln1_w = sb("ln1_w", [P, FT])
        ln1_b = sb("ln1_b", [P, FT])
        a_neg = sb("a_neg", [P, JT, DS])
        f2_b = sb("f2_b", [1, DM])
        gate_b = sb("gate_b", [1, NE])
        before = sb("before", [P, P])
        token_no = sb("token_no", [P, 2, TT])
        mod_col = sb("mod_col", [P, 4, B])
        mod_now = sb("mod_now", [P, 4])
        xrow = sb("xrow", [P, TT, DM])
        h_t = sb("h_t", [P, FT, L])
        h_res = sb("h_res", [P, FT, L])
        xs = sb("xs", [P, 2, JT, L])
        zs = sb("zs", [P, JT, L])
        x_dbl = sb("x_dbl", [DTR + 2 * DS, L])
        relu_dt = sb("relu_dt", [P, 2, L])
        dt = sb("dt", [P, JT, L])
        u = sb("u", [P, JT, L])
        b_bc = sb("b_bc", [P, DS, L])
        c_bc = sb("c_bc", [P, DS, L])
        bx = sb("bx", [P, NBX, 2, L])
        hc = sb("hc", [P, NHC, L])
        yg = sb("yg", [P, JT, L])
        norm = sb("norm", [P, TT, DM])
        h2_t = sb("h2_t", [P, FT, L])
        f1 = sb("f1", [P, JT, L])
        mod_row = sb("mod_row", [P, 4, DM])
        x1 = sb("x1", [P, TT, DM])
        h3 = sb("h3", [P, TT, RW])
        stats = sb("stats", [P, TT, 6])
        mv = sb("mv", [P, TT, 2])
        lnv = sb("lnv", [P, TT])
        rstd = sb("rstd", [P, TT])
        tmp = sb("tmp", [P, TT])
        stats0 = sb("stats0", [P, TT, 6])
        mv0 = sb("mv0", [P, TT, 2])
        lnv0 = sb("lnv0", [P, TT])
        rstd0 = sb("rstd0", [P, TT])
        tmp0 = sb("tmp0", [P, TT])
        logits = sb("logits", [P, TT, NE])
        top_v = sb("top_v", [P, TT, 8])
        top_i = sb("top_i", [P, TT, 8], U32)
        top_f = sb("top_f", [P, TT, 8])
        pick1 = sb("pick1", [P, TT, NE])
        pick2 = sb("pick2", [P, TT, NE])
        picks = sb("picks", [P, TT, NE])
        slot_f = sb("slot_f", [P, TT, NE])
        prod = sb("prod", [P, TT, NE])
        slot_s = sb("slot_s", [P, 2, TT])
        slot_i = sb("slot_i", [P, 2, TT], U32)
        flat_b = b_bc[:, :, :].rearrange("p n l -> p (n l)")
        w_mod = flat_b[:, 0:FT * 6 * DM].rearrange("p (k n) -> p k n", k=FT)
        cond_t = flat_b[:, 3072:3072 + FT * B].rearrange("p (k b) -> p k b", k=FT)
        mod8 = flat_b[0:B, 3328:3328 + 6 * DM].rearrange("p (k n) -> p k n", k=6)
        row8 = flat_b[0:B, 4864:4864 + 5 * DM].rearrange("p (k n) -> p k n", k=5)
        ln2w8 = flat_b[0:B, 6144:6144 + DM]
        ln2b8 = flat_b[0:B, 6400:6400 + DM]
        mag8 = flat_b[0:B, 6656:6656 + 2 * DM].rearrange("p (k n) -> p k n", k=2)
        sgn8 = flat_b[0:B, 7168:7168 + 2 * DM].rearrange("p (k n) -> p k n", k=2)
        flat_c = c_bc[:, :, :].rearrange("p n l -> p (n l)")
        pad_rows = flat_c[:, 0:2 * RW].rearrange("p (k n) -> p k n", k=2)
        pad_no = flat_c[:, 1024:1026]

        ss = [ctx.enter_context(nc.psum_tensor(f"ss{i}", [P, L], F32)) for i in range(NSS)]
        ysum = ctx.enter_context(nc.psum_tensor("ysum", [P, L], F32))
        fp = [ctx.enter_context(nc.psum_tensor(f"fp{i}", [P, L], F32)) for i in range(2)]
        bp = [ctx.enter_context(nc.psum_tensor(f"bp{i}", [P, L], F32)) for i in range(2)]

        loaded = sem("loaded")
        rows_stored = sem("rows_stored")
        inits_stored = sem("inits_stored")
        x_loaded = sem("x_loaded")
        res_loaded = sem("res_loaded")
        bc_stored = sem("bc_stored")
        bc_loaded = [sem(f"bc_loaded{g}") for g in range(4)]
        x1_stored = sem("x1_stored")
        scattered = sem("scattered")
        consts_set = sem("consts_set")
        pool_set = sem("pool_set")
        cond_silu = sem("cond_silu")
        mod_full = sem("mod_full")
        mod_copied = sem("mod_copied")
        a_ready = sem("a_ready")
        rows_ready = sem("rows_ready")
        x_normed = sem("x_normed")
        xt_full = sem("xt_full")
        h_ready = sem("h_ready")
        xin_full = sem("xin_full")
        tap_last = sem("tap_last")
        conv_done = sem("conv_done")
        xs_ready = sem("xs_ready")
        zin_full = sem("zin_full")
        z_copied = sem("z_copied")
        z_ready = sem("z_ready")
        xproj_full = sem("xproj_full")
        xdbl_ready = sem("xdbl_ready")
        dt_full = sem("dt_full")
        log_ready = sem("log_ready")
        relu_ready = sem("relu_ready")
        dt_ready = sem("dt_ready")
        u_ready = sem("u_ready")
        exp_done = sem("exp_done")
        bx_ready = sem("bx_ready")
        scan_done = sem("scan_done")
        hc_ready = sem("hc_ready")
        y_summed = sem("y_summed")
        y_read = sem("y_read")
        y_gated = sem("y_gated")
        out_full = sem("out_full")
        res_copied = sem("res_copied")
        n1_ready = sem("n1_ready")
        n1t_full = sem("n1t_full")
        h2_ready = sem("h2_ready")
        f1_full = sem("f1_full")
        f1_copied = sem("f1_copied")
        f1_ready = sem("f1_ready")
        f2_full = sem("f2_full")
        n2_ready = sem("n2_ready")
        x1_ready = sem("x1_ready")
        n3_ready = sem("n3_ready")
        h3_ready = sem("h3_ready")
        h3t_full = sem("h3t_full")
        h3t_ready = sem("h3t_ready")
        logits_full = sem("logits_full")
        picks_ready = sem("picks_ready")
        rank_full = sem("rank_full")
        slots_ready = sem("slots_ready")
        v_own = sem("v_own")
        vf_own = sem("vf_own")
        p_own = sem("p_own")
        a_own = sem("a_own")
        v0_own = sem("v0_own")
        vt_own = sem("vt_own")
        pp_own = sem("pp_own")
        tap_own = sem("tap_own")

        NW = 26

        block = ctx.enter_context(nc.Block())

        def program(engine, prelude, front, gates, back, tail, scan):
            def slots(f, g, k, s, e):
                for n in range(NSLOT):
                    if s is not None:
                        scan(s, n)
                    for table, seq in ((gates, g), (tail, e), (back, k), (front, f)):
                        if seq is not None:
                            for step in table.get(n, ()):
                                step(seq)
            prelude()
            slots(0, None, None, None, None)
            slots(1, 0, None, 0, None)
            slots(2, 1, 0, 1, None)
            slots(3, 2, 1, 2, 0)
            with engine.Fori(0, B - 4) as i:
                slots(i + 4, i + 3, i + 2, i + 3, i + 1)
            slots(None, B - 1, B - 2, B - 1, B - 3)
            slots(None, None, B - 1, None, B - 2)
            slots(None, None, None, None, B - 1)

        @block.sync
        def _(sp):
            def prelude():
                for dst, src in (
                    (w_mod, t["wmod"].rearrange("(k p) n -> p k n", p=P)),
                    (cond_t, t["cond_t"].rearrange("(k p) b -> p k b", p=P)),
                    (w_in[:, :, :], t["in_proj_t"].rearrange("(k p) n -> p k n", p=P)),
                    (conv_w[:, :, :], t["conv_w"].rearrange("(j p) k -> p j k", p=P)),
                    (conv_b[:, :], t["conv_b"]),
                    (w_x[:, :, :], t["x_proj_t"].rearrange("(k p) n -> p k n", p=P)),
                    (w_dt[:, :], t["dt_proj_t"]),
                    (dt_b[:, :], t["dt_b"]),
                    (a_neg[:, :, :], t["A_log"].rearrange("(j p) n -> p j n", p=P)),
                    (d_skip[:, :], t["D"]),
                    (w_out[:, :, :], t["out_proj_t"].rearrange("(k p) n -> p k n", p=P)),
                    (w_f1[:, :, :], t["ffn_w1_t"].rearrange("(k p) n -> p k n", p=P)),
                    (w_f2[:, :, :], t["ffn_w2_t"].rearrange("(k p) n -> p k n", p=P)),
                    (w_gate[:, :, :], t["gate_w"].rearrange("(k p) n -> p k n", p=P)),
                    (f1_b[:, :], t["ffn_b1"]),
                    (ln1_w[:, :], t["ln1_w"]),
                    (ln1_b[:, :], t["ln1_b"]),
                    (f2_b[:, :], t["ffn_b2"]),
                    (gate_b[:, :], t["gate_b"]),
                    (ln2w8, t["ln2_w"].to_broadcast([B, DM])),
                    (ln2b8, t["ln2_b"].to_broadcast([B, DM])),
                    (ident[:, :], t["ident"]),
                    (before[:, :], t["before"]),
                    (e_base[:, :], t["e_base"].to_broadcast([P, NE])),
                    (e_iota8[:, :], t["e_iota"].to_broadcast([P, NE])),
                    (token_no[:, 0, :], t["token_no"]),
                ):
                    sp.dma_start(dst, src).then_inc(loaded, 16)
                sp.wait_ge(rows_ready, 1)
                sp.dma_start(d["mod_rows"], row8[:, 0:4, :]).then_inc(rows_stored, 16)
                sp.dma_start(d["gate_rows"][0:B, :], row8[:, 4, :]).then_inc(rows_stored, 16)
                sp.wait_ge(pool_set, 1)
                sp.dma_start(d["gate_rows"][B:B + 1, :], pad_rows[0:1, 0, 0:DM]).then_inc(rows_stored, 16)
                sp.wait_ge(rows_stored, 48)
                sp.dma_start(d["region"][IDLE_ROW:IDLE_ROW + ROWS, :].rearrange("(k p) n -> p k n", p=P),
                             pad_rows).then_inc(inits_stored, 16)
                sp.dma_start(d["pads"], pad_rows).then_inc(inits_stored, 16)
                sp.wait_ge(inits_stored, 32)

            def load_x(s):
                wait(sp, x_normed, s)
                sp.dma_start(xrow[:, :, :], t["x"][s, :, :].rearrange("(k p) n -> p k n", p=P)).then_inc(x_loaded, 16)

            def store_bc(s):
                sp.wait_ge(xdbl_ready, s + 1)
                sp.dma_start(d["bc"], x_dbl[DTR:DTR + 2 * DS, :]).then_inc(bc_stored, 16)
                sp.wait_ge(bc_stored, 16 * (s + 1))

            def load_bc(g):
                def step(s):
                    wait(sp, hc_ready, s * UNITS - (UNITS - (JT - 1) * DS - 4 * (g + 1)))
                    n = slice(4 * g, 4 * g + 4)
                    for dst, at in ((b_bc, 0), (c_bc, DS)):
                        src = d["bc"][at + 4 * g:at + 4 * g + 4, :].unsqueeze(0).to_broadcast([P, 4, L])
                        sp.dma_start(dst[:, n, :], src).then_inc(bc_loaded[g], 16)
                return step

            def load_res(s):
                wait(sp, x1_stored, 16 * s)
                wait(sp, n3_ready, s)
                wait(sp, h3_ready, s)
                sp.dma_start(x1[:, :, :], t["x"][s, :, :].rearrange("(k p) n -> p k n", p=P)).then_inc(res_loaded, 16)
                sp.dma_start(mod_row[:, :, :],
                             d["mod_rows"][bass.ds(s, 1), :, :].to_broadcast([P, 4, DM])).then_inc(res_loaded, 16)

            def store_x1(s):
                sp.wait_ge(x1_ready, s + 1)
                sp.dma_start(out[s, :, :].rearrange("(k p) n -> p k n", p=P), x1[:, :, :]).then_inc(x1_stored, 16)

            program(sp, prelude,
                    front={0: [load_x], 25: [store_bc], 26: [load_bc(0)], 28: [load_bc(1)],
                           30: [load_bc(2)], 31: [load_bc(3)]},
                    gates={}, back={6: [load_res]}, tail={0: [store_x1]}, scan=lambda s, n: None)
            sp.wait_ge(x1_stored, 16 * B)

        @block.gpsimd
        def _(pool):
            own = Ordered(pool, p_own, 3)

            def prelude():
                nc.gpsimd.memset(flat_c[:, 0:4096], 0.0).then_inc(pp_own, 1)
                pool.wait_ge(pp_own, 1)
                nc.gpsimd.iota(pad_no[:, 0:1].bitcast(U32), [[0, 1]], base=0, channel_multiplier=1)
                nc.gpsimd.iota(pad_no[:, 1:2].bitcast(U32), [[0, 1]], base=B, channel_multiplier=0).then_inc(pp_own, 1)
                pool.wait_ge(pp_own, 2)
                for k in range(2):
                    last = nc.gpsimd.tensor_copy(pad_rows[:, k, DM:RW].bitcast(U32), pad_no.bitcast(U32))
                last.then_inc(pool_set, 1)

            def times_dt(j):
                def step(s):
                    pool.wait_ge(dt_ready, s * JT + j + 1)
                    nc.gpsimd.tensor_tensor(u[:, j, :], dt[:, j, :], xs[:, s % 2, j, :], ALU.mult).then_inc(u_ready, 1)
                return step

            def gate_y(j):
                def step(s):
                    pool.wait_ge(y_read, JT * s + j + 1)
                    pool.wait_ge(z_ready, s + 1)
                    nc.gpsimd.tensor_tensor(yg[:, j, :], yg[:, j, :], zs[:, j, :], ALU.mult).then_inc(y_gated, 1)
                return step

            def row(k):
                return mod_row[:, k, :].unsqueeze(1).to_broadcast([P, TT, DM])

            def scale_n2(s):
                pool.wait_ge(n2_ready, s + 1)
                pool.wait_ge(res_loaded, 32 * (s + 1))
                own.done(nc.gpsimd.tensor_tensor(norm[:, :, :], norm[:, :, :], row(0), ALU.mult))

            def shift_n2(s):
                own.settle(s)
                own.done(nc.gpsimd.tensor_tensor(norm[:, :, :], norm[:, :, :], row(1), ALU.add))

            def residual(s):
                own.settle(s)
                nc.gpsimd.tensor_tensor(x1[:, :, :], norm[:, :, :], x1[:, :, :], ALU.add).then_inc(x1_ready, 1)

            def scale_n3(s):
                pool.wait_ge(n3_ready, s + 1)
                own.done(nc.gpsimd.tensor_tensor(norm[:, :, :], norm[:, :, :], row(2), ALU.mult))

            def shift_n3(s):
                own.settle(s)
                wait(pool, scattered, 16 * 2 * TT * s)
                nc.gpsimd.tensor_tensor(h3[:, :, 0:DM], norm[:, :, :], row(3), ALU.add).then_inc(h3_ready, 1)
                own.finish()

            def scatter(q):
                def step(s):
                    if q == 0:
                        wait_apart(pool, slots_ready, s + 1, pool_set)
                    for k in range(2):
                        nc.gpsimd.indirect_dma_start(
                            d["region"], bass.IndirectOffsetOnAxis(slot_i[:, k, q:q + 1], 0), h3[:, q, :], None,
                        ).then_inc(scattered, 16)
                return step

            def products(s, n):
                q, j, st = n, n * SLOT // DS, n * SLOT % DS
                if q % (DS // 2) == 0:
                    pool.wait_ge(u_ready, JT * s + j + 1)
                if j == 0 and st % 4 == 0:
                    pool.wait_ge(bc_loaded[st // 4], 32 * (s + 1))
                back_to = {0: -2, 1: 0, 2: -4}.get(q, 2 * q - 4)
                wait(pool, scan_done, UNITS * s + back_to)
                nc.gpsimd.tensor_tensor(bx[:, q % NBX, :, :], u[:, j, :].unsqueeze(1).to_broadcast([P, 2, L]),
                                        b_bc[:, st:st + 2, :], ALU.mult).then_inc(bx_ready, 1)

            program(pool, prelude,
                    front={29: [times_dt(0)], 30: [times_dt(1)]},
                    gates={4: [times_dt(2)], 5: [times_dt(3)],
                           14: [gate_y(0)], 19: [gate_y(1)], 27: [gate_y(2)]},
                    back={3: [gate_y(3)], 24: [scale_n2], 25: [shift_n2], 26: [residual], 29: [scale_n3],
                          30: [shift_n3]},
                    tail={6: [scatter(0)], 7: [scatter(1)], 8: [scatter(2)], 9: [scatter(3)]},
                    scan=products)
            pool.wait_ge(scattered, 16 * 2 * TT * B)

        @block.scalar
        def _(act):
            def prelude():
                act.wait_ge(loaded, 16 * NW)
                act.wait_ge(consts_set, 1)
                nc.scalar.activation(cond_t, cond_t, ACT.Silu).then_inc(cond_silu, 1)
                nc.scalar.preload_act_table_set("natural_log_exp_and_others")
                nc.scalar.activation(a_neg[:, :, :], a_neg[:, :, :], ACT.Exp).then_inc(a_ready, 1)
                act.wait_ge(a_ready, 1)
                nc.scalar.activation(a_neg[:, :, :], a_neg[:, :, :], ACT.Identity, scale=-1.0,
                                     bias=zero_bias[:, 0:1]).then_inc(a_ready, 1)
                act.wait_ge(a_ready, 2)

            def hidden(s):
                act.wait_ge(xt_full, s + 1)
                wait(act, res_copied, s)
                wait(act, zin_full, JT * s)
                act.wait_ge(mod_copied, 2 + s + 1)
                for f in range(FT):
                    nc.scalar.activation(h_t[:, f, :], fp[f][:, :], ACT.Identity, scale=mod_now[:, 2 + f:3 + f],
                                         bias=mod_now[:, f:f + 1]).then_inc(h_ready, 1)

            def tap(j):
                def step(s):
                    if j == 0:
                        wait(act, u_ready, JT * (s - 1))
                        wait(act, y_read, JT * (s - 1))
                    wait_apart(act, xin_full, JT * s + j + 1, consts_set)
                    nc.scalar.activation(xs[:, s % 2, j, :], fp[j % 2][:, :], ACT.Identity,
                                         scale=conv_w[:, j, DC - 1:DC], bias=conv_b[:, j:j + 1]).then_inc(tap_last, 1)
                return step

            def silu_x(s):
                wait_apart(act, conv_done, JT * (s + 1), consts_set)
                nc.scalar.activation(xs[:, s % 2, :, :], xs[:, s % 2, :, :], ACT.Silu).then_inc(xs_ready, 1)
                nc.scalar.preload_act_table_set("natural_log_exp_and_others")

            def silu_z(s):
                act.wait_ge(z_copied, JT * (s + 1))
                nc.scalar.activation(zs[:, :, :], zs[:, :, :], ACT.Silu).then_inc(z_ready, 1)
                nc.scalar.preload_act_table_set("natural_log_exp_and_others")

            def copy_z(j):
                def step(s):
                    act.wait_ge(zin_full, JT * s + j + 1)
                    if j == 0:
                        wait(act, y_gated, JT * s)
                    nc.scalar.activation(zs[:, j, :], fp[(1, 0, 1, 0)[j]][:, :], ACT.Identity,
                                         bias=zero_bias[:, 0:1]).then_inc(z_copied, 1)
                return step

            def copy_xdbl(s):
                act.wait_ge(xproj_full, s + 1)
                wait(act, bc_stored, 16 * s)
                wait(act, dt_full, JT * s)
                nc.scalar.activation(x_dbl[:, :], fp[0][0:DTR + 2 * DS, :], ACT.Identity,
                                     bias=zero_bias[0:DTR + 2 * DS, 0:1]).then_inc(xdbl_ready, 1)

            def softplus(j):
                def step(s):
                    act.wait_ge(dt_full, JT * s + j + 1)
                    wait(act, dt_ready, JT * s + j - 1)
                    bank = fp[(1, 0, 1, 0)[j]][:, :]
                    nc.scalar.activation(relu_dt[:, j % 2, :], bank, ACT.Relu, bias=dt_b[:, j:j + 1])
                    wait(act, exp_done, UNITS * (s - 1) + (j + 1) * DS)
                    nc.scalar.activation(dt[:, j, :], bank, ACT.Abs, bias=dt_b[:, j:j + 1]).then_inc(relu_ready, 1)
                    act.wait_ge(relu_ready, JT * s + j + 1)
                    nc.scalar.activation(dt[:, j, :], dt[:, j, :], ACT.Exp, scale=-1.0,
                                         bias=zero_bias[:, 0:1]).then_inc(a_own, 1)
                    act.wait_ge(a_own, JT * s + j + 1)
                    nc.scalar.activation(dt[:, j, :], dt[:, j, :], ACT.Ln, bias=ones[:, 0:1]).then_inc(log_ready, 1)
                return step

            def copy_res(s):
                wait(act, out_full, s)
                nc.scalar.activation(h_res[:, :, :], h_t[:, :, :], ACT.Identity,
                                     bias=zero_bias[:, 0:1]).then_inc(res_copied, 1)

            def hidden2(s):
                act.wait_ge(n1t_full, s + 1)
                wait(act, logits_full, s)
                for f in range(FT):
                    nc.scalar.activation(h2_t[:, f, :], bp[f][:, :], ACT.Identity, scale=ln1_w[:, f:f + 1],
                                         bias=ln1_b[:, f:f + 1]).then_inc(h2_ready, 1)

            def copy_f1(j):
                def step(s):
                    act.wait_ge(f1_full, JT * s + j + 1)
                    if j == 0:
                        wait(act, f2_full, s)
                    nc.scalar.activation(f1[:, j, :], bp[j % 2][:, :], ACT.Identity,
                                         bias=f1_b[:, j:j + 1]).then_inc(f1_copied, 1)
                return step

            def copy_h3(s):
                act.wait_ge(h3t_full, s + 1)
                for f in range(FT):
                    nc.scalar.activation(h2_t[:, f, :], bp[f][:, :], ACT.Identity,
                                         bias=zero_bias[:, 0:1]).then_inc(h3t_ready, 1)

            def decay(s, n):
                for k in range(n * SLOT, (n + 1) * SLOT):
                    j, st = divmod(k, DS)
                    if st == 0:
                        act.wait_ge(dt_ready, JT * s + j + 1)
                    before_it = {0: 0, 1: -2, 2: -1}.get(k, k - 2)
                    wait(act, hc_ready, UNITS * s + before_it)
                    nc.scalar.activation(ss[k % NSS][:, :], dt[:, j, :], ACT.Exp, scale=a_neg[:, j, st:st + 1],
                                         bias=zero_bias[:, 0:1]).then_inc(exp_done, 1)

            program(act, prelude,
                    front={14: [hidden], 16: [tap(0)], 17: [tap(1)], 19: [tap(2)], 20: [tap(3)],
                           22: [silu_x], 25: [copy_xdbl], 27: [softplus(0)], 28: [softplus(1)]},
                    gates={2: [softplus(2)], 3: [softplus(3)], 5: [copy_z(0)], 6: [copy_z(1)],
                           10: [copy_res], 11: [copy_z(2)], 12: [copy_z(3)], 13: [silu_z]},
                    back={12: [hidden2], 14: [copy_f1(0)], 15: [copy_f1(1)], 16: [copy_f1(2)], 17: [copy_f1(3)]},
                    tail={0: [copy_h3]},
                    scan=decay)

        @block.tensor
        def _(pe):
            def prelude():
                pe.wait_ge(loaded, 16 * NW)
                pe.wait_ge(cond_silu, 1)
                pe.wait_ge(consts_set, 1)
                for k in range(3):
                    for f in range(FT):
                        last = nc.tensor.matmul(ss[k][0:B, :], cond_t[:, f, :], w_mod[:, f, k * L:(k + 1) * L],
                                                start=(f == 0), stop=(f == FT - 1))
                last.then_inc(mod_full, 1)
                for c in range(4):
                    for f in range(FT):
                        last = nc.tensor.matmul(ysum[:, c * B:(c + 1) * B], w_mod[:, f, c * P:(c + 1) * P],
                                                cond_t[:, f, :], start=(f == 0), stop=(f == FT - 1))
                last.then_inc(mod_full, 1)

            def transposes(src, dst, width=None):
                for f in range(FT):
                    for q in range(TT):
                        last = nc.tensor.transpose(dst[f][:, q * P:(q + 1) * P], src[:, q, f * P:(f + 1) * P],
                                                   ident[:, :])
                return last

            def turn_x(s):
                pe.wait_ge(x_normed, s + 1)
                wait(pe, z_copied, JT * s)
                transposes(xrow, fp).then_inc(xt_full, 1)

            def in_proj(dst, col):
                for f in range(FT):
                    last = nc.tensor.matmul(dst, w_in[:, f, col:col + P], h_t[:, f, :],
                                            start=(f == 0), stop=(f == FT - 1))
                return last

            def x_in(j):
                def step(s):
                    pe.wait_ge(h_ready, FT * (s + 1))
                    if j >= 2:
                        pe.wait_ge(conv_done, JT * s + j - 1)
                    in_proj(fp[j % 2][:, :], j * P).then_inc(xin_full, 1)
                return step

            def z_in(j):
                def step(s):
                    if j < 2:
                        pe.wait_ge(relu_ready, JT * s + j + 3)
                    else:
                        pe.wait_ge(z_copied, JT * s + j - 1)
                    in_proj(fp[(1, 0, 1, 0)[j]][:, :], DI + j * P).then_inc(zin_full, 1)
                return step

            def x_proj(half):
                def step(s):
                    if half == 0:
                        pe.wait_ge(xs_ready, s + 1)
                    for j in (2 * half, 2 * half + 1):
                        last = nc.tensor.matmul(fp[0][0:DTR + 2 * DS, :], w_x[:, j, :], xs[:, s % 2, j, :],
                                                start=(j == 0), stop=(j == JT - 1))
                    if half == 1:
                        last.then_inc(xproj_full, 1)
                return step

            def dt_proj(j):
                def step(s):
                    pe.wait_ge(xdbl_ready, s + 1)
                    if j >= 2:
                        pe.wait_ge(relu_ready, JT * s + j - 1)
                    nc.tensor.matmul(fp[(1, 0, 1, 0)[j]][:, :], w_dt[:, j * P:(j + 1) * P], x_dbl[0:DTR, :],
                                     start=True, stop=True).then_inc(dt_full, 1)
                return step

            def out_proj(q):
                def step(s):
                    if q == 0:
                        pe.wait_ge(y_gated, JT * (s + 1))
                        pe.wait_ge(res_copied, s + 1)
                        wait(pe, slots_ready, s)
                    o = bp[q // 2][:, (q % 2) * DM:(q % 2 + 1) * DM]
                    for j in range(JT):
                        nc.tensor.matmul(o, yg[:, j, q * P:(q + 1) * P], w_out[:, j, :], start=(j == 0), stop=False)
                    for f in range(FT):
                        last = nc.tensor.matmul(o[:, f * P:(f + 1) * P], h_res[:, f, q * P:(q + 1) * P], ident[:, :],
                                                start=False, stop=(f == FT - 1))
                    if q == TT - 1:
                        last.then_inc(out_full, 1)
                return step

            def turn_n1(s):
                pe.wait_ge(n1_ready, s + 1)
                transposes(norm, bp).then_inc(n1t_full, 1)

            def ffn1(j):
                def step(s):
                    pe.wait_ge(h2_ready, FT * (s + 1))
                    if j >= 2:
                        pe.wait_ge(f1_copied, JT * s + j - 1)
                    for f in range(FT):
                        last = nc.tensor.matmul(bp[j % 2][:, :], w_f1[:, f, j * P:(j + 1) * P], h2_t[:, f, :],
                                                start=(f == 0), stop=(f == FT - 1))
                    last.then_inc(f1_full, 1)
                return step

            def ffn2(q):
                def step(s):
                    if q == 0:
                        pe.wait_ge(f1_ready, s + 1)
                    o = bp[q // 2][:, (q % 2) * DM:(q % 2 + 1) * DM]
                    nc.tensor.matmul(o, ones[0:1, :], f2_b[0:1, :], start=True, stop=False)
                    for j in range(JT):
                        nc.tensor.matmul(o, f1[:, j, q * P:(q + 1) * P], w_f2[:, j, :], start=False, stop=False)
                    for f in range(FT):
                        last = nc.tensor.matmul(o[:, f * P:(f + 1) * P], h2_t[:, f, q * P:(q + 1) * P], ident[:, :],
                                                start=False, stop=(f == FT - 1))
                    if q == TT - 1:
                        last.then_inc(f2_full, 1)
                return step

            def turn_h3(s):
                pe.wait_ge(h3_ready, s + 1)
                transposes(h3, bp).then_inc(h3t_full, 1)

            def gate(s):
                pe.wait_ge(h3t_ready, FT * (s + 1))
                for q in range(TT):
                    o = bp[0][:, q * NE:(q + 1) * NE]
                    nc.tensor.matmul(o, ones[0:1, :], gate_b[0:1, :], start=True, stop=False)
                    for f in range(FT):
                        last = nc.tensor.matmul(o, h2_t[:, f, q * P:(q + 1) * P], w_gate[:, f, :],
                                                start=False, stop=(f == FT - 1))
                last.then_inc(logits_full, 1)

            def rank(s):
                pe.wait_ge(picks_ready, s + 1)
                m = picks[:, :, :].rearrange("p q e -> p (q e)")
                nc.tensor.matmul(bp[1][:, 0:TT * NE], before[:, :], m, start=True, stop=True)
                nc.tensor.matmul(bp[1][:, TT * NE:2 * TT * NE], ones[:, :], m, start=True, stop=True).then_inc(rank_full, 1)

            def state_sum(s, n):
                for k in range(n * SLOT, (n + 1) * SLOT):
                    j, st = divmod(k, DS)
                    if st == 0:
                        wait(pe, y_read, JT * s + j)
                    pe.wait_ge(hc_ready, UNITS * s + k + 1)
                    nc.tensor.matmul(ysum[:, :], ident[:, :], hc[:, k % NHC, :], start=(st == 0),
                                     stop=(st == DS - 1)).then_inc(y_summed, 1)

            def prelude_all():
                prelude()
                pe.wait_ge(mod_copied, 2)

            program(pe, prelude_all,
                    front={12: [turn_x], 14: [x_in(0)], 15: [x_in(1)], 18: [x_in(2)], 19: [x_in(3)],
                           22: [x_proj(0)], 23: [x_proj(1)], 25: [dt_proj(0), dt_proj(1)]},
                    gates={0: [dt_proj(2)], 1: [dt_proj(3)], 2: [z_in(0)], 3: [z_in(1)], 9: [z_in(2)],
                           10: [z_in(3)]},
                    back={4: [out_proj(0)], 5: [out_proj(1)], 6: [out_proj(2)], 7: [out_proj(3)],
                          10: [turn_n1], 12: [ffn1(0)], 13: [ffn1(1)], 14: [ffn1(2)], 15: [ffn1(3)],
                          17: [ffn2(0), ffn2(1)], 19: [ffn2(2)], 20: [ffn2(3)], 30: [turn_h3]},
                    tail={0: [gate], 2: [rank]},
                    scan=state_sum)

        @block.vector
        def _(dve):
            LN = 5 + 3 * NEWTON
            own = Ordered(dve, v_own, 3 * LN)
            own_tail = Ordered(dve, vt_own, 12 + TT)
            own_front = Ordered(dve, vf_own, LN)
            pre = [0]

            def link(ins):
                pre[0] += 1
                ins.then_inc(v0_own, 1)
                dve.wait_ge(v0_own, pre[0])

            def prelude():
                nc.vector.memset(ones[:, :], 1.0)
                nc.vector.memset(zero_bias[:, :], 0.0)
                nc.vector.memset(token_no[:, 1, :], 0.0)
                nc.vector.memset(count[:, :], 0.0).then_inc(consts_set, 1)
                dve.wait_ge(loaded, 16 * NW)
                dve.wait_ge(mod_full, 2)
                for k in range(3):
                    link(nc.vector.tensor_copy(mod8[:, 2 * k:2 * k + 2, :].rearrange("p k n -> p (k n)"), ss[k][0:B, :]))
                nc.vector.tensor_copy(mod_col[:, 0:2, :].rearrange("p k b -> p (k b)"),
                                      ysum[:, 0:2 * B]).then_inc(mod_copied, 1)
                nc.vector.tensor_scalar(mod_col[:, 2:4, :].rearrange("p k b -> p (k b)"), ysum[:, 2 * B:4 * B],
                                        1.0, None, ALU.add).then_inc(mod_copied, 1)
                dve.wait_ge(mod_copied, 2)
                for k, part in enumerate((2, 5)):
                    g = mod8[:, part, :]
                    link(nc.vector.scalar_tensor_tensor(mag8[:, k, :], g, -1.0, g, ALU.mult, ALU.max))
                    link(nc.vector.tensor_scalar(mag8[:, k, :], mag8[:, k, :], 0.25, None, ALU.max))
                    link(nc.vector.tensor_scalar(sgn8[:, k, :], g, 0.0, 2.0, ALU.is_ge, ALU.mult))
                    link(nc.vector.scalar_tensor_tensor(mag8[:, k, :], sgn8[:, k, :], -1.0, mag8[:, k, :],
                                                        ALU.add, ALU.mult))
                link(nc.vector.tensor_tensor(row8[:, 0, :], mag8[:, 0, :], ln2w8, ALU.mult))
                link(nc.vector.tensor_tensor(row8[:, 1, :], mag8[:, 0, :], ln2b8, ALU.mult))
                link(nc.vector.tensor_scalar(row8[:, 2, :], mod8[:, 4, :], 1.0, None, ALU.add))
                link(nc.vector.tensor_copy(row8[:, 3, :], mod8[:, 3, :]))
                nc.vector.tensor_copy(row8[:, 4, :], mag8[:, 1, :]).then_inc(rows_ready, 1)

            def layer_norm(s, o, src, dst, eps, ready, bufs):
                st_, mv_, var_, root_, tmp_ = bufs
                for q in range(TT):
                    last = nc.vector.bn_stats(st_[:, q, :], src(q))
                o.done(last)
                o.settle_apart(s, consts_set)
                for q in range(TT):
                    last = nc.vector.bn_aggr(mv_[:, q, :], st_[:, q, :])
                o.done(last)
                o.settle(s)
                o.done(nc.vector.tensor_scalar(var_[:, :], mv_[:, :, 1], eps, None, ALU.add))
                o.settle(s)
                o.done(nc.vector.tensor_scalar(tmp_[:, :].bitcast(I32), var_[:, :].bitcast(I32), 1, None,
                                               ALU.logical_shift_right))
                o.settle(s)
                o.done(nc.vector.tensor_scalar(root_[:, :].bitcast(I32), tmp_[:, :].bitcast(I32), -1.0, float(ROOT_GUESS),
                                               ALU.mult, ALU.add))
                o.settle(s)
                for _ in range(NEWTON):
                    o.done(nc.vector.scalar_tensor_tensor(tmp_[:, :], root_[:, :], -0.5, root_[:, :], ALU.mult, ALU.mult))
                    o.settle(s)
                    o.done(nc.vector.tensor_tensor(tmp_[:, :], tmp_[:, :], var_[:, :], ALU.mult))
                    o.settle(s)
                    o.done(nc.vector.scalar_tensor_tensor(root_[:, :], tmp_[:, :], 1.5, root_[:, :], ALU.add, ALU.mult))
                    o.settle(s)
                for q in range(TT):
                    last = nc.vector.tensor_scalar(dst(q), src(q), mv_[:, q, 0:1], root_[:, q:q + 1],
                                                   ALU.subtract, ALU.mult)
                last.then_inc(ready, 1)

            back_bufs = (stats, mv, lnv, rstd, tmp)
            front_bufs = (stats0, mv0, lnv0, rstd0, tmp0)

            def norm_x(s):
                dve.wait_ge(x_loaded, 16 * (s + 1))
                layer_norm(s, own_front, lambda q: xrow[:, q, :], lambda q: xrow[:, q, :], LN_EPS_OUT,
                           x_normed, front_bufs)
                wait(dve, h_ready, FT * s)
                nc.vector.tensor_copy(mod_now[:, :], mod_col[:, :, s]).then_inc(mod_copied, 1)
                own_front.finish()

            def conv(j):
                def step(s):
                    dve.wait_ge(tap_last, JT * s + j + 1)
                    for k in range(1, DC):
                        dst = xs[:, s % 2, j, k:L]
                        ins = nc.vector.scalar_tensor_tensor(dst, fp[j % 2][:, 0:L - k], conv_w[:, j, DC - 1 - k:DC - k],
                                                             dst, ALU.mult, ALU.add)
                        if k < DC - 1:
                            ins.then_inc(tap_own, 1)
                            dve.wait_ge(tap_own, (JT * s + j) * (DC - 2) + k)
                        else:
                            ins.then_inc(conv_done, 1)
                return step

            def add_dt(j):
                def step(s):
                    dve.wait_ge(log_ready, JT * s + j + 1)
                    nc.vector.tensor_tensor(dt[:, j, :], dt[:, j, :], relu_dt[:, j % 2, :], ALU.add).then_inc(dt_ready, 1)
                return step

            def read_y(j):
                def step(s):
                    dve.wait_ge(y_summed, UNITS * s + (j + 1) * DS)
                    if j == 0:
                        wait(dve, out_full, s)
                    nc.vector.scalar_tensor_tensor(yg[:, j, :], xs[:, s % 2, j, :], d_skip[:, j:j + 1], ysum[:, :],
                                                   ALU.mult, ALU.add).then_inc(y_read, 1)
                return step

            def half(q):
                return bp[q // 2][:, (q % 2) * DM:(q % 2 + 1) * DM]

            def norm1(s):
                dve.wait_ge(out_full, s + 1)
                wait(dve, h3_ready, s)
                layer_norm(s, own, half, lambda q: norm[:, q, :], LN_EPS_IN, n1_ready, back_bufs)

            def leaky(s):
                dve.wait_ge(f1_copied, JT * (s + 1))
                nc.vector.scalar_tensor_tensor(f1[:, :, :], f1[:, :, :], SLOPE, f1[:, :, :],
                                               ALU.mult, ALU.max).then_inc(f1_ready, 1)

            def norm2(s):
                dve.wait_ge(f2_full, s + 1)
                layer_norm(s, own, half, lambda q: norm[:, q, :], LN_EPS_IN, n2_ready, back_bufs)

            def norm3(s):
                dve.wait_ge(x1_ready, s + 1)
                layer_norm(s, own, lambda q: x1[:, q, :], lambda q: norm[:, q, :], LN_EPS_OUT, n3_ready, back_bufs)
                own.finish()

            def top2(s):
                dve.wait_ge(logits_full, s + 1)
                own_tail.done(nc.vector.tensor_copy(logits[:, :, :].rearrange("p q e -> p (q e)"), bp[0][:, 0:TT * NE]))
                own_tail.settle_apart(s, consts_set)
                for q in range(TT):
                    last = nc.vector.max(top_v[:, q, :], logits[:, q, :])
                own_tail.done(last)
                own_tail.settle_apart(s, consts_set)
                for q in range(TT):
                    last = nc.vector.max_index(top_i[:, q, :], top_v[:, q, :], logits[:, q, :])
                own_tail.done(last)
                own_tail.settle(s)
                own_tail.done(nc.vector.tensor_copy(top_f[:, :, :], top_i[:, :, :]))
                own_tail.settle(s)
                for k, pick in enumerate((pick1, pick2)):
                    own_tail.done(nc.vector.tensor_tensor(pick[:, :, :], e_iota8[:, :].unsqueeze(1).to_broadcast([P, TT, NE]),
                                                     top_f[:, :, k:k + 1].to_broadcast([P, TT, NE]), ALU.is_equal))
                own_tail.settle(s)
                nc.vector.tensor_tensor(picks[:, :, :], pick1[:, :, :], pick2[:, :, :], ALU.add).then_inc(picks_ready, 1)

            def slots(s):
                dve.wait_ge(rank_full, s + 1)
                wait(dve, scattered, 16 * 2 * TT * s)
                in_tile = bp[1][:, 0:TT * NE].rearrange("p (q e) -> p q e", q=TT)
                of_tile = bp[1][:, TT * NE:2 * TT * NE].rearrange("p (q e) -> p q e", q=TT)
                own_tail.done(nc.vector.tensor_tensor(slot_f[:, :, :], in_tile,
                                                 e_base[:, :].unsqueeze(1).to_broadcast([P, TT, NE]), ALU.add))
                own_tail.settle(s)
                for q in range(TT):
                    nc.vector.tensor_tensor(slot_f[:, q, :], slot_f[:, q, :], count[:, :], ALU.add)
                    own_tail.done(nc.vector.tensor_tensor(count[:, :], count[:, :], of_tile[:, q, :], ALU.add))
                    own_tail.settle(s)
                for k, pick in enumerate((pick1, pick2)):
                    own_tail.done(nc.vector.tensor_tensor(prod[:, :, :], slot_f[:, :, :], pick[:, :, :], ALU.mult))
                    own_tail.settle(s)
                    own_tail.done(nc.vector.tensor_reduce(slot_s[:, k, :], prod[:, :, :], AX.X, ALU.add))
                    own_tail.settle(s)
                for k in range(2):
                    nc.vector.tensor_copy(h3[:, :, DM + k].bitcast(U32), token_no[:, k, :])
                own_tail.done(nc.vector.tensor_copy(slot_i[:, :, :], slot_s[:, :, :]))
                own_tail.settle(s)
                nc.vector.tensor_scalar(token_no[:, 0, :], token_no[:, 0, :], float(L), None, ALU.add)
                nc.vector.tensor_scalar(token_no[:, 1, :], token_no[:, 1, :], 1.0, None, ALU.add).then_inc(slots_ready, 1)
                own_tail.finish()

            def recur(k, s):
                dve.wait_ge(exp_done, UNITS * s + k + 1)
                if k % 2 == 0:
                    dve.wait_ge(bx_ready, PAIRS * s + k // 2 + 1)
                bank = ss[k % NSS][:, :]
                nc.vector.tensor_tensor_scan(bank, bank, bx[:, (k // 2) % NBX, k % 2, :], 0.0,
                                             ALU.mult, ALU.add).then_inc(scan_done, 1)

            def times_c(k, s):
                dve.wait_ge(scan_done, UNITS * s + k + 1)
                if k < DS and k % 4 == 0:
                    dve.wait_ge(bc_loaded[k // 4], 32 * (s + 1))
                wait(dve, y_summed, UNITS * s + k + 1 - NHC)
                nc.vector.tensor_tensor(hc[:, k % NHC, :], ss[k % NSS][:, :], c_bc[:, k % DS, :],
                                        ALU.mult).then_inc(hc_ready, 1)

            def scans(s, n):
                if n == 0:
                    recur(0, s)
                for k in range(n * SLOT, (n + 1) * SLOT):
                    if k + 1 < UNITS:
                        recur(k + 1, s)
                    times_c(k, s)

            program(dve, prelude,
                    front={9: [norm_x], 16: [conv(0)], 17: [conv(1)], 19: [conv(2)], 20: [conv(3)],
                           27: [add_dt(0)], 28: [add_dt(1)]},
                    gates={2: [add_dt(2)], 3: [add_dt(3)], 8: [read_y(0)], 16: [read_y(1)], 24: [read_y(2)]},
                    back={1: [read_y(3)], 10: [norm1], 17: [leaky], 22: [norm2], 27: [norm3]},
                    tail={2: [top2], 4: [slots]},
                    scan=scans)


def expert_program(nc, t, d, out, keep):
    ident, zero_bias, e_iota8, e_base, count = (keep[k] for k in ("ident", "zero_bias", "e_iota8", "e_base", "count"))
    RB = ROWS // P
    MT = FF // P
    STEPS = B * L // ROWS
    ctx = ExitStack()
    with ctx:
        def sb(name, shape, dt=F32):
            return ctx.enter_context(nc.sbuf_tensor(name, shape, dt))

        def ps(name):
            return ctx.enter_context(nc.psum_tensor(name, [P, 512], F32))

        def sem(name):
            return ctx.enter_context(nc.semaphore(name))

        steps = sb("steps", [1, STEPS])
        tile_no = sb("tile_no", [1, NTILE])
        more = sb("more", [1, NE, STEPS])
        tiles = sb("tiles", [1, NE])
        t_end = sb("t_end", [1, NE])
        t_start = sb("t_start", [1, NE])
        one8 = sb("one8", [1, NE])
        origin = sb("origin", [1, NE])
        owned = sb("owned", [1, NTILE, NE])
        under = sb("under", [1, NTILE, NE])
        row_f = sb("row_f", [1, 3, NTILE])
        tab_f = sb("tab_f", [1, 2 * NTILE + NE])
        tab = sb("tab", [1, 2 * NTILE + NE], I32)
        w1_all = sb("w1_all", [P, NE, FT * FF])
        w2_all = sb("w2_all", [P, NE, MT * DM])
        b1_all = sb("b1_all", [P, NE, MT])
        b2_all = sb("b2_all", [P, NE, DM])
        rows = [sb(f"rows{i}", [P, RB, RW]) for i in range(2)]
        w1 = [sb(f"w1_{i}", [P, FT, FF]) for i in range(2)]
        w2 = [sb(f"w2_{i}", [P, MT, DM]) for i in range(2)]
        b1 = [sb(f"b1_{i}", [P, MT]) for i in range(2)]
        rows_t = [sb(f"rows_t{i}", [P, FT, ROWS]) for i in range(2)]
        tokens = [sb(f"tokens{i}", [P, RB, 2], U32) for i in range(2)]
        gates = [sb(f"gates{i}", [P, RB, DM]) for i in range(2)]
        hidden = [sb(f"hidden{i}", [P, MT, ROWS]) for i in range(2)]
        pads = hidden[0][:, :, :].rearrange("p m n -> p (m n)")[:, 0:RB * RW].rearrange("p (k n) -> p k n", k=RB)
        result = [sb(f"result{i}", [P, RB, DM]) for i in range(2)]
        up = [ps(f"up{i}") for i in range(4)]
        turn = [ps(f"turn{i}") for i in range(2)]
        down = [ps(f"down{i}") for i in range(2)]

        consts_in = sem("consts_in")
        tab_own = sem("tab_own")
        tab_ready = sem("tab_ready")
        padded = sem("padded")
        expert_in = [sem(f"expert_in{e}") for e in range(NE)]
        experts_ready = sem("experts_ready")
        rows_in = [sem(f"rows_in{i}") for i in range(2)]
        w1_ready = sem("w1_ready")
        w2_ready = sem("w2_ready")
        turned = sem("turned")
        rows_t_ready = sem("rows_t_ready")
        gates_in = [sem(f"gates_in{i}") for i in range(2)]
        up_full = sem("up_full")
        hidden_ready = sem("hidden_ready")
        down_full = sem("down_full")
        biased = sem("biased")
        result_ready = sem("result_ready")
        added = sem("added")

        block = ctx.enter_context(nc.Block())
        PAIRS_OF_TILES = NTILE // 2
        assert NTILE % 2 == 1

        def tile_loop(engine, step):
            step(0, 0, 0)
            step(1, 1, 0)
            with engine.Fori(0, PAIRS_OF_TILES - 1) as i:
                step(2 * i + 2, 0, i + 1)
                step(2 * i + 3, 1, i + 1)
            step(NTILE - 1, 0, PAIRS_OF_TILES)

        def expert_of(engine, j):
            return engine.value_load(tab[0:1, bass.ds(j + NTILE, 1)], min_val=0, max_val=NE - 1)

        @block.sync
        def _(sp):
            def load_expert(e):
                for dst, src in (
                    (w1_all[:, e, :].rearrange("p (k n) -> p k n", k=FT), t["w1"][e, :, :].rearrange("(k p) n -> p k n", p=P)),
                    (b1_all[:, e, :], t["b1"][e, :, :]),
                    (w2_all[:, e, :].rearrange("p (k n) -> p k n", k=MT), t["w2"][e, :, :].rearrange("(k p) n -> p k n", p=P)),
                    (b2_all[:, e, :], t["b2"][e:e + 1, :].to_broadcast([P, DM])),
                ):
                    sp.dma_start(dst, src).then_inc(expert_in[e], 16)

            sp.dma_start(steps[:, :], t["steps"]).then_inc(consts_in, 16)
            sp.dma_start(tile_no[:, :], t["tile_no"]).then_inc(consts_in, 16)
            sp.dma_start(pads, d["pads"]).then_inc(consts_in, 16)
            sp.wait_ge(consts_in, 48)
            load_expert(0)
            sp.wait_ge(tab_ready, 1)
            for e in range(NE):
                end = sp.value_load(tab[0:1, 2 * NTILE + e:2 * NTILE + e + 1], min_val=0, max_val=NE * CAP - ROWS)
                sp.dma_start(d["region"][bass.ds(end, ROWS), :].rearrange("(k p) n -> p k n", p=P),
                             pads).then_inc(padded, 16)
            for e in range(NE):
                if e + 1 < NE:
                    load_expert(e + 1)
                sp.wait_ge(expert_in[e], 64)
                sp.sem_inc(experts_ready, 1)

        @block.gpsimd
        def _(pool):
            pool.wait_ge(tab_ready, 1)
            pool.wait_ge(padded, 16 * NE)

            def load_rows(j, par):
                row = pool.value_load(tab[0:1, bass.ds(j, 1)], min_val=0, max_val=IDLE_ROW)
                wait_apart(pool, rows_t_ready, j - 1, tab_ready)
                nc.gpsimd.dma_start(rows[par][:, :, :],
                                    d["region"][bass.ds(row, ROWS), :].rearrange("(k p) n -> p k n", p=P)).then_inc(rows_in[par], 16)

            def load_gates(j, par):
                if not isinstance(j, int) or j > 1:
                    wait_apart(pool, result_ready, j - 1, tab_ready)
                for k in range(RB):
                    wait_apart(pool, rows_t_ready, j + 1, tab_ready)
                    nc.gpsimd.indirect_dma_start(
                        gates[par][:, k, :], None, d["gate_rows"],
                        bass.IndirectOffsetOnAxis(tokens[par][:, k, 1:2], 0)).then_inc(gates_in[par], 16)

            def add_rows(j, par):
                pool.wait_ge(result_ready, j + 1)
                for k in range(RB):
                    wait_apart(pool, added, RB * 16 * j + 16 * k, tab_ready)
                    nc.gpsimd.indirect_dma_start(
                        d["out_rows"], bass.IndirectOffsetOnAxis(tokens[par][:, k, 0:1], 0),
                        result[par][:, k, :], None, compute_op=ALU.add).then_inc(added, 16)

            load_rows(0, 0)
            load_rows(1, 1)
            load_gates(0, 0)
            load_rows(2, 0)
            load_gates(1, 1)
            add_rows(0, 0)
            with pool.Fori(0, PAIRS_OF_TILES - 1) as i:
                load_rows(2 * i + 3, 1)
                load_gates(2 * i + 2, 0)
                add_rows(2 * i + 1, 1)
                load_rows(2 * i + 4, 0)
                load_gates(2 * i + 3, 1)
                add_rows(2 * i + 2, 0)
            load_gates(NTILE - 1, 0)
            add_rows(NTILE - 2, 1)
            add_rows(NTILE - 1, 0)
            pool.wait_ge(added, RB * 16 * NTILE)

        @block.scalar
        def _(act):
            act.wait_ge(tab_ready, 1)

            def copy_w2(j, par, i):
                e = expert_of(act, j)
                act.wait_ge(experts_ready, e + 1)
                wait_apart(act, down_full, j - 1, tab_ready)
                nc.scalar.activation(w2[par][:, :, :].rearrange("p m n -> p (m n)"),
                                     w2_all[:, bass.ds(e, 1), :].rearrange("p o n -> p (o n)"), ACT.Identity,
                                     bias=zero_bias[:, 0:1]).then_inc(w2_ready, 1)

            def relu(j, par, i):
                act.wait_ge(w1_ready, j + 1)
                if not isinstance(j, int) or j > 1:
                    act.wait_ge(down_full, j - 1)
                for c in range(4):
                    act.wait_ge(up_full, 4 * j + c + 1)
                    for m in (2 * c, 2 * c + 1):
                        last = nc.scalar.activation(hidden[par][:, m, :], up[c][:, (m % 2) * ROWS:(m % 2 + 1) * ROWS],
                                                    ACT.Relu, bias=b1[par][:, m:m + 1])
                    last.then_inc(hidden_ready, 1)

            def tile(j, par, i):
                copy_w2(j, par, i)
                relu(j, par, i)

            tile_loop(act, tile)

        @block.tensor
        def _(pe):
            def turn_rows(j, par, i):
                pe.wait_ge(rows_in[par], 16 * (i + 1))
                wait(pe, rows_t_ready, j - 1)
                for f in range(FT):
                    for k in range(RB):
                        last = nc.tensor.transpose(turn[par][:, f * ROWS + k * P:f * ROWS + (k + 1) * P],
                                                   rows[par][:, k, f * P:(f + 1) * P], ident[:, :])
                last.then_inc(turned, 1)

            def up_product(j, par, i):
                pe.wait_ge(rows_t_ready, j + 1)
                pe.wait_ge(w1_ready, j + 1)
                for c in range(4):
                    wait(pe, hidden_ready, 4 * j - 4 + c + 1)
                    for m in (2 * c, 2 * c + 1):
                        for f in range(FT):
                            last = nc.tensor.matmul(up[c][:, (m % 2) * ROWS:(m % 2 + 1) * ROWS],
                                                    w1[par][:, f, m * P:(m + 1) * P], rows_t[par][:, f, :],
                                                    start=(f == 0), stop=(f == FT - 1))
                    last.then_inc(up_full, 1)

            def down_product(j, par, i):
                pe.wait_ge(w2_ready, j + 1)
                wait(pe, result_ready, j - 1)
                for k in range(RB):
                    for m in range(MT):
                        if k == 0 and m % 2 == 0:
                            pe.wait_ge(hidden_ready, 4 * j + m // 2 + 1)
                        last = nc.tensor.matmul(down[par][:, k * DM:(k + 1) * DM], hidden[par][:, m, k * P:(k + 1) * P],
                                                w2[par][:, m, :], start=(m == 0), stop=(m == MT - 1))
                last.then_inc(down_full, 1)

            def pair(i, following=True):
                up_product(2 * i, 0, i)
                turn_rows(2 * i + 1, 1, i)
                down_product(2 * i, 0, i)
                up_product(2 * i + 1, 1, i)
                turn_rows(2 * i + 2, 0, i + 1)
                down_product(2 * i + 1, 1, i)

            turn_rows(0, 0, 0)
            pair(0)
            with pe.Fori(0, PAIRS_OF_TILES - 1) as i:
                pair(i + 1)
            up_product(NTILE - 1, 0, PAIRS_OF_TILES)
            down_product(NTILE - 1, 0, PAIRS_OF_TILES)

        @block.vector
        def _(dve):
            n = [0]

            def link(ins):
                n[0] += 1
                ins.then_inc(tab_own, 1)
                dve.wait_ge(tab_own, n[0])

            dve.wait_ge(consts_in, 48)
            nc.vector.memset(one8[:, :], 1.0)
            link(nc.vector.tensor_tensor(more[:, :, :], count[0:1, :].unsqueeze(2).to_broadcast([1, NE, STEPS]),
                                         steps[:, :].unsqueeze(1).to_broadcast([1, NE, STEPS]), ALU.is_gt))
            link(nc.vector.tensor_reduce(tiles[:, :], more[:, :, :], AX.X, ALU.add))
            link(nc.vector.tensor_tensor_scan(t_end[:, :], one8[:, :], tiles[:, :], 0.0, ALU.mult, ALU.add))
            link(nc.vector.tensor_tensor(t_start[:, :], t_end[:, :], tiles[:, :], ALU.subtract))
            link(nc.vector.scalar_tensor_tensor(origin[:, :], t_start[:, :], -float(ROWS), e_base[0:1, :],
                                                ALU.mult, ALU.add))
            tile_b = tile_no[:, :].unsqueeze(2).to_broadcast([1, NTILE, NE])

            def per_tile(x):
                return x.unsqueeze(1).to_broadcast([1, NTILE, NE])

            link(nc.vector.tensor_tensor(owned[:, :, :], tile_b, per_tile(t_start[:, :]), ALU.is_ge))
            link(nc.vector.tensor_tensor(under[:, :, :], tile_b, per_tile(t_end[:, :]), ALU.is_lt))
            link(nc.vector.tensor_tensor(owned[:, :, :], owned[:, :, :], under[:, :, :], ALU.mult))
            link(nc.vector.tensor_reduce(row_f[:, 0, :], owned[:, :, :], AX.X, ALU.add))
            link(nc.vector.tensor_tensor(under[:, :, :], owned[:, :, :], per_tile(origin[:, :]), ALU.mult))
            link(nc.vector.tensor_reduce(row_f[:, 1, :], under[:, :, :], AX.X, ALU.add))
            link(nc.vector.tensor_tensor(under[:, :, :], owned[:, :, :], per_tile(e_iota8[0:1, :]), ALU.mult))
            link(nc.vector.tensor_reduce(tab_f[:, NTILE:2 * NTILE], under[:, :, :], AX.X, ALU.add))
            link(nc.vector.tensor_scalar(row_f[:, 2, :], tile_no[:, :], float(ROWS), -float(IDLE_ROW),
                                         ALU.mult, ALU.add))
            link(nc.vector.tensor_tensor(row_f[:, 2, :], row_f[:, 2, :], row_f[:, 0, :], ALU.mult))
            link(nc.vector.scalar_tensor_tensor(tab_f[:, 0:NTILE], row_f[:, 2, :], float(IDLE_ROW), row_f[:, 1, :],
                                                ALU.add, ALU.add))
            link(nc.vector.tensor_tensor(tab_f[:, 2 * NTILE:], e_base[0:1, :], count[0:1, :], ALU.add))
            nc.vector.tensor_copy(tab[:, :], tab_f[:, :]).then_inc(tab_ready, 1)

            dve.wait_ge(tab_ready, 1)

            def copy_rows(j, par, i):
                dve.wait_ge(turned, j + 1)
                wait(dve, up_full, 4 * (j - 1))
                nc.vector.tensor_copy(rows_t[par][:, :, :].rearrange("p f n -> p (f n)"), turn[par][:, :])
                wait(dve, added, RB * 16 * (j - 1))
                nc.vector.tensor_copy(tokens[par][:, :, :], rows[par][:, :, DM:RW].bitcast(U32)).then_inc(rows_t_ready, 1)

            def copy_w1(j, par, i):
                e = expert_of(dve, j)
                dve.wait_ge(experts_ready, e + 1)
                wait_apart(dve, hidden_ready, 4 * (j - 1), tab_ready)
                nc.vector.tensor_copy(b1[par][:, :], b1_all[:, bass.ds(e, 1), :].rearrange("p o n -> p (o n)"))
                nc.vector.tensor_copy(w1[par][:, :, :].rearrange("p m n -> p (m n)"),
                                      w1_all[:, bass.ds(e, 1), :].rearrange("p o n -> p (o n)")).then_inc(w1_ready, 1)

            def finish_rows(j, par, i):
                e = expert_of(dve, j)
                dve.wait_ge(down_full, j + 1)
                wait(dve, added, RB * 16 * (j - 1))
                nc.vector.tensor_tensor(result[par][:, :, :], down[par][:, :].rearrange("p (k n) -> p k n", k=RB),
                                        b2_all[:, bass.ds(e, 1), :].to_broadcast([P, RB, DM]), ALU.add).then_inc(biased, 1)
                dve.wait_ge(gates_in[par], 16 * RB * (i + 1))
                dve.wait_ge(biased, j + 1)
                nc.vector.tensor_tensor(result[par][:, :, :], result[par][:, :, :], gates[par][:, :, :],
                                        ALU.mult).then_inc(result_ready, 1)

            def prepare(j, par, i):
                copy_rows(j, par, i)
                copy_w1(j, par, i)

            def pair(i):
                prepare(2 * i + 1, 1, i)
                finish_rows(2 * i, 0, i)
                prepare(2 * i + 2, 0, i + 1)
                finish_rows(2 * i + 1, 1, i)

            prepare(0, 0, 0)
            pair(0)
            with dve.Fori(0, PAIRS_OF_TILES - 1) as i:
                pair(i + 1)
            finish_rows(NTILE - 1, 0, PAIRS_OF_TILES)


def build(nc, t, out):
    d = {
        "mod_rows": nc.dram_tensor("mod_rows", (B, 4, DM), F32).ap(),
        "gate_rows": nc.dram_tensor("gate_rows", (B + 1, DM), F32).ap(),
        "bc": nc.dram_tensor("bc", (2 * DS, L), F32).ap(),
        "region": nc.dram_tensor("region", (IDLE_ROW + ROWS, RW), F32).ap(),
        "pads": nc.dram_tensor("pad_tile", (P, 2, RW), F32).ap(),
        "out_rows": out.rearrange("s l n -> (s l) n"),
    }
    with ExitStack() as ctx:
        keep = {name: ctx.enter_context(nc.sbuf_tensor(name, [P, n], F32)) for name, n in
                (("ident", P), ("ones", P), ("zero_bias", 1), ("e_iota8", NE), ("e_base", NE), ("count", NE))}
        scan_program(nc, t, d, out, keep)
        expert_program(nc, t, d, out, keep)


def kernel(**inputs):
    import numpy as np
    import concourse.bacc as bacc
    from concourse.bass_utils import run_bass_kernel_spmd

    a = {k: np.asarray(v) for k, v in inputs.items()}
    m = {k[len("L0_attn_"):]: v for k, v in a.items() if k.startswith("L0_attn_")}
    f = {k[len("L0_ffn_"):]: v for k, v in a.items() if k.startswith("L0_ffn_")}
    q = np.arange(P)
    arrays = {
        "x": m["x"], "cond_t": a["L0_c"].T, "wmod": a["L0_wmod"],
        "in_proj_t": m["in_proj_w"].T, "conv_w": m["conv_w"], "conv_b": m["conv_b"].reshape(JT, P).T,
        "x_proj_t": m["x_proj_w"].T, "dt_proj_t": m["dt_proj_w"].T, "dt_b": m["dt_proj_b"].reshape(JT, P).T,
        "A_log": m["A_log"], "D": m["D"].reshape(JT, P).T, "out_proj_t": m["out_proj_w"].T,
        "ln1_w": m["ln1_w"].reshape(FT, P).T, "ln1_b": m["ln1_b"].reshape(FT, P).T,
        "ffn_w1_t": m["ffn_w1"].T, "ffn_b1": m["ffn_b1"].reshape(JT, P).T, "ffn_w2_t": m["ffn_w2"].T,
        "ffn_b2": m["ffn_b2"].reshape(1, DM), "ln2_w": m["ln2_w"].reshape(1, DM), "ln2_b": m["ln2_b"].reshape(1, DM),
        "gate_w": f["gate_w"], "gate_b": f["gate_b"].reshape(1, NE), "w1": f["w1"],
        "b1": f["b1"].reshape(NE, FF // P, P).transpose(0, 2, 1), "w2": f["w2"], "b2": f["b2"],
        "ident": np.eye(P, dtype=np.float32), "before": (q[:, None] < q[None, :]).astype(np.float32),
        "e_iota": np.arange(NE, dtype=np.float32).reshape(1, NE),
        "e_base": (np.arange(NE) * CAP).astype(np.float32).reshape(1, NE),
        "token_no": np.arange(L, dtype=np.float32).reshape(TT, P).T,
        "steps": (np.arange(B * L // ROWS) * ROWS).astype(np.float32).reshape(1, -1),
        "tile_no": np.arange(NTILE, dtype=np.float32).reshape(1, NTILE),
    }
    arrays = {k: np.ascontiguousarray(v) for k, v in arrays.items()}
    nc = bacc.Bacc("TRN2", target_bir_lowering=False, num_devices=1)
    t = {k: nc.dram_tensor(f"in_{k}", v.shape, mybir.dt.from_np(v.dtype), kind="ExternalInput").ap()
         for k, v in arrays.items()}
    out = nc.dram_tensor("out", (B, L, DM), F32, kind="ExternalOutput").ap()
    build(nc, t, out)
    r = run_bass_kernel_spmd(nc, [{f"in_{k}": v for k, v in arrays.items()}], core_ids=[0])
    return r.results[0]["out"]
```

```python
import concourse.bass as bass
from concourse import mybir
from contextlib import ExitStack

B, L, DM = 8, 512, 256
DI, DS, DC, DTR = 512, 16, 4, 16
NE, FF = 8, 1024
P = 128
TT = L // P
FT = DM // P
JT = DI // P
UNITS = JT * DS
PAIRS = UNITS // 2
NBX = 3
NHC = 6
NSS = 3
ROWS = 128
CAP = B * L + ROWS
NTILE = (2 * B * L + NE * (ROWS - 1)) // ROWS
IDLE_ROW = NE * CAP
RW = DM + 2
LN_EPS_OUT, LN_EPS_IN = 1e-5, 1e-12
SLOPE = 0.01
ROOT_GUESS = 0x5F3759DF
NEWTON = 3

F32 = mybir.dt.float32
U32 = mybir.dt.uint32
I32 = mybir.dt.int32
ALU = mybir.AluOpType
ACT = mybir.ActivationFunctionType
AX = mybir.AxisListType


def wait(engine, sem, value):
    if isinstance(value, int) and value <= 0:
        return
    engine.wait_ge(sem, value)


def wait_apart(engine, sem, value, long_done):
    if not isinstance(value, int):
        value = engine.to_reg(value)
    engine.wait_ge(long_done, 1)
    wait(engine, sem, value)


def used_before(k, ring, total):
    return k - ring if k >= ring else (total - 1 - k) // ring * ring + k - total


class Ordered:

    def __init__(self, engine, sem, n):
        self.engine, self.sem, self.n, self.at = engine, sem, n, 0

    def done(self, ins):
        self.at += 1
        ins.then_inc(self.sem, 1)

    def settle(self, seq):
        wait(self.engine, self.sem, seq * self.n + self.at)

    def settle_apart(self, seq, long_done):
        wait_apart(self.engine, self.sem, seq * self.n + self.at, long_done)

    def finish(self):
        assert self.at == self.n, (self.at, self.n)
        self.at = 0


def scan_program(nc, t, d, out, keep, expert_in, done):
    ident, ones, zero_bias, e_iota8, e_base, count = (
        keep[k] for k in ("ident", "ones", "zero_bias", "e_iota8", "e_base", "count"))
    ctx = ExitStack()
    with ctx:
        def sb(name, shape, dt=F32):
            return ctx.enter_context(nc.sbuf_tensor(name, shape, dt))

        def sem(name):
            return ctx.enter_context(nc.semaphore(name))

        w_in = sb("w_in", [P, FT, 2 * DI])
        w_x = sb("w_x", [P, JT, DTR + 2 * DS])
        w_dt = sb("w_dt", [DTR, DI])
        w_out = sb("w_out", [P, JT, DM])
        w_f1 = sb("w_f1", [P, FT, 2 * DM])
        w_f2 = sb("w_f2", [P, JT, DM])
        w_gate = sb("w_gate", [P, FT, NE])
        gate_b = sb("gate_b", [P, NE])
        conv_w = sb("conv_w", [P, JT, DC])
        conv_b = sb("conv_b", [P, JT])
        dt_b = sb("dt_b", [P, JT])
        d_skip = sb("d_skip", [P, JT])
        f1_b = sb("f1_b", [P, JT])
        ln1_w = sb("ln1_w", [P, FT])
        ln1_b = sb("ln1_b", [P, FT])
        a_neg = sb("a_neg", [P, JT, DS])
        f2_b = sb("f2_b", [1, DM])
        before = sb("before", [P, P])
        token_no = sb("token_no", [P, 2, TT])
        mod_col = sb("mod_col", [P, 4, B])
        mod_now = sb("mod_now", [P, 4])
        h_t = sb("h_t", [P, FT, L])
        h_res = sb("h_res", [P, FT, L])
        xs = sb("xs", [P, 2, JT, L])
        zs = sb("zs", [P, JT, L])
        x_dbl = sb("x_dbl", [DTR + 2 * DS, L])
        relu_dt = sb("relu_dt", [P, 2, L])
        dt = sb("dt", [P, JT, L])
        u = sb("u", [P, JT, L])
        b_bc, c_bc = (keep["wide"][:, k * DS * L:(k + 1) * DS * L].rearrange("p (n l) -> p n l", n=DS) for k in range(2))
        bx = sb("bx", [P, NBX, 2, L])
        hc = sb("hc", [P, NHC, L])
        yg = sb("yg", [P, JT, L])
        norm = sb("norm", [P, TT, DM])
        h2_t = sb("h2_t", [P, FT, L])
        f1 = sb("f1", [P, JT, L])
        xrow = f1[:, :, :].rearrange("p j l -> p (j l)")[:, 0:TT * DM].rearrange("p (q n) -> p q n", q=TT)
        mod_row = sb("mod_row", [P, 4, DM])
        x1 = sb("x1", [P, TT, DM])
        h3 = sb("h3", [P, TT, RW])
        stats = sb("stats", [P, TT, 6])
        mv = sb("mv", [P, TT, 2])
        lnv = sb("lnv", [P, TT])
        rstd = sb("rstd", [P, TT])
        tmp = sb("tmp", [P, TT])
        stats0 = sb("stats0", [P, TT, 6])
        mv0 = sb("mv0", [P, TT, 2])
        lnv0 = sb("lnv0", [P, TT])
        rstd0 = sb("rstd0", [P, TT])
        tmp0 = sb("tmp0", [P, TT])
        logits = sb("logits", [P, TT, NE])
        top_v = sb("top_v", [P, TT, 8])
        top_i = sb("top_i", [P, TT, 8], U32)
        top_f = sb("top_f", [P, TT, 8])
        pick1 = sb("pick1", [P, TT, NE])
        pick2 = sb("pick2", [P, TT, NE])
        picks = sb("picks", [P, TT, NE])
        ranks = sb("ranks", [P, 2, TT, NE])
        slot_f = sb("slot_f", [P, TT, NE])
        prod = sb("prod", [P, 2, TT, NE])
        slot_s = sb("slot_s", [P, 2, TT])
        slot_i = sb("slot_i", [P, 2, TT], U32)
        flat_b = b_bc[:, :, :].rearrange("p n l -> p (n l)")
        w_mod = flat_b[:, 0:FT * 6 * DM].rearrange("p (k n) -> p k n", k=FT)
        cond_t = flat_b[:, 3072:3072 + FT * B].rearrange("p (k b) -> p k b", k=FT)
        mod8 = flat_b[0:B, 3328:3328 + 6 * DM].rearrange("p (k n) -> p k n", k=6)
        row8 = flat_b[0:B, 4864:4864 + 5 * DM].rearrange("p (k n) -> p k n", k=5)
        ln2w8 = flat_b[0:B, 6144:6144 + DM]
        ln2b8 = flat_b[0:B, 6400:6400 + DM]
        mag8 = flat_b[0:B, 6656:6656 + 2 * DM].rearrange("p (k n) -> p k n", k=2)
        sgn8 = flat_b[0:B, 7168:7168 + 2 * DM].rearrange("p (k n) -> p k n", k=2)
        flat_c = c_bc[:, :, :].rearrange("p n l -> p (n l)")
        pad_rows = flat_c[:, 0:ROWS // P * RW].rearrange("p (k n) -> p k n", k=ROWS // P)
        pad_no = flat_c[:, 1024:1026]

        ss = [ctx.enter_context(nc.psum_tensor(f"ss{i}", [P, L], F32)) for i in range(NSS)]
        ysum = ctx.enter_context(nc.psum_tensor("ysum", [P, L], F32))
        fp = [ctx.enter_context(nc.psum_tensor(f"fp{i}", [P, L], F32)) for i in range(2)]
        bp = [ctx.enter_context(nc.psum_tensor(f"bp{i}", [P, L], F32)) for i in range(2)]

        loaded = sem("loaded")
        rows_stored = sem("rows_stored")
        inits_stored = sem("inits_stored")
        x_loaded = sem("x_loaded")
        res_loaded = sem("res_loaded")
        bc_stored = sem("bc_stored")
        bc_loaded = [sem(f"bc_loaded{g}") for g in range(4)]
        x1_stored = sem("x1_stored")
        scattered = sem("scattered")
        consts_set = sem("consts_set")
        pool_set = sem("pool_set")
        cond_silu = sem("cond_silu")
        mod_in = sem("mod_in")
        mod_full = sem("mod_full")
        mod_copied = sem("mod_copied")
        a_ready = sem("a_ready")
        rows_ready = sem("rows_ready")
        x_normed = sem("x_normed")
        xt_full = sem("xt_full")
        h_ready = sem("h_ready")
        xin_full = sem("xin_full")
        tap_last = sem("tap_last")
        conv_done = sem("conv_done")
        xs_ready = sem("xs_ready")
        zin_full = sem("zin_full")
        z_copied = sem("z_copied")
        z_ready = sem("z_ready")
        xproj_full = sem("xproj_full")
        xdbl_ready = sem("xdbl_ready")
        dt_full = sem("dt_full")
        log_ready = sem("log_ready")
        relu_ready = sem("relu_ready")
        dt_ready = sem("dt_ready")
        u_ready = sem("u_ready")
        exp_done = sem("exp_done")
        bx_ready = sem("bx_ready")
        scan_done = sem("scan_done")
        hc_ready = sem("hc_ready")
        y_summed = sem("y_summed")
        y_read = sem("y_read")
        y_gated = sem("y_gated")
        out_full = sem("out_full")
        res_copied = sem("res_copied")
        n1_ready = sem("n1_ready")
        n1t_full = sem("n1t_full")
        h2_ready = sem("h2_ready")
        f1_full = sem("f1_full")
        f1_copied = sem("f1_copied")
        f1_ready = sem("f1_ready")
        f2_full = sem("f2_full")
        n2_ready = sem("n2_ready")
        x1_ready = sem("x1_ready")
        n3_ready = sem("n3_ready")
        h3_ready = sem("h3_ready")
        h3t_full = sem("h3t_full")
        h3t_ready = sem("h3t_ready")
        logits_full = sem("logits_full")
        picks_ready = sem("picks_ready")
        rank_full = sem("rank_full")
        ranks_taken = sem("ranks_taken")
        slots_ready = sem("slots_ready")
        v_own = sem("v_own")
        vf_own = sem("vf_own")
        p_own = sem("p_own")
        a_own = sem("a_own")
        v0_own = sem("v0_own")
        vt_own = sem("vt_own")
        ends_ready = sem("ends_ready")
        tab_own = sem("tab_own")
        tab_ready, padded = done["tab_ready"], done["padded"]
        pp_own = sem("pp_own")
        tap_own = sem("tap_own")

        NW = 26

        block = ctx.enter_context(nc.Block())

        def first_only(step):
            return lambda s: step() if isinstance(s, int) and s == 0 else None

        def program(engine, prelude, front, gates, back, tail, scan, places=UNITS, scans_over=lambda: None):
            def slots(f, g, k, s, e):
                for n in range(places):
                    if s is not None:
                        scan(s, n)
                    for table, seq in ((gates, g), (tail, e), (back, k), (front, f)):
                        if seq is not None:
                            for step in table.get(n, ()):
                                step(seq)
            prelude()
            slots(0, None, None, None, None)
            slots(1, 0, None, 0, None)
            slots(2, 1, 0, 1, None)
            slots(3, 2, 1, 2, 0)
            with engine.Fori(0, B - 4) as i:
                slots(i + 4, i + 3, i + 2, i + 3, i + 1)
            slots(None, B - 1, B - 2, B - 1, B - 3)
            scans_over()
            slots(None, None, B - 1, None, B - 2)
            slots(None, None, None, None, B - 1)

        @block.sync
        def _(sp):
            def load_x(s):
                wait(sp, f2_full, 2 * (s - 2))
                if isinstance(s, int) and s < 2:
                    wait(sp, xt_full, s)
                sp.dma_start(xrow[:, :, :], t["x"][s, :, :].rearrange("(k p) n -> p k n", p=P)).then_inc(x_loaded, 16)

            def next_x(s):
                if not (isinstance(s, int) and s == 0):
                    load_x(s)

            def prelude():
                sp.dma_start(cond_t, t["cond_t"].rearrange("(k p) b -> p k b", p=P)).then_inc(mod_in, 16)
                sp.dma_start(w_mod, t["wmod"].rearrange("(k p) n -> p k n", p=P)).then_inc(mod_in, 16)
                load_x(0)
                for dst, src in (
                    (ident[:, :], t["ident"]),
                    (w_in[:, :, :], t["in_proj_t"].rearrange("(k p) n -> p k n", p=P)),
                    (conv_w[:, :, :], t["conv_w"].rearrange("(j p) k -> p j k", p=P)),
                    (conv_b[:, :], t["conv_b"]),
                    (w_x[:, :, :], t["x_proj_t"].rearrange("(k p) n -> p k n", p=P)),
                    (w_dt[:, :], t["dt_proj_t"]),
                    (dt_b[:, :], t["dt_b"]),
                    (a_neg[:, :, :], t["A_log"].rearrange("(j p) n -> p j n", p=P)),
                    (d_skip[:, :], t["D"]),
                    (w_out[:, :, :], t["out_proj_t"].rearrange("(k p) n -> p k n", p=P)),
                    (w_f1[:, :, :], t["ffn_w1_t"].rearrange("(k p) n -> p k n", p=P)),
                    (w_f2[:, :, :], t["ffn_w2_t"].rearrange("(k p) n -> p k n", p=P)),
                    (w_gate[:, :, :], t["gate_w"].rearrange("(k p) n -> p k n", p=P)),
                    (f1_b[:, :], t["ffn_b1"]),
                    (ln1_w[:, :], t["ln1_w"]),
                    (ln1_b[:, :], t["ln1_b"]),
                    (f2_b[:, :], t["ffn_b2"]),
                    (gate_b[:, :], t["gate_b"].to_broadcast([P, NE])),
                    (ln2w8, t["ln2_w"].to_broadcast([B, DM])),
                    (ln2b8, t["ln2_b"].to_broadcast([B, DM])),
                    (before[:, :], t["before"]),
                    (e_base[:, :], t["e_base"].to_broadcast([P, NE])),
                    (e_iota8[:, :], t["e_iota"].to_broadcast([P, NE])),
                    (token_no[:, 0, :], t["token_no"]),
                    (keep["steps"][:, :], t["steps"]),
                    (keep["tile_no"][:, :], t["tile_no"]),
                ):
                    sp.dma_start(dst, src).then_inc(loaded, 16)

            def store_rows():
                sp.wait_ge(rows_ready, 1)
                sp.dma_start(d["mod_rows"], row8[:, 0:4, :]).then_inc(rows_stored, 16)
                sp.dma_start(d["gate_rows"][0:B, :], row8[:, 4, :]).then_inc(rows_stored, 16)
                sp.wait_ge(pool_set, 1)
                sp.dma_start(d["gate_rows"][B:B + 1, :], pad_rows[0:1, 0, 0:DM]).then_inc(rows_stored, 16)
                sp.wait_ge(rows_stored, 48)
                sp.dma_start(d["region"][IDLE_ROW:IDLE_ROW + ROWS, :].rearrange("(k p) n -> p k n", p=P),
                             pad_rows).then_inc(inits_stored, 16)
                sp.dma_start(d["pads"], pad_rows).then_inc(inits_stored, 16)
                sp.wait_ge(inits_stored, 32)

            def store_bc(s):
                sp.wait_ge(xdbl_ready, s + 1)
                sp.dma_start(d["bc"], x_dbl[DTR:DTR + 2 * DS, :]).then_inc(bc_stored, 16)
                sp.wait_ge(bc_stored, 16 * (s + 1))

            def load_bc(g):
                def step(s):
                    wait(sp, hc_ready, s * UNITS - (UNITS - (JT - 1) * DS - 4 * (g + 1)))
                    n = slice(4 * g, 4 * g + 4)
                    for dst, at in ((b_bc, 0), (c_bc, DS)):
                        src = d["bc"][at + 4 * g:at + 4 * g + 4, :].unsqueeze(0).to_broadcast([P, 4, L])
                        sp.dma_start(dst[:, n, :], src).then_inc(bc_loaded[g], 16)
                return step

            def load_res(s):
                wait(sp, x1_stored, 16 * s)
                wait(sp, n3_ready, s)
                wait(sp, h3_ready, s)
                sp.dma_start(x1[:, :, :], t["x"][s, :, :].rearrange("(k p) n -> p k n", p=P)).then_inc(res_loaded, 16)
                sp.dma_start(mod_row[:, :, :],
                             d["mod_rows"][bass.ds(s, 1), :, :].to_broadcast([P, 4, DM])).then_inc(res_loaded, 16)

            def store_x1(s):
                sp.wait_ge(x1_ready, s + 1)
                sp.dma_start(out[s, :, :].rearrange("(k p) n -> p k n", p=P), x1[:, :, :]).then_inc(x1_stored, 16)

            def load_w1():
                sp.wait_ge(bx_ready, PAIRS * B)
                sp.wait_ge(hc_ready, UNITS * B)
                for e in range(NE):
                    sp.dma_start(keep["wide"][:, e * FT * FF:(e + 1) * FT * FF].rearrange("p (k n) -> p k n", k=FT),
                                 t["w1"][e, :, :].rearrange("(k p) n -> p k n", p=P)).then_inc(expert_in[e], 16)

            program(sp, prelude,
                    front={1: [next_x], 40: [first_only(store_rows)], 51: [store_bc], 55: [load_bc(0)], 56: [load_bc(1)], 60: [load_bc(2)], 62: [load_bc(3)]},
                    gates={}, back={13: [load_res]}, tail={2: [store_x1]}, scan=lambda s, n: None, scans_over=load_w1)
            sp.wait_ge(ends_ready, 1)
            for e in range(NE):
                end = sp.value_load(keep["ends"][0:1, e:e + 1], min_val=0, max_val=NE * CAP - ROWS)
                sp.dma_start(d["region"][bass.ds(end, ROWS), :].rearrange("(k p) n -> p k n", p=P),
                             d["pads"]).then_inc(padded, 16)
            sp.wait_ge(x1_stored, 16 * B)

        @block.gpsimd
        def _(pool):
            own = Ordered(pool, p_own, 3)

            def prelude():
                nc.gpsimd.memset(flat_c[:, 0:4096], 0.0).then_inc(pp_own, 1)
                pool.wait_ge(pp_own, 1)
                nc.gpsimd.iota(pad_no[:, 0:1].bitcast(U32), [[0, 1]], base=0, channel_multiplier=1)
                nc.gpsimd.iota(pad_no[:, 1:2].bitcast(U32), [[0, 1]], base=B, channel_multiplier=0).then_inc(pp_own, 1)
                pool.wait_ge(pp_own, 2)
                for k in range(ROWS // P):
                    last = nc.gpsimd.tensor_copy(pad_rows[:, k, DM:RW].bitcast(U32), pad_no.bitcast(U32))
                last.then_inc(pool_set, 1)

            def times_dt(j):
                def step(s):
                    pool.wait_ge(dt_ready, s * JT + j + 1)
                    nc.gpsimd.tensor_tensor(u[:, j, :], dt[:, j, :], xs[:, s % 2, j, :], ALU.mult).then_inc(u_ready, 1)
                return step

            def gate_y(j):
                def step(s):
                    pool.wait_ge(y_read, JT * s + j + 1)
                    pool.wait_ge(z_ready, s + 1)
                    nc.gpsimd.tensor_tensor(yg[:, j, :], yg[:, j, :], zs[:, j, :], ALU.mult).then_inc(y_gated, 1)
                return step

            def row(k):
                return mod_row[:, k, :].unsqueeze(1).to_broadcast([P, TT, DM])

            def shift_x(s):
                pool.wait_ge(res_loaded, 32 * (s + 1))
                own.done(nc.gpsimd.tensor_tensor(x1[:, :, :], x1[:, :, :], row(1), ALU.add))

            def scale_n2(s):
                pool.wait_ge(n2_ready, s + 1)
                own.done(nc.gpsimd.tensor_tensor(norm[:, :, :], norm[:, :, :], row(0), ALU.mult))

            def residual(s):
                own.settle(s)
                nc.gpsimd.tensor_tensor(x1[:, :, :], norm[:, :, :], x1[:, :, :], ALU.add).then_inc(x1_ready, 1)

            def scale_n3(s):
                pool.wait_ge(n3_ready, s + 1)
                own.done(nc.gpsimd.tensor_tensor(norm[:, :, :], norm[:, :, :], row(2), ALU.mult))

            def shift_n3(s):
                own.settle(s)
                wait(pool, scattered, 16 * 2 * TT * s)
                nc.gpsimd.tensor_tensor(h3[:, :, 0:DM], norm[:, :, :], row(3), ALU.add).then_inc(h3_ready, 1)
                own.finish()

            def scatter(q):
                def step(s):
                    if q == 0:
                        wait_apart(pool, slots_ready, s + 1, pool_set)
                    for k in range(2):
                        nc.gpsimd.indirect_dma_start(
                            d["region"], bass.IndirectOffsetOnAxis(slot_i[:, k, q:q + 1], 0), h3[:, q, :], None,
                        ).then_inc(scattered, 16)
                return step

            def products(s, k):
                if k % 2:
                    return
                q, j, st = k // 2, k // DS, k % DS
                if st == 0:
                    pool.wait_ge(u_ready, JT * s + j + 1)
                if j == 0 and st % 4 == 0:
                    pool.wait_ge(bc_loaded[st // 4], 32 * (s + 1))
                wait(pool, scan_done, UNITS * s + 2 * (used_before(q, NBX, PAIRS) + 1))
                nc.gpsimd.tensor_tensor(bx[:, q % NBX, :, :], u[:, j, :].unsqueeze(1).to_broadcast([P, 2, L]),
                                        b_bc[:, st:st + 2, :], ALU.mult).then_inc(bx_ready, 1)

            program(pool, prelude,
                    front={61: [times_dt(0), times_dt(1)]},
                    gates={9: [times_dt(2)], 15: [times_dt(3)], 50: [gate_y(0)], 57: [gate_y(1)], 63: [gate_y(2)]},
                    back={3: [gate_y(3)], 40: [shift_x], 48: [scale_n2], 52: [residual], 60: [scale_n3], 61: [shift_n3]},
                    tail={15: [scatter(0)], 17: [scatter(1)], 19: [scatter(2)], 21: [scatter(3)]},
                    scan=products)
            pool.wait_ge(scattered, 16 * 2 * TT * B)

        @block.scalar
        def _(act):
            def prelude():
                act.wait_ge(mod_in, 32)
                act.wait_ge(consts_set, 1)
                nc.scalar.activation(cond_t, cond_t, ACT.Silu).then_inc(cond_silu, 1)
                nc.scalar.preload_act_table_set("natural_log_exp_and_others")
                act.wait_ge(loaded, 16 * NW)
                nc.scalar.activation(a_neg[:, :, :], a_neg[:, :, :], ACT.Exp).then_inc(a_ready, 1)
                act.wait_ge(a_ready, 1)
                nc.scalar.activation(a_neg[:, :, :], a_neg[:, :, :], ACT.Identity, scale=-1.0,
                                     bias=zero_bias[:, 0:1]).then_inc(a_ready, 1)
                act.wait_ge(a_ready, 2)

            def hidden(f):
                def step(s):
                    if f == 0:
                        act.wait_ge(xt_full, s + 1)
                        wait(act, res_copied, FT * s)
                        wait(act, zin_full, JT * s)
                        act.wait_ge(mod_copied, 2 + s + 1)
                    nc.scalar.activation(h_t[:, f, :], fp[f][:, :], ACT.Identity, scale=mod_now[:, 2 + f:3 + f],
                                         bias=mod_now[:, f:f + 1]).then_inc(h_ready, 1)
                return step

            def tap(j):
                def step(s):
                    if j == 0:
                        wait(act, u_ready, JT * (s - 1))
                        wait(act, y_read, JT * (s - 1))
                    wait_apart(act, xin_full, JT * s + j + 1, consts_set)
                    nc.scalar.activation(xs[:, s % 2, j, :], fp[j % 2][:, :], ACT.Identity,
                                         scale=conv_w[:, j, DC - 1:DC], bias=conv_b[:, j:j + 1]).then_inc(tap_last, 1)
                return step

            def silu_x(s):
                wait_apart(act, conv_done, JT * (s + 1), consts_set)
                nc.scalar.activation(xs[:, s % 2, :, :], xs[:, s % 2, :, :], ACT.Silu).then_inc(xs_ready, 1)
                nc.scalar.preload_act_table_set("natural_log_exp_and_others")

            def silu_z(s):
                act.wait_ge(z_copied, JT * (s + 1))
                nc.scalar.activation(zs[:, :, :], zs[:, :, :], ACT.Silu).then_inc(z_ready, 1)
                if isinstance(s, int) and s == B - 1:
                    nc.scalar.preload_act_table_set("natural_log_exp_and_others")

            def copy_z(j):
                def step(s):
                    act.wait_ge(zin_full, JT * s + j + 1)
                    if j == 0:
                        wait(act, y_gated, JT * s)
                    nc.scalar.activation(zs[:, j, :], fp[(1, 0, 1, 0)[j]][:, :], ACT.Identity,
                                         bias=zero_bias[:, 0:1]).then_inc(z_copied, 1)
                return step

            def copy_xdbl(s):
                act.wait_ge(xproj_full, s + 1)
                wait(act, bc_stored, 16 * s)
                wait(act, dt_full, JT * s)
                nc.scalar.activation(x_dbl[:, :], fp[0][0:DTR + 2 * DS, :], ACT.Identity,
                                     bias=zero_bias[0:DTR + 2 * DS, 0:1]).then_inc(xdbl_ready, 1)

            def dt_bank(j):
                return fp[(1, 0, 1, 0)[j]][:, :]

            def dt_relu(j):
                def step(s):
                    act.wait_ge(dt_full, JT * s + j + 1)
                    wait(act, dt_ready, JT * s + j - 1)
                    nc.scalar.activation(relu_dt[:, j % 2, :], dt_bank(j), ACT.Relu, bias=dt_b[:, j:j + 1])
                return step

            def dt_abs(j):
                def step(s):
                    wait(act, exp_done, UNITS * (s - 1) + (j + 1) * DS)
                    nc.scalar.activation(dt[:, j, :], dt_bank(j), ACT.Abs, bias=dt_b[:, j:j + 1]).then_inc(relu_ready, 1)
                return step

            def dt_exp(j):
                def step(s):
                    act.wait_ge(relu_ready, JT * s + j + 1)
                    nc.scalar.activation(dt[:, j, :], dt[:, j, :], ACT.Exp, scale=-1.0,
                                         bias=zero_bias[:, 0:1]).then_inc(a_own, 1)
                return step

            def dt_log(j):
                def step(s):
                    act.wait_ge(a_own, JT * s + j + 1)
                    nc.scalar.activation(dt[:, j, :], dt[:, j, :], ACT.Ln, bias=ones[:, 0:1]).then_inc(log_ready, 1)
                return step

            def copy_res(f):
                def step(s):
                    if f == 0:
                        wait(act, out_full, 2 * s)
                    nc.scalar.activation(h_res[:, f, :], h_t[:, f, :], ACT.Identity,
                                         bias=zero_bias[:, 0:1]).then_inc(res_copied, 1)
                return step

            def hidden2(f):
                def step(s):
                    if f == 0:
                        act.wait_ge(n1t_full, s + 1)
                        wait(act, logits_full, s)
                    nc.scalar.activation(h2_t[:, f, :], bp[f][:, :], ACT.Identity, scale=ln1_w[:, f:f + 1],
                                         bias=ln1_b[:, f:f + 1]).then_inc(h2_ready, 1)
                return step

            def copy_f1(j):
                def step(s):
                    act.wait_ge(f1_full, JT * s + j + 1)
                    if j == 0:
                        wait(act, f2_full, 2 * s)
                        act.wait_ge(xt_full, min(s + 3, B) if isinstance(s, int) else s + 3)
                    nc.scalar.activation(f1[:, j, :], bp[j % 2][:, :], ACT.Identity,
                                         bias=f1_b[:, j:j + 1]).then_inc(f1_copied, 1)
                return step

            def copy_h3(f):
                def step(s):
                    if f == 0:
                        act.wait_ge(h3t_full, s + 1)
                    nc.scalar.activation(h2_t[:, f, :], bp[f][:, :], ACT.Identity,
                                         bias=zero_bias[:, 0:1]).then_inc(h3t_ready, 1)
                return step

            def decay(s, k):
                j, st = divmod(k, DS)
                if st == 0:
                    act.wait_ge(dt_ready, JT * s + j + 1)
                wait(act, hc_ready, UNITS * s + used_before(k, NSS, UNITS) + 1)
                nc.scalar.activation(ss[k % NSS][:, :], dt[:, j, :], ACT.Exp, scale=a_neg[:, j, st:st + 1],
                                     bias=zero_bias[:, 0:1]).then_inc(exp_done, 1)

            program(act, prelude,
                    front={29: [hidden(0)], 30: [hidden(1)], 33: [tap(0)], 35: [tap(1)], 39: [tap(2)], 42: [tap(3)], 45: [silu_x], 51: [copy_xdbl], 52: [dt_relu(1)], 54: [dt_relu(0), dt_abs(0)], 55: [dt_exp(0)], 56: [dt_log(0), dt_abs(1)], 58: [dt_exp(1), dt_log(1)]},
                    gates={4: [dt_relu(2)], 6: [dt_abs(2), dt_exp(2), dt_relu(3)], 7: [dt_log(2), dt_abs(3)], 8: [dt_exp(3)], 9: [dt_log(3)], 11: [copy_z(0)], 16: [copy_z(1)], 21: [copy_res(0)], 22: [copy_res(1)], 23: [copy_z(2)], 27: [copy_z(3)], 45: [silu_z]},
                    back={25: [hidden2(0)], 26: [hidden2(1)], 29: [copy_f1(0)], 30: [copy_f1(1)], 32: [copy_f1(2)], 35: [copy_f1(3)]},
                    tail={3: [copy_h3(0)], 4: [copy_h3(1)]},
                    scan=decay)

        @block.tensor
        def _(pe):
            def prelude():
                pe.wait_ge(mod_in, 32)
                pe.wait_ge(cond_silu, 1)
                for c in range(4):
                    for f in range(FT):
                        last = nc.tensor.matmul(ysum[:, c * B:(c + 1) * B], w_mod[:, f, c * P:(c + 1) * P],
                                                cond_t[:, f, :], start=(f == 0), stop=(f == FT - 1))
                last.then_inc(mod_full, 1)
                pe.wait_ge(loaded, 16 * NW)
                pe.wait_ge(consts_set, 1)

            def modulation_rows():
                for k in range(3):
                    for f in range(FT):
                        last = nc.tensor.matmul(ss[k][0:B, :], cond_t[:, f, :], w_mod[:, f, k * L:(k + 1) * L],
                                                start=(f == 0), stop=(f == FT - 1))
                last.then_inc(mod_full, 1)

            def transposes(src, dst, width=None):
                for f in range(FT):
                    for q in range(TT):
                        last = nc.tensor.transpose(dst[f][:, q * P:(q + 1) * P], src[:, q, f * P:(f + 1) * P],
                                                   ident[:, :])
                return last

            def turn_x(s):
                pe.wait_ge(x_normed, s + 1)
                wait(pe, z_copied, JT * s)
                transposes(xrow, fp).then_inc(xt_full, 1)

            def in_proj(dst, col):
                for f in range(FT):
                    last = nc.tensor.matmul(dst, w_in[:, f, col:col + P], h_t[:, f, :],
                                            start=(f == 0), stop=(f == FT - 1))
                return last

            def x_in(j):
                def step(s):
                    pe.wait_ge(h_ready, FT * (s + 1))
                    if j >= 2:
                        pe.wait_ge(conv_done, JT * s + j - 1)
                    in_proj(fp[j % 2][:, :], j * P).then_inc(xin_full, 1)
                return step

            def z_in(j):
                def step(s):
                    if j < 2:
                        pe.wait_ge(relu_ready, JT * s + j + 3)
                    else:
                        pe.wait_ge(z_copied, JT * s + j - 1)
                    in_proj(fp[(1, 0, 1, 0)[j]][:, :], DI + j * P).then_inc(zin_full, 1)
                return step

            def x_proj(half):
                def step(s):
                    if half == 0:
                        pe.wait_ge(xs_ready, s + 1)
                    for j in (2 * half, 2 * half + 1):
                        last = nc.tensor.matmul(fp[0][0:DTR + 2 * DS, :], w_x[:, j, :], xs[:, s % 2, j, :],
                                                start=(j == 0), stop=(j == JT - 1))
                    if half == 1:
                        last.then_inc(xproj_full, 1)
                return step

            def dt_proj(j):
                def step(s):
                    pe.wait_ge(xdbl_ready, s + 1)
                    if j >= 2:
                        pe.wait_ge(relu_ready, JT * s + j - 1)
                    nc.tensor.matmul(fp[(1, 0, 1, 0)[j]][:, :], w_dt[:, j * P:(j + 1) * P], x_dbl[0:DTR, :],
                                     start=True, stop=True).then_inc(dt_full, 1)
                return step

            def out_proj(q):
                def step(s):
                    if q == 0:
                        pe.wait_ge(y_gated, JT * (s + 1))
                        pe.wait_ge(res_copied, FT * (s + 1))
                        wait(pe, ranks_taken, s)
                    o = bp[q // 2][:, (q % 2) * DM:(q % 2 + 1) * DM]
                    for j in range(JT):
                        nc.tensor.matmul(o, yg[:, j, q * P:(q + 1) * P], w_out[:, j, :], start=(j == 0), stop=False)
                    for f in range(FT):
                        last = nc.tensor.matmul(o[:, f * P:(f + 1) * P], h_res[:, f, q * P:(q + 1) * P], ident[:, :],
                                                start=False, stop=(f == FT - 1))
                    if q % 2:
                        last.then_inc(out_full, 1)
                return step

            def turn_n1(s):
                pe.wait_ge(n1_ready, s + 1)
                transposes(norm, bp).then_inc(n1t_full, 1)

            def ffn1(j):
                def step(s):
                    pe.wait_ge(h2_ready, FT * (s + 1))
                    if j >= 2:
                        pe.wait_ge(f1_copied, JT * s + j - 1)
                    for f in range(FT):
                        last = nc.tensor.matmul(bp[j % 2][:, :], w_f1[:, f, j * P:(j + 1) * P], h2_t[:, f, :],
                                                start=(f == 0), stop=(f == FT - 1))
                    last.then_inc(f1_full, 1)
                return step

            def ffn2(q):
                def step(s):
                    if q == 0:
                        pe.wait_ge(f1_ready, JT * (s + 1))
                    o = bp[q // 2][:, (q % 2) * DM:(q % 2 + 1) * DM]
                    nc.tensor.matmul(o, ones[0:1, :], f2_b[0:1, :], start=True, stop=False)
                    for j in range(JT):
                        nc.tensor.matmul(o, f1[:, j, q * P:(q + 1) * P], w_f2[:, j, :], start=False, stop=False)
                    for f in range(FT):
                        last = nc.tensor.matmul(o[:, f * P:(f + 1) * P], h2_t[:, f, q * P:(q + 1) * P], ident[:, :],
                                                start=False, stop=(f == FT - 1))
                    if q % 2:
                        last.then_inc(f2_full, 1)
                return step

            def turn_h3(s):
                pe.wait_ge(h3_ready, s + 1)
                transposes(h3, bp).then_inc(h3t_full, 1)

            def gate(s):
                pe.wait_ge(h3t_ready, FT * (s + 1))
                for q in range(TT):
                    o = bp[0][:, q * NE:(q + 1) * NE]
                    for f in range(FT):
                        last = nc.tensor.matmul(o, h2_t[:, f, q * P:(q + 1) * P], w_gate[:, f, :],
                                                start=(f == 0), stop=(f == FT - 1))
                last.then_inc(logits_full, 1)

            def rank(s):
                pe.wait_ge(picks_ready, s + 1)
                m = picks[:, :, :].rearrange("p q e -> p (q e)")
                nc.tensor.matmul(bp[1][:, 0:TT * NE], before[:, :], m, start=True, stop=True)
                nc.tensor.matmul(bp[1][:, TT * NE:2 * TT * NE], ones[:, :], m, start=True, stop=True).then_inc(rank_full, 1)

            def state_sum(s, k):
                j, st = divmod(k, DS)
                if st == 0:
                    wait(pe, y_read, JT * s + j)
                pe.wait_ge(hc_ready, UNITS * s + k + 1)
                nc.tensor.matmul(ysum[:, :], ident[:, :], hc[:, k % NHC, :], start=(st == 0),
                                 stop=(st == DS - 1)).then_inc(y_summed, 1)

            program(pe, prelude,
                    front={25: [turn_x, first_only(modulation_rows)], 29: [x_in(0)], 31: [x_in(1)], 34: [x_in(2)], 39: [x_in(3)], 45: [x_proj(0)], 47: [x_proj(1), dt_proj(0)], 48: [dt_proj(1)]},
                    gates={1: [dt_proj(2), dt_proj(3)], 6: [z_in(0)], 7: [z_in(1)], 17: [z_in(2)], 19: [z_in(3)]},
                    back={9: [out_proj(0)], 11: [out_proj(1)], 13: [out_proj(2)], 15: [out_proj(3)], 20: [turn_n1], 24: [ffn1(0)], 25: [ffn1(1)], 27: [ffn1(2)], 31: [ffn1(3)], 35: [ffn2(0)], 36: [ffn2(1)], 38: [ffn2(2)], 40: [ffn2(3)], 56: [turn_h3]},
                    tail={4: [gate], 6: [rank]},
                    scan=state_sum)

        @block.vector
        def _(dve):
            LN = 5 + 3 * NEWTON
            own = Ordered(dve, v_own, 3 * LN)
            own_tail = Ordered(dve, vt_own, 10 + TT)
            own_front = Ordered(dve, vf_own, LN)
            pre = [0]

            def link(ins):
                pre[0] += 1
                ins.then_inc(v0_own, 1)
                dve.wait_ge(v0_own, pre[0])

            def prelude():
                nc.vector.memset(ones[:, :], 1.0)
                nc.vector.memset(zero_bias[:, :], 0.0)
                nc.vector.memset(token_no[:, 1, :], 0.0)
                nc.vector.memset(count[:, :], 0.0).then_inc(consts_set, 1)
                dve.wait_ge(mod_full, 1)
                nc.vector.tensor_copy(mod_col[:, 0:2, :].rearrange("p k b -> p (k b)"),
                                      ysum[:, 0:2 * B]).then_inc(mod_copied, 1)
                nc.vector.tensor_scalar(mod_col[:, 2:4, :].rearrange("p k b -> p (k b)"), ysum[:, 2 * B:4 * B],
                                        1.0, None, ALU.add).then_inc(mod_copied, 1)
                dve.wait_ge(mod_copied, 2)

            def row_parts():
                dve.wait_ge(loaded, 16 * NW)
                dve.wait_ge(mod_full, 2)
                for k in range(3):
                    last = nc.vector.tensor_copy(mod8[:, 2 * k:2 * k + 2, :].rearrange("p k n -> p (k n)"), ss[k][0:B, :])
                link(last)
                gates2 = mod8[:, 2:6:3, :]
                link(nc.vector.scalar_tensor_tensor(mag8, gates2, -1.0, gates2, ALU.mult, ALU.max))
                nc.vector.tensor_scalar(sgn8, gates2, 0.0, 2.0, ALU.is_ge, ALU.mult)
                link(nc.vector.tensor_scalar(mag8, mag8, 0.25, None, ALU.max))
                link(nc.vector.scalar_tensor_tensor(mag8, sgn8, -1.0, mag8, ALU.add, ALU.mult))
                nc.vector.tensor_tensor(row8[:, 0, :], mag8[:, 0, :], ln2w8, ALU.mult)
                nc.vector.tensor_tensor(row8[:, 1, :], mag8[:, 0, :], ln2b8, ALU.mult)
                nc.vector.tensor_scalar(row8[:, 2, :], mod8[:, 4, :], 1.0, None, ALU.add)
                nc.vector.tensor_copy(row8[:, 3, :], mod8[:, 3, :])
                nc.vector.tensor_copy(row8[:, 4, :], mag8[:, 1, :]).then_inc(rows_ready, 1)

            def packed(steps, n):
                def pack(some):
                    def step(s):
                        for one in some:
                            one(s)
                    return step
                return [pack(steps[k:k + n]) for k in range(0, len(steps), n)]

            def layer_norm(o, before, src, dst, eps, ready, after, bufs):
                st_, mv_, var_, root_, tmp_ = bufs
                vector = nc.vector

                def stats(half):
                    def step(s):
                        before(half, s)
                        for q in (2 * half, 2 * half + 1):
                            last = vector.bn_stats(st_[:, q, :], src(q))
                        if half == 1:
                            o.done(last)
                    return step

                def aggregate(s):
                    o.settle_apart(s, consts_set)
                    for q in range(TT):
                        last = vector.bn_aggr(mv_[:, q, :], st_[:, q, :])
                    o.done(last)

                def small(op):
                    def step(s):
                        o.settle(s)
                        o.done(op())
                    return step

                def scale(half):
                    def step(s):
                        if half == 0:
                            o.settle(s)
                        for q in (2 * half, 2 * half + 1):
                            last = vector.tensor_scalar(dst(q), src(q), mv_[:, q, 0:1], root_[:, q:q + 1],
                                                        ALU.subtract, ALU.mult)
                        if half == 1:
                            last.then_inc(ready, 1)
                            after(s)
                    return step

                variance = small(lambda: vector.tensor_scalar(var_[:, :], mv_[:, :, 1], eps, None, ALU.add))
                halve = small(lambda: vector.tensor_scalar(tmp_[:, :].bitcast(I32), var_[:, :].bitcast(I32), 1, None,
                                                           ALU.logical_shift_right))
                guess = small(lambda: vector.tensor_scalar(root_[:, :].bitcast(I32), tmp_[:, :].bitcast(I32), -1.0,
                                                           float(ROOT_GUESS), ALU.mult, ALU.add))
                newton = [
                    small(lambda: vector.scalar_tensor_tensor(tmp_[:, :], root_[:, :], -0.5, root_[:, :],
                                                              ALU.mult, ALU.mult)),
                    small(lambda: vector.tensor_tensor(tmp_[:, :], tmp_[:, :], var_[:, :], ALU.mult)),
                    small(lambda: vector.scalar_tensor_tensor(root_[:, :], tmp_[:, :], 1.5, root_[:, :],
                                                              ALU.add, ALU.mult)),
                ]
                shorts = [aggregate, variance, halve, guess, *(newton * NEWTON)]
                return [stats(0), stats(1), *(packed(shorts, 3)), scale(0), scale(1)]

            back_bufs = (stats, mv, lnv, rstd, tmp)
            front_bufs = (stats0, mv0, lnv0, rstd0, tmp0)

            def next_modulation(s):
                wait(dve, h_ready, FT * s)
                nc.vector.tensor_copy(mod_now[:, :], mod_col[:, :, s]).then_inc(mod_copied, 1)
                own_front.finish()

            norm_x = layer_norm(own_front, lambda half, s: dve.wait_ge(x_loaded, 16 * (s + 1)), lambda q: xrow[:, q, :],
                                lambda q: xrow[:, q, :], LN_EPS_OUT, x_normed, next_modulation, front_bufs)

            def conv(j):
                def tap(k):
                    def step(s):
                        if k == 1:
                            dve.wait_ge(tap_last, JT * s + j + 1)
                        else:
                            dve.wait_ge(tap_own, (JT * s + j) * (DC - 2) + k - 1)
                        dst = xs[:, s % 2, j, k:L]
                        nc.vector.scalar_tensor_tensor(dst, fp[j % 2][:, 0:L - k], conv_w[:, j, DC - 1 - k:DC - k],
                                                       dst, ALU.mult, ALU.add).then_inc(tap_own if k < DC - 1 else conv_done, 1)
                    return step
                return [tap(k) for k in range(1, DC)]

            def add_dt(j):
                def step(s):
                    dve.wait_ge(log_ready, JT * s + j + 1)
                    nc.vector.tensor_tensor(dt[:, j, :], dt[:, j, :], relu_dt[:, j % 2, :], ALU.add).then_inc(dt_ready, 1)
                return step

            def read_y(j):
                def step(s):
                    dve.wait_ge(y_summed, UNITS * s + (j + 1) * DS)
                    if j == 0:
                        wait(dve, out_full, 2 * s)
                    nc.vector.scalar_tensor_tensor(yg[:, j, :], xs[:, s % 2, j, :], d_skip[:, j:j + 1], ysum[:, :],
                                                   ALU.mult, ALU.add).then_inc(y_read, 1)
                return step

            def half(q):
                return bp[q // 2][:, (q % 2) * DM:(q % 2 + 1) * DM]

            def before_norm1(half, s):
                dve.wait_ge(out_full, 2 * s + half + 1)
                wait(dve, h3_ready, s)

            norm1 = layer_norm(own, before_norm1, half, lambda q: norm[:, q, :], LN_EPS_IN, n1_ready,
                               lambda s: None, back_bufs)

            def leaky(j):
                def step(s):
                    dve.wait_ge(f1_copied, JT * s + j + 1)
                    nc.vector.scalar_tensor_tensor(f1[:, j, :], f1[:, j, :], SLOPE, f1[:, j, :],
                                                   ALU.mult, ALU.max).then_inc(f1_ready, 1)
                return step

            norm2 = layer_norm(own, lambda half, s: dve.wait_ge(f2_full, 2 * s + half + 1), half, lambda q: norm[:, q, :], LN_EPS_IN,
                               n2_ready, lambda s: None, back_bufs)
            norm3 = layer_norm(own, lambda half, s: dve.wait_ge(x1_ready, s + 1), lambda q: x1[:, q, :],
                               lambda q: norm[:, q, :], LN_EPS_OUT, n3_ready, lambda s: own.finish(), back_bufs)

            def take_logits(s):
                dve.wait_ge(logits_full, s + 1)
                own_tail.done(nc.vector.tensor_tensor(logits[:, :, :], bp[0][:, 0:TT * NE].rearrange("p (q e) -> p q e", q=TT),
                                                      gate_b[:, :].unsqueeze(1).to_broadcast([P, TT, NE]), ALU.add))

            def largest(s):
                own_tail.settle_apart(s, consts_set)
                for q in range(TT):
                    last = nc.vector.max(top_v[:, q, :], logits[:, q, :])
                own_tail.done(last)

            def places_of_largest(s):
                own_tail.settle_apart(s, consts_set)
                for q in range(TT):
                    last = nc.vector.max_index(top_i[:, q, :], top_v[:, q, :], logits[:, q, :])
                own_tail.done(last)

            def as_floats(s):
                own_tail.settle(s)
                own_tail.done(nc.vector.tensor_copy(top_f[:, :, :], top_i[:, :, :]))

            def mark_picks(s):
                own_tail.settle(s)
                for k, pick in enumerate((pick1, pick2)):
                    own_tail.done(nc.vector.tensor_tensor(pick[:, :, :], e_iota8[:, :].unsqueeze(1).to_broadcast([P, TT, NE]),
                                                          top_f[:, :, k:k + 1].to_broadcast([P, TT, NE]), ALU.is_equal))

            def join_picks(s):
                own_tail.settle(s)
                nc.vector.tensor_tensor(picks[:, :, :], pick1[:, :, :], pick2[:, :, :], ALU.add).then_inc(picks_ready, 1)

            top2 = packed([take_logits, largest, places_of_largest, as_floats, mark_picks, join_picks], 2)

            def take_ranks(s):
                dve.wait_ge(rank_full, s + 1)
                nc.vector.tensor_copy(ranks[:, :, :, :].rearrange("p k q e -> p (k q e)"),
                                      bp[1][:, 0:2 * TT * NE]).then_inc(ranks_taken, 1)

            def rank_in_tile(s):
                dve.wait_ge(ranks_taken, s + 1)
                wait(dve, scattered, 16 * 2 * TT * s)
                own_tail.done(nc.vector.tensor_tensor(slot_f[:, :, :], ranks[:, 0, :, :],
                                                      e_base[:, :].unsqueeze(1).to_broadcast([P, TT, NE]), ALU.add))

            def rank_before_tile(q):
                def step(s):
                    own_tail.settle(s)
                    nc.vector.tensor_tensor(slot_f[:, q, :], slot_f[:, q, :], count[:, :], ALU.add)
                    own_tail.done(nc.vector.tensor_tensor(count[:, :], count[:, :], ranks[:, 1, q, :], ALU.add))
                return step

            def keep_picked(s):
                own_tail.settle(s)
                for k, pick in enumerate((pick1, pick2)):
                    own_tail.done(nc.vector.tensor_tensor(prod[:, k, :, :], slot_f[:, :, :], pick[:, :, :], ALU.mult))
                for k in range(2):
                    nc.vector.tensor_copy(h3[:, :, DM + k].bitcast(U32), token_no[:, k, :])

            def sum_picked(s):
                own_tail.settle(s)
                own_tail.done(nc.vector.tensor_reduce(slot_s[:, :, :], prod[:, :, :, :], AX.X, ALU.add))

            def as_numbers(s):
                own_tail.settle(s)
                nc.vector.tensor_copy(slot_i[:, :, :], slot_s[:, :, :])
                nc.vector.tensor_scalar(token_no[:, 0, :], token_no[:, 0, :], float(L), None, ALU.add)
                nc.vector.tensor_scalar(token_no[:, 1, :], token_no[:, 1, :], 1.0, None, ALU.add).then_inc(slots_ready, 1)
                own_tail.finish()

            slots = packed([take_ranks, rank_in_tile, *(rank_before_tile(q) for q in range(TT)), keep_picked, sum_picked, as_numbers], 2)

            def recur(k, s):
                dve.wait_ge(exp_done, UNITS * s + k + 1)
                if k % 2 == 0:
                    dve.wait_ge(bx_ready, PAIRS * s + k // 2 + 1)
                bank = ss[k % NSS][:, :]
                nc.vector.tensor_tensor_scan(bank, bank, bx[:, (k // 2) % NBX, k % 2, :], 0.0,
                                             ALU.mult, ALU.add).then_inc(scan_done, 1)

            def times_c(k, s):
                dve.wait_ge(scan_done, UNITS * s + k + 1)
                if k < DS and k % 4 == 0:
                    dve.wait_ge(bc_loaded[k // 4], 32 * (s + 1))
                wait(dve, y_summed, UNITS * s + used_before(k, NHC, UNITS) + 1)
                nc.vector.tensor_tensor(hc[:, k % NHC, :], ss[k % NSS][:, :], c_bc[:, k % DS, :],
                                        ALU.mult).then_inc(hc_ready, 1)

            def scans(s, n):
                (times_c if n % 2 else recur)(n // 2, s)

            def spread(*chains):
                table = {}
                for place, steps in chains:
                    for k, step in enumerate(steps):
                        table.setdefault(place + k, []).append(step)
                return table

            program(dve, prelude,
                    front=spread((22, norm_x), (50, [first_only(row_parts)]), (65, conv(0)), (70, conv(1)), (78, conv(2)), (82, conv(3)), (111, [add_dt(0)]), (113, [add_dt(1)])),
                    gates=spread((15, [add_dt(2)]), (19, [add_dt(3)]), (36, [read_y(0)]), (67, [read_y(1)]), (97, [read_y(2)])),
                    back=spread((2, [read_y(3)]), (35, norm1), (62, [leaky(0)]), (64, [leaky(1)]), (67, [leaky(2)]), (70, [leaky(3)]), (82, norm2), (104, norm3)),
                    tail=spread((13, top2), (17, slots)),
                    scan=scans, places=2 * UNITS)

            linked = [0]

            def link_tab(ins):
                linked[0] += 1
                ins.then_inc(tab_own, 1)
                dve.wait_ge(tab_own, linked[0])

            used = [0]

            def part(shape):
                size = 1
                for x in shape:
                    size *= x
                used[0] += size
                flat = hc[0:1, :, :].rearrange("p k l -> p (k l)")[:, used[0] - size:used[0]]
                if len(shape) == 1:
                    return flat
                return flat.rearrange("p (a b) -> p a b", a=shape[0])

            STEPS = B * L // ROWS
            more, tiles, t_end, t_start, one8, origin = (part(x) for x in ([NE, STEPS], [NE], [NE], [NE], [NE], [NE]))
            owned, under, row_f, tab_f, end_f = (part(x) for x in ([NTILE, NE], [NTILE, NE], [3, NTILE], [2 * NTILE], [NE]))
            steps, tile_no, tab, ends = (keep[k] for k in ("steps", "tile_no", "tab", "ends"))
            dve.wait_ge(y_summed, UNITS * B)
            link_tab(nc.vector.tensor_tensor(end_f, e_base[0:1, :], count[0:1, :], ALU.add))
            nc.vector.tensor_copy(ends[:, :], end_f).then_inc(ends_ready, 1)
            nc.vector.memset(one8, 1.0)
            link_tab(nc.vector.tensor_tensor(more[:, :, :], count[0:1, :].unsqueeze(2).to_broadcast([1, NE, STEPS]),
                                         steps[:, :].unsqueeze(1).to_broadcast([1, NE, STEPS]), ALU.is_gt))
            link_tab(nc.vector.tensor_reduce(tiles, more[:, :, :], AX.X, ALU.add))
            link_tab(nc.vector.tensor_tensor_scan(t_end, one8, tiles, 0.0, ALU.mult, ALU.add))
            link_tab(nc.vector.tensor_tensor(t_start, t_end, tiles, ALU.subtract))
            link_tab(nc.vector.scalar_tensor_tensor(origin, t_start, -float(ROWS), e_base[0:1, :],
                                                ALU.mult, ALU.add))
            tile_b = tile_no[:, :].unsqueeze(2).to_broadcast([1, NTILE, NE])

            def per_tile(x):
                return x.unsqueeze(1).to_broadcast([1, NTILE, NE])

            link_tab(nc.vector.tensor_tensor(owned[:, :, :], tile_b, per_tile(t_start), ALU.is_ge))
            link_tab(nc.vector.tensor_tensor(under[:, :, :], tile_b, per_tile(t_end), ALU.is_lt))
            link_tab(nc.vector.tensor_tensor(owned[:, :, :], owned[:, :, :], under[:, :, :], ALU.mult))
            link_tab(nc.vector.tensor_reduce(row_f[:, 0, :], owned[:, :, :], AX.X, ALU.add))
            link_tab(nc.vector.tensor_tensor(under[:, :, :], owned[:, :, :], per_tile(origin), ALU.mult))
            link_tab(nc.vector.tensor_reduce(row_f[:, 1, :], under[:, :, :], AX.X, ALU.add))
            link_tab(nc.vector.tensor_tensor(under[:, :, :], owned[:, :, :], per_tile(e_iota8[0:1, :]), ALU.mult))
            link_tab(nc.vector.tensor_reduce(tab_f[:, NTILE:2 * NTILE], under[:, :, :], AX.X, ALU.add))
            link_tab(nc.vector.tensor_scalar(row_f[:, 2, :], tile_no[:, :], float(ROWS), -float(IDLE_ROW),
                                         ALU.mult, ALU.add))
            link_tab(nc.vector.tensor_tensor(row_f[:, 2, :], row_f[:, 2, :], row_f[:, 0, :], ALU.mult))
            link_tab(nc.vector.scalar_tensor_tensor(tab_f[:, 0:NTILE], row_f[:, 2, :], float(IDLE_ROW), row_f[:, 1, :],
                                                ALU.add, ALU.add))
            nc.vector.tensor_copy(tab[:, :], tab_f).then_inc(tab_ready, 1)


def expert_program(nc, t, d, out, keep, expert_in, done):
    ident = keep["ident"]
    RB = ROWS // P
    MT = FF // P
    ctx = ExitStack()
    with ctx:
        def sb(name, shape, dt=F32):
            return ctx.enter_context(nc.sbuf_tensor(name, shape, dt))

        def ps(name):
            return ctx.enter_context(nc.psum_tensor(name, [P, 512], F32))

        def sem(name):
            return ctx.enter_context(nc.semaphore(name))

        tab = keep["tab"]
        w1_all = keep["wide"][:, :].rearrange("p (e n) -> p e n", e=NE)
        w2_all = sb("w2_all", [P, NE, MT * DM])
        b1_all = sb("b1_all", [P, NE, MT])
        b2_all = sb("b2_all", [P, NE, DM])
        rows = [sb(f"rows{i}", [P, RB, RW]) for i in range(2)]
        w1 = [sb(f"w1_{i}", [P, FT, FF]) for i in range(2)]
        b1 = [sb(f"b1_{i}", [P, MT]) for i in range(2)]
        rows_t = [sb(f"rows_t{i}", [P, FT, ROWS]) for i in range(2)]
        tokens = [sb(f"tokens{i}", [P, RB, 2], U32) for i in range(2)]
        gates = [sb(f"gates{i}", [P, RB, DM]) for i in range(2)]
        hidden = [sb(f"hidden{i}", [P, MT, ROWS]) for i in range(2)]
        result = [sb(f"result{i}", [P, RB, DM]) for i in range(2)]
        up = [ps(f"up{i}") for i in range(4)]
        turn = [ps(f"turn{i}") for i in range(2)]
        down = [ps(f"down{i}") for i in range(2)]

        tab_ready, padded = done["tab_ready"], done["padded"]
        experts_ready = sem("experts_ready")
        rows_in = [sem(f"rows_in{i}") for i in range(2)]
        w1_ready = sem("w1_ready")
        turned = sem("turned")
        rows_t_ready = sem("rows_t_ready")
        gates_in = [sem(f"gates_in{i}") for i in range(2)]
        up_full = sem("up_full")
        hidden_ready = sem("hidden_ready")
        down_full = sem("down_full")
        biased = sem("biased")
        result_ready = sem("result_ready")
        added = sem("added")

        block = ctx.enter_context(nc.Block())
        PAIRS_OF_TILES = NTILE // 2
        assert NTILE % 2 == 1

        def tile_loop(engine, step):
            step(0, 0, 0)
            step(1, 1, 0)
            with engine.Fori(0, PAIRS_OF_TILES - 1) as i:
                step(2 * i + 2, 0, i + 1)
                step(2 * i + 3, 1, i + 1)
            step(NTILE - 1, 0, PAIRS_OF_TILES)

        def expert_of(engine, j):
            return engine.value_load(tab[0:1, bass.ds(j + NTILE, 1)], min_val=0, max_val=NE - 1)

        @block.sync
        def _(sp):
            def load_expert(e):
                for dst, src in (
                    (b1_all[:, e, :], t["b1"][e, :, :]),
                    (w2_all[:, e, :].rearrange("p (k n) -> p k n", k=MT), t["w2"][e, :, :].rearrange("(k p) n -> p k n", p=P)),
                    (b2_all[:, e, :], t["b2"][e:e + 1, :].to_broadcast([P, DM])),
                ):
                    sp.dma_start(dst, src).then_inc(expert_in[e], 16)

            load_expert(0)
            for e in range(NE):
                if e + 1 < NE:
                    load_expert(e + 1)
                sp.wait_ge(expert_in[e], 64)
                sp.sem_inc(experts_ready, 1)

        @block.gpsimd
        def _(pool):
            pool.wait_ge(tab_ready, 1)
            pool.wait_ge(padded, 16 * NE)

            def load_rows(j, par):
                row = pool.value_load(tab[0:1, bass.ds(j, 1)], min_val=0, max_val=IDLE_ROW)
                wait_apart(pool, rows_t_ready, j - 1, tab_ready)
                nc.gpsimd.dma_start(rows[par][:, :, :],
                                    d["region"][bass.ds(row, ROWS), :].rearrange("(k p) n -> p k n", p=P)).then_inc(rows_in[par], 16)

            def load_gates(j, par):
                if not isinstance(j, int) or j > 1:
                    wait_apart(pool, result_ready, j - 1, tab_ready)
                for k in range(RB):
                    wait_apart(pool, rows_t_ready, j + 1, tab_ready)
                    nc.gpsimd.indirect_dma_start(
                        gates[par][:, k, :], None, d["gate_rows"],
                        bass.IndirectOffsetOnAxis(tokens[par][:, k, 1:2], 0)).then_inc(gates_in[par], 16)

            def add_rows(j, par):
                pool.wait_ge(result_ready, j + 1)
                for k in range(RB):
                    wait_apart(pool, added, RB * 16 * j + 16 * k, tab_ready)
                    nc.gpsimd.indirect_dma_start(
                        d["out_rows"], bass.IndirectOffsetOnAxis(tokens[par][:, k, 0:1], 0),
                        result[par][:, k, :], None, compute_op=ALU.add).then_inc(added, 16)

            load_rows(0, 0)
            load_rows(1, 1)
            load_gates(0, 0)
            load_rows(2, 0)
            load_gates(1, 1)
            add_rows(0, 0)
            with pool.Fori(0, PAIRS_OF_TILES - 1) as i:
                load_rows(2 * i + 3, 1)
                load_gates(2 * i + 2, 0)
                add_rows(2 * i + 1, 1)
                load_rows(2 * i + 4, 0)
                load_gates(2 * i + 3, 1)
                add_rows(2 * i + 2, 0)
            load_gates(NTILE - 1, 0)
            add_rows(NTILE - 2, 1)
            add_rows(NTILE - 1, 0)
            pool.wait_ge(added, RB * 16 * NTILE)

        @block.scalar
        def _(act):
            act.wait_ge(tab_ready, 1)

            def relu(j, par, i):
                act.wait_ge(w1_ready, j + 1)
                if not isinstance(j, int) or j > 1:
                    act.wait_ge(down_full, j - 1)
                for c in range(4):
                    act.wait_ge(up_full, 4 * j + c + 1)
                    for m in (2 * c, 2 * c + 1):
                        last = nc.scalar.activation(hidden[par][:, m, :], up[c][:, (m % 2) * ROWS:(m % 2 + 1) * ROWS],
                                                    ACT.Relu, bias=b1[par][:, m:m + 1])
                    last.then_inc(hidden_ready, 1)

            tile_loop(act, relu)

        @block.tensor
        def _(pe):
            def turn_rows(j, par, i):
                pe.wait_ge(rows_in[par], 16 * (i + 1))
                wait(pe, rows_t_ready, j - 1)
                for f in range(FT):
                    for k in range(RB):
                        last = nc.tensor.transpose(turn[par][:, f * ROWS + k * P:f * ROWS + (k + 1) * P],
                                                   rows[par][:, k, f * P:(f + 1) * P], ident[:, :])
                last.then_inc(turned, 1)

            def up_product(j, par, i):
                pe.wait_ge(rows_t_ready, j + 1)
                pe.wait_ge(w1_ready, j + 1)
                for c in range(4):
                    wait(pe, hidden_ready, 4 * j - 4 + c + 1)
                    for m in (2 * c, 2 * c + 1):
                        for f in range(FT):
                            last = nc.tensor.matmul(up[c][:, (m % 2) * ROWS:(m % 2 + 1) * ROWS],
                                                    w1[par][:, f, m * P:(m + 1) * P], rows_t[par][:, f, :],
                                                    start=(f == 0), stop=(f == FT - 1))
                    last.then_inc(up_full, 1)

            def down_product(j, par, i):
                e = expert_of(pe, j)
                pe.wait_ge(experts_ready, e + 1)
                wait(pe, result_ready, j - 1)
                for k in range(RB):
                    for m in range(MT):
                        if k == 0 and m % 2 == 0:
                            pe.wait_ge(hidden_ready, 4 * j + m // 2 + 1)
                        last = nc.tensor.matmul(down[par][:, k * DM:(k + 1) * DM], hidden[par][:, m, k * P:(k + 1) * P],
                                                w2_all[:, bass.ds(e, 1), m * DM:(m + 1) * DM].rearrange("p o n -> p (o n)"),
                                                start=(m == 0), stop=(m == MT - 1))
                last.then_inc(down_full, 1)

            def pair(i, following=True):
                up_product(2 * i, 0, i)
                turn_rows(2 * i + 1, 1, i)
                down_product(2 * i, 0, i)
                up_product(2 * i + 1, 1, i)
                turn_rows(2 * i + 2, 0, i + 1)
                down_product(2 * i + 1, 1, i)

            pe.wait_ge(tab_ready, 1)
            turn_rows(0, 0, 0)
            pair(0)
            with pe.Fori(0, PAIRS_OF_TILES - 1) as i:
                pair(i + 1)
            up_product(NTILE - 1, 0, PAIRS_OF_TILES)
            down_product(NTILE - 1, 0, PAIRS_OF_TILES)

        @block.vector
        def _(dve):
            dve.wait_ge(tab_ready, 1)

            def copy_rows(j, par, i):
                dve.wait_ge(turned, j + 1)
                wait(dve, up_full, 4 * (j - 1))
                nc.vector.tensor_copy(rows_t[par][:, :, :].rearrange("p f n -> p (f n)"), turn[par][:, 0:FT * ROWS])
                wait(dve, added, RB * 16 * (j - 1))
                nc.vector.tensor_copy(tokens[par][:, :, :], rows[par][:, :, DM:RW].bitcast(U32)).then_inc(rows_t_ready, 1)

            def copy_w1(j, par, i):
                e = expert_of(dve, j)
                dve.wait_ge(experts_ready, e + 1)
                wait_apart(dve, hidden_ready, 4 * (j - 1), tab_ready)
                nc.vector.tensor_copy(b1[par][:, :], b1_all[:, bass.ds(e, 1), :].rearrange("p o n -> p (o n)"))
                nc.vector.tensor_copy(w1[par][:, :, :].rearrange("p m n -> p (m n)"),
                                      w1_all[:, bass.ds(e, 1), :].rearrange("p o n -> p (o n)")).then_inc(w1_ready, 1)

            def finish_rows(j, par, i):
                e = expert_of(dve, j)
                dve.wait_ge(down_full, j + 1)
                wait(dve, added, RB * 16 * (j - 1))
                nc.vector.tensor_tensor(result[par][:, :, :], down[par][:, 0:RB * DM].rearrange("p (k n) -> p k n", k=RB),
                                        b2_all[:, bass.ds(e, 1), :].to_broadcast([P, RB, DM]), ALU.add).then_inc(biased, 1)
                dve.wait_ge(gates_in[par], 16 * RB * (i + 1))
                dve.wait_ge(biased, j + 1)
                nc.vector.tensor_tensor(result[par][:, :, :], result[par][:, :, :], gates[par][:, :, :],
                                        ALU.mult).then_inc(result_ready, 1)

            def prepare(j, par, i):
                copy_rows(j, par, i)
                copy_w1(j, par, i)

            def pair(i):
                prepare(2 * i + 1, 1, i)
                finish_rows(2 * i, 0, i)
                prepare(2 * i + 2, 0, i + 1)
                finish_rows(2 * i + 1, 1, i)

            prepare(0, 0, 0)
            pair(0)
            with dve.Fori(0, PAIRS_OF_TILES - 1) as i:
                pair(i + 1)
            finish_rows(NTILE - 1, 0, PAIRS_OF_TILES)


def build(nc, t, out):
    d = {
        "mod_rows": nc.dram_tensor("mod_rows", (B, 4, DM), F32).ap(),
        "gate_rows": nc.dram_tensor("gate_rows", (B + 1, DM), F32).ap(),
        "bc": nc.dram_tensor("bc", (2 * DS, L), F32).ap(),
        "region": nc.dram_tensor("region", (IDLE_ROW + ROWS, RW), F32).ap(),
        "pads": nc.dram_tensor("pad_tile", (P, ROWS // P, RW), F32).ap(),
        "out_rows": out.rearrange("s l n -> (s l) n"),
    }
    with ExitStack() as ctx:
        keep = {name: ctx.enter_context(nc.sbuf_tensor(name, [p, n], F32)) for name, p, n in
                (("ident", P, P), ("ones", P, P), ("zero_bias", P, 1), ("e_iota8", P, NE), ("e_base", P, NE),
                 ("count", P, NE), ("steps", 1, B * L // ROWS), ("tile_no", 1, NTILE), ("wide", P, 2 * DS * L))}
        keep["tab"] = ctx.enter_context(nc.sbuf_tensor("tab", [1, 2 * NTILE], I32))
        keep["ends"] = ctx.enter_context(nc.sbuf_tensor("ends", [1, NE], I32))
        done = {name: ctx.enter_context(nc.semaphore(name)) for name in ("tab_ready", "padded")}
        expert_in = [ctx.enter_context(nc.semaphore(f"expert_in{e}")) for e in range(NE)]
        scan_program(nc, t, d, out, keep, expert_in, done)
        expert_program(nc, t, d, out, keep, expert_in, done)


def kernel(**inputs):
    import numpy as np
    import concourse.bacc as bacc
    from concourse.bass_utils import run_bass_kernel_spmd

    a = {k: np.asarray(v) for k, v in inputs.items()}
    m = {k[len("L0_attn_"):]: v for k, v in a.items() if k.startswith("L0_attn_")}
    f = {k[len("L0_ffn_"):]: v for k, v in a.items() if k.startswith("L0_ffn_")}
    q = np.arange(P)
    arrays = {
        "x": m["x"], "cond_t": a["L0_c"].T, "wmod": a["L0_wmod"],
        "in_proj_t": m["in_proj_w"].T, "conv_w": m["conv_w"], "conv_b": m["conv_b"].reshape(JT, P).T,
        "x_proj_t": m["x_proj_w"].T, "dt_proj_t": m["dt_proj_w"].T, "dt_b": m["dt_proj_b"].reshape(JT, P).T,
        "A_log": m["A_log"], "D": m["D"].reshape(JT, P).T, "out_proj_t": m["out_proj_w"].T,
        "ln1_w": m["ln1_w"].reshape(FT, P).T, "ln1_b": m["ln1_b"].reshape(FT, P).T,
        "ffn_w1_t": m["ffn_w1"].T, "ffn_b1": m["ffn_b1"].reshape(JT, P).T, "ffn_w2_t": m["ffn_w2"].T,
        "ffn_b2": m["ffn_b2"].reshape(1, DM), "ln2_w": m["ln2_w"].reshape(1, DM), "ln2_b": m["ln2_b"].reshape(1, DM),
        "gate_w": f["gate_w"], "gate_b": f["gate_b"].reshape(1, NE), "w1": f["w1"],
        "b1": f["b1"].reshape(NE, FF // P, P).transpose(0, 2, 1), "w2": f["w2"], "b2": f["b2"],
        "ident": np.eye(P, dtype=np.float32), "before": (q[:, None] < q[None, :]).astype(np.float32),
        "e_iota": np.arange(NE, dtype=np.float32).reshape(1, NE),
        "e_base": (np.arange(NE) * CAP).astype(np.float32).reshape(1, NE),
        "token_no": np.arange(L, dtype=np.float32).reshape(TT, P).T,
        "steps": (np.arange(B * L // ROWS) * ROWS).astype(np.float32).reshape(1, -1),
        "tile_no": np.arange(NTILE, dtype=np.float32).reshape(1, NTILE),
    }
    arrays = {k: np.ascontiguousarray(v) for k, v in arrays.items()}
    nc = bacc.Bacc("TRN2", target_bir_lowering=False, num_devices=1)
    t = {k: nc.dram_tensor(f"in_{k}", v.shape, mybir.dt.from_np(v.dtype), kind="ExternalInput").ap()
         for k, v in arrays.items()}
    out = nc.dram_tensor("out", (B, L, DM), F32, kind="ExternalOutput").ap()
    build(nc, t, out)
    r = run_bass_kernel_spmd(nc, [{f"in_{k}": v for k, v in arrays.items()}], core_ids=[0])
    return r.results[0]["out"]
```
